# Optimizing a Trainium2 kernel written in Bass

```python
import numpy as np
import jax
import jax.numpy as jnp

def _softmax(x, axis=-1):
    return jax.nn.softmax(x, axis=axis)

def _gelu(x):
    return jax.nn.gelu(x, approximate=True)

def _silu(x):
    return jax.nn.silu(x)

def _sigmoid(x):
    return jax.nn.sigmoid(x)

def _layernorm(x, axis=-1, eps=1e-05):
    m = jnp.mean(x, axis=axis, keepdims=True)
    v = jnp.var(x, axis=axis, keepdims=True)
    return (x - m) / jnp.sqrt(v + eps)

def _scatter_add(tgt, idx, src, axis=0):
    return tgt.at[idx].add(src)

def _segment_sum(src, seg, n):
    return jax.ops.segment_sum(src, seg, n)
kernel_name = 'mk_macaron_d1_jaxref_r8_2a1462'

def setup_inputs(seed: int=0):
    np.random.seed(seed)
    _w = jnp.asarray

    def _L0_attn_setup():
        import jax, jax.numpy as jnp
        import numpy as np
        B, S, D = (2, 256, 128)
        H = 16
        HD = D // H
        SCALE = HD ** (-0.5)
        EPS = 1e-12

        def _rope_sin_cos(length, half, dtype):
            positions = jnp.arange(length, dtype=dtype)
            freqs = jnp.arange(half, dtype=dtype)
            inv_freq = 1.0 / 1250 ** (freqs / max(1, half))
            theta = jnp.einsum('s,f->sf', positions, inv_freq)
            return (jnp.sin(theta)[None, None], jnp.cos(theta)[None, None])

        def _rotate(x, sin, cos):
            x_even = x[..., 0::2]
            x_odd = x[..., 1::2]
            r_even = x_even * cos - x_odd * sin
            r_odd = x_even * sin + x_odd * cos
            return jnp.stack([r_even, r_odd], axis=-1).reshape(x.shape)
        key = jax.random.key(seed)
        k1, k2, k3 = jax.random.split(key, 3)
        tokens = jax.random.normal(k1, (B, S, D), dtype=jnp.float32)
        qkv_w = jax.random.normal(k2, (3 * D, D), dtype=jnp.float32) * D ** (-0.5)
        qkv_b = jnp.zeros((3 * D,), dtype=jnp.float32)
        out_w = jax.random.normal(k3, (D, D), dtype=jnp.float32) * D ** (-0.5)
        out_b = jnp.zeros((D,), dtype=jnp.float32)
        return {'tokens': tokens, 'qkv_w': qkv_w, 'qkv_b': qkv_b, 'out_w': out_w, 'out_b': out_b}
    _L0_attn_in = _L0_attn_setup()

    def _L0_ffn_setup():
        import jax, jax.numpy as jnp
        import numpy as np
        B, S, DIM = (2, 256, 128)
        HID = 256
        E, NSH, TOPK = (8, 2, 2)

        def _ffn(x, w1, w2, w3):
            return jax.nn.silu(x @ w1.T) * (x @ w3.T) @ w2.T
        key = jax.random.key(seed)
        ks = jax.random.split(key, 8)
        sc = 0.02
        return {'x': jax.random.normal(ks[0], (B, S, DIM), jnp.float32), 'router_w': jax.random.normal(ks[1], (E, DIM), jnp.float32) * sc, 'expert_bias': jnp.zeros((E,), jnp.float32), 'w1': jax.random.normal(ks[2], (E, HID, DIM), jnp.float32) * sc, 'w3': jax.random.normal(ks[3], (E, HID, DIM), jnp.float32) * sc, 'w2': jax.random.normal(ks[4], (E, DIM, HID), jnp.float32) * sc, 'sw1': jax.random.normal(ks[5], (NSH, HID, DIM), jnp.float32) * sc, 'sw3': jax.random.normal(ks[6], (NSH, HID, DIM), jnp.float32) * sc, 'sw2': jax.random.normal(ks[7], (NSH, DIM, HID), jnp.float32) * sc}
    _L0_ffn_in = _L0_ffn_setup()
    _d = {'L0_attn_tokens': _L0_attn_in['tokens'], 'L0_attn_qkv_w': _L0_attn_in['qkv_w'], 'L0_attn_qkv_b': _L0_attn_in['qkv_b'], 'L0_attn_out_w': _L0_attn_in['out_w'], 'L0_attn_out_b': _L0_attn_in['out_b'], 'L0_ffn_router_w': _L0_ffn_in['router_w'], 'L0_ffn_expert_bias': _L0_ffn_in['expert_bias'], 'L0_ffn_w1': _L0_ffn_in['w1'], 'L0_ffn_w3': _L0_ffn_in['w3'], 'L0_ffn_w2': _L0_ffn_in['w2'], 'L0_ffn_sw1': _L0_ffn_in['sw1'], 'L0_ffn_sw3': _L0_ffn_in['sw3'], 'L0_ffn_sw2': _L0_ffn_in['sw2']}
    _x0 = _d['L0_attn_tokens']
    _d['L0_attn_tokens'] = jax.random.normal(jax.random.fold_in(jax.random.key(seed), 1), (16, 512, 128), dtype=_x0.dtype)
    del _x0
    return _d

def reference(L0_attn_tokens, L0_attn_qkv_w, L0_attn_qkv_b, L0_attn_out_w, L0_attn_out_b, L0_ffn_router_w, L0_ffn_expert_bias, L0_ffn_w1, L0_ffn_w3, L0_ffn_w2, L0_ffn_sw1, L0_ffn_sw3, L0_ffn_sw2):

    def _L0_attn_ref(tokens, qkv_w, qkv_b, out_w, out_b):
        import jax, jax.numpy as jnp
        import numpy as np
        B, S, D = (2, 256, 128)
        H = 16
        HD = D // H
        SCALE = HD ** (-0.5)
        EPS = 1e-12

        def _rope_sin_cos(length, half, dtype):
            positions = jnp.arange(length, dtype=dtype)
            freqs = jnp.arange(half, dtype=dtype)
            inv_freq = 1.0 / 1250 ** (freqs / max(1, half))
            theta = jnp.einsum('s,f->sf', positions, inv_freq)
            return (jnp.sin(theta)[None, None], jnp.cos(theta)[None, None])

        def _rotate(x, sin, cos):
            x_even = x[..., 0::2]
            x_odd = x[..., 1::2]
            r_even = x_even * cos - x_odd * sin
            r_odd = x_even * sin + x_odd * cos
            return jnp.stack([r_even, r_odd], axis=-1).reshape(x.shape)
        batch, length, _ = tokens.shape
        qkv = tokens @ qkv_w.T + qkv_b
        qkv = qkv.reshape(batch, length, 3, H, HD)
        qkv = jnp.transpose(qkv, (0, 3, 1, 2, 4))
        q, k, v = (qkv[..., 0, :], qkv[..., 1, :], qkv[..., 2, :])
        sin, cos = _rope_sin_cos(length, HD // 2, q.dtype)
        q = _rotate(q, sin, cos)
        k = _rotate(k, sin, cos)
        q = q / jnp.maximum(jnp.linalg.norm(q, axis=-1, keepdims=True), EPS)
        k = k / jnp.maximum(jnp.linalg.norm(k, axis=-1, keepdims=True), EPS)
        scores = jnp.einsum('bhqd,bhkd->bhqk', q, k) * SCALE
        attn = jax.nn.softmax(scores, axis=-1)
        out = jnp.einsum('bhqk,bhkd->bhqd', attn, v)
        out = jnp.transpose(out, (0, 2, 1, 3)).reshape(batch, length, D)
        return out @ out_w.T + out_b

    def _L0_ffn_ref(x, router_w, expert_bias, w1, w3, w2, sw1, sw3, sw2):
        import jax, jax.numpy as jnp
        import numpy as np
        B, S, DIM = (2, 256, 128)
        HID = 256
        E, NSH, TOPK = (8, 2, 2)

        def _ffn(x, w1, w2, w3):
            return jax.nn.silu(x @ w1.T) * (x @ w3.T) @ w2.T
        bs, sl, d = x.shape
        xf = x.reshape(-1, d)
        shared = jnp.zeros_like(xf)
        for i in range(sw1.shape[0]):
            shared = shared + _ffn(xf, sw1[i], sw2[i], sw3[i])
        logits = xf @ router_w.T + expert_bias
        rw, sel = jax.lax.top_k(logits, TOPK)
        rw = jax.nn.softmax(rw.astype(jnp.float32), axis=-1).astype(x.dtype)
        onehot = jax.nn.one_hot(sel, E, dtype=x.dtype)
        combine = jnp.einsum('tk,tke->te', rw, onehot)

        def body(acc, ew):
            e1, e3, e2, cw = ew
            acc = acc + cw[:, None] * _ffn(xf, e1, e2, e3)
            return (acc, None)
        out, _ = jax.lax.scan(body, jnp.zeros_like(xf), (w1, w3, w2, combine.T))
        out = out + shared
        return out.reshape(bs, sl, -1)
    x = L0_attn_tokens
    x = x + 0.5 * _L0_ffn_ref(_layernorm(x, axis=-1), L0_ffn_router_w, L0_ffn_expert_bias, L0_ffn_w1, L0_ffn_w3, L0_ffn_w2, L0_ffn_sw1, L0_ffn_sw3, L0_ffn_sw2)
    x = x + _L0_attn_ref(_layernorm(x, axis=-1), L0_attn_qkv_w, L0_attn_qkv_b, L0_attn_out_w, L0_attn_out_b)
    x = x + 0.5 * _L0_ffn_ref(_layernorm(x, axis=-1), L0_ffn_router_w, L0_ffn_expert_bias, L0_ffn_w1, L0_ffn_w3, L0_ffn_w2, L0_ffn_sw1, L0_ffn_sw3, L0_ffn_sw2)
    return x

_drawn_inputs = setup_inputs


def setup_inputs(seed=0):
    import zlib

    import numpy as np

    out = dict(_drawn_inputs(seed))
    spreads = {'L0_attn_qkv_b': (0.0, 0.1), 'L0_attn_out_b': (0.0, 0.1), 'L0_ffn_expert_bias': (0.0, 0.8)}
    factors = {'L0_ffn_router_w': 8.0,
     'L0_ffn_w1': 8.0,
     'L0_ffn_w3': 8.0,
     'L0_ffn_w2': 8.0,
     'L0_ffn_sw1': 4.917,
     'L0_ffn_sw3': 4.898,
     'L0_ffn_sw2': 4.908}
    for name, (base, spread) in spreads.items():
        noise = np.random.default_rng([zlib.crc32(name.encode()), seed]).standard_normal(out[name].shape)
        drawn = base * np.exp(spread * noise) if base else spread * noise
        out[name] = jnp.asarray(drawn.astype(out[name].dtype))
    for name, factor in factors.items():
        out[name] = (out[name] * factor).astype(out[name].dtype)
    return out
```

```python
from contextlib import ExitStack

import numpy as np
import concourse.bass as bass
from concourse import mybir

F32 = mybir.dt.float32
F32R = mybir.dt.float32r
F16 = mybir.dt.float16
ALU = mybir.AluOpType
ACT = mybir.ActivationFunctionType
AX = mybir.AxisListType

P = 128
D = 128
BATCH, SEQ = 16, 512
NT = SEQ // P
TILES = BATCH * NT
HEADS, HD = 16, 8
HID = 256
EXPERTS, SHARED = 8, 2
FFNS = EXPERTS + SHARED
HC = HID // P
CHUNKS = FFNS * HC
ROUTED = EXPERTS * HC
FW = 3 * HID
QKV0 = FFNS * FW
OUT0 = QKV0 + 3 * D
WCOLS = OUT0 + D
STAGE = 1024
LN_EPS = 1e-5
NORM_EPS2 = 1e-24
MASKED = -3.0e38
LN_SCALE = 2.0 ** 16
SLOT = 32

C_ID, C_RANK = 0, P
C_COS = C_RANK + EXPERTS
C_SIN = C_COS + NT * HD
C_ALL = C_SIN + NT * HD


def w1_cols(f, k):
    return slice(f * FW + k * P, f * FW + (k + 1) * P)


def w3_cols(f, k):
    return slice(f * FW + HID + k * P, f * FW + HID + (k + 1) * P)


def w2_cols(f, k):
    return slice(f * FW + 2 * HID + k * D, f * FW + 2 * HID + (k + 1) * D)


def tiles_of(x, b):
    return x[:, bass.ds(b * NT, NT), :]


class Steps:

    def __init__(self, eng, sem, base):
        self.eng, self.sem, self.base, self.n = eng, sem, base, 0

    def did(self, instruction):
        self.n += 1
        return instruction.then_inc(self.sem, 1)

    def settle(self):
        self.eng.wait_ge(self.sem, self.base + self.n)


def load_stage(nc, sem, shared, dram):
    x, wh, wl, cst, sel, rwh, rwl, eb, qb, ob, half, euler = (
        shared[k] for k in ("x", "wh", "wl", "cst", "sel", "rwh", "rwl", "eb", "qb", "ob", "half", "euler"))
    pieces = WCOLS // STAGE
    with ExitStack() as ctx:
        stage = ctx.enter_context(nc.sbuf_tensor("w_stage", [P, pieces, STAGE], F32))
        rw = ctx.enter_context(nc.sbuf_tensor("rw_stage", [P, EXPERTS], F32))
        picks = ctx.enter_context(nc.sbuf_tensor("sel_stage", [P, EXPERTS, P], F32))
        w_in = [sem(f"load_w{n}") for n in range(pieces)]
        c_in, x_in, w_hi, c_hi, split, ones_set = (sem(n) for n in (
            "load_c", "load_x", "load_hi", "load_chi", "load_split", "load_const"))
        with nc.Block() as block:
            @block.sync
            def _(sp):
                sp.dma_start(cst[:], dram["consts"][:, :]).then_inc(c_in, 16)
                sp.dma_start(rw[:], dram["router"][:, :]).then_inc(c_in, 16)
                sp.dma_start(picks[:], dram["selectors"][:, :, :]).then_inc(c_in, 16)
                for n in range(pieces):
                    sp.dma_start(stage[:, n, :], dram["weights"][:, n * STAGE:(n + 1) * STAGE]).then_inc(w_in[n], 16)
                sp.wait_ge(c_in, 48)

            @block.gpsimd
            def _(pool):
                nc.gpsimd.memset(half[:], -0.5)
                nc.gpsimd.memset(euler[:], float(np.float32(np.e))).then_inc(ones_set, 1)
                pool.wait_ge(ones_set, 1)

            @block.scalar
            def _(act):
                act.dma_start(x[:], dram["x"].rearrange("(n p) d -> p n d", p=P)).then_inc(x_in, 16)
                act.dma_start(eb[:], dram["expert_bias"].broadcast_to([P, EXPERTS])).then_inc(x_in, 16)
                act.dma_start(qb[:], dram["qkv_b"].broadcast_to([P, 3 * D])).then_inc(x_in, 16)
                act.dma_start(ob[:], dram["out_b"].broadcast_to([P, D])).then_inc(x_in, 16)
                act.wait_ge(c_in, 48)
                nc.scalar.copy(sel[:], picks[:])
                nc.scalar.copy(rwh[:], rw[:]).then_inc(c_hi, 1)
                for n in range(pieces):
                    act.wait_ge(w_in[n], 16)
                    nc.scalar.copy(wh[:, n * STAGE:(n + 1) * STAGE], stage[:, n, :]).then_inc(w_hi, 1)
                act.wait_ge(x_in, 64)

            @block.vector
            def _(dve):
                dve.wait_ge(c_hi, 1)
                nc.vector.tensor_tensor(rwl[:], rw[:], rwh[:].bitcast(F32), ALU.subtract)
                for n in range(pieces):
                    dve.wait_ge(w_hi, n + 1)
                    part = slice(n * STAGE, (n + 1) * STAGE)
                    last = nc.vector.tensor_tensor(wl[:, part], stage[:, n, :], wh[:, part].bitcast(F32), ALU.subtract)
                last.then_inc(split, 1)
                dve.wait_ge(split, 1)


def three_pass(nc, out, ah, al, bh, bl, start=True, stop=True):
    nc.tensor.matmul(out, ah, bh, start=start, stop=False)
    nc.tensor.matmul(out, ah, bl, start=False, stop=False)
    return nc.tensor.matmul(out, al, bh, start=False, stop=stop)


def norm_stats(nc, dve, s, x, stats, mv, var, fence, b, var_done):
    for t in range(NT):
        last = nc.vector.bn_stats(stats[:, t, :], x[:, bass.ds(b * NT + t, 1), :])
    s.did(last)
    s.settle()
    nc.vector.memset(fence[:], 0.0)
    for t in range(NT):
        last = nc.vector.bn_aggr(mv[:, t, :], stats[:, t, :])
    s.did(last)
    s.settle()
    nc.vector.tensor_scalar(var[:], mv[:, :, 1], LN_EPS, None, ALU.add).then_inc(var_done, 1)


def ffn_stage(nc, sem_of, shared, tag):
    x, wh, wl, cst, sel, rwh, rwl, eb, half, euler = (
        shared[k] for k in ("x", "wh", "wl", "cst", "sel", "rwh", "rwl", "eb", "half", "euler"))
    ident = cst[:, C_ID:C_ID + P]
    rank = cst[:, C_RANK:C_RANK + EXPERTS]
    DEEP = 4
    with ExitStack() as ctx:
        def sb(name, shape, dt=F32):
            return ctx.enter_context(nc.sbuf_tensor(f"{tag}_{name}", shape, dt))

        def pb(name):
            return ctx.enter_context(nc.psum_tensor(f"{tag}_{name}", [P, SEQ], F32))

        def sem(name):
            return sem_of(f"{tag}_{name}")

        silu = sb("silu", [P, DEEP, SEQ])
        scaled = sb("scaled", [P, DEEP, SEQ])
        hid = sb("hid", [P, DEEP, SEQ])
        hid_h = sb("hid_h", [P, DEEP, SEQ], F32R)
        hid_l = sb("hid_l", [P, DEEP, SEQ], F32R)
        xn = sb("xn", [P, NT, D])
        xt_h = sb("xt_h", [P, 2, SEQ], F32R)
        xt_l = sb("xt_l", [P, 2, SEQ], F32R)
        cwb = sb("cwb", [P, 2, EXPERTS, SEQ])
        cwt = sb("cwt", [P, SEQ], F32R)
        cwp = sb("cwp", [P, NT, P])
        yt = sb("yt", [P, SEQ])
        stats = sb("stats", [P, NT, 6])
        mv = sb("mv", [P, NT, 2])
        var = sb("var", [P, NT])
        rstd = sb("rstd", [P, NT])
        fence = sb("fence", [P, 1])
        lg = sb("lg", [P, NT, EXPERTS])
        lg2 = sb("lg2", [P, NT, EXPERTS])
        eq = sb("eq", [P, NT, EXPERTS])
        ranked = sb("ranked", [P, NT, EXPERTS])
        first = sb("first", [P, NT, EXPERTS])
        second = sb("second", [P, NT, EXPERTS])
        cw = sb("cw", [P, NT, EXPERTS])
        cw_h = sb("cw_h", [P, NT, EXPERTS], F32R)
        m1 = sb("m1", [P, NT])
        m2 = sb("m2", [P, NT])
        k1 = sb("k1", [P, NT])
        k2 = sb("k2", [P, NT])
        diff = sb("diff", [P, NT])
        ediff = sb("ediff", [P, NT])
        den = sb("den", [P, NT])
        pr1 = sb("pr1", [P, NT])
        pr2 = sb("pr2", [P, NT])

        G = [pb("gate0"), pb("gate1")]
        U = [pb("up0"), pb("up1")]
        Y = [pb("y0"), pb("y1")]
        M = [pb("misc0"), pb("misc1")]

        gate_done, up_done, down_done = sem("gate_done"), sem("up_done"), sem("down_done")
        silu_done, scaled_done, hid_done = sem("silu_done"), sem("scaled_done"), sem("hid_done")
        hi_done, lo_done = sem("hi_done"), sem("lo_done")
        var_done, rstd_done, xn_done, xnt_done = sem("var_done"), sem("rstd_done"), sem("xn_done"), sem("xnt_done")
        xh_done, xl_done, logits_done = sem("xh_done"), sem("xl_done"), sem("logits_done")
        diff_done, ediff_done, cw_done, cwt_done = sem("diff_done"), sem("ediff_done"), sem("cw_done"), sem("cwt_done")
        cwt_copied, cwb_done, cwb_copied = sem("cwt_copied"), sem("cwb_done"), sem("cwb_copied")
        y_copied, yt_done, x_done = sem("y_copied"), sem("yt_done"), sem("x_done")
        chain = sem("dve_chain")
        CHAIN = 15

        def pe_norm_transpose(pe, b):
            pe.wait_ge(xn_done, b + 1)
            for t in range(NT):
                last = nc.tensor.transpose(M[0][:, t * P:(t + 1) * P], xn[:, t, :], ident)
            last.then_inc(xnt_done, 1)

        def pe_logits(pe, b, par):
            pe.wait_ge(xl_done, b + 1)
            for t in range(NT):
                c = slice(t * P, (t + 1) * P)
                last = three_pass(nc, M[1][:, t * EXPERTS:(t + 1) * EXPERTS],
                                  xt_h[:, par, c], xt_l[:, par, c], rwh[:], rwl[:])
            last.then_inc(logits_done, 1)

        def pe_cw_transpose(pe, b):
            pe.wait_ge(cw_done, b + 1)
            for t in range(NT):
                last = nc.tensor.transpose(M[1][:, t * P:(t + 1) * P], cwp[:, t, :], ident)
            last.then_inc(cwt_done, 1)

        def pe_cw_broadcast(pe, b, e):
            if e == 0:
                pe.wait_ge(cwt_copied, b + 1)
            if e >= 2:
                pe.wait_ge(cwb_copied, b * EXPERTS + e - 1)
            nc.tensor.matmul(M[e % 2][:], sel[:, e, :], cwt[:], start=True, stop=True).then_inc(cwb_done, 1)

        def pe_gate_up(pe, b, c, par, first_seq):
            f, k = divmod(c, HC)
            if c == 0:
                pe.wait_ge(xl_done, b + 1)
            if not (first_seq and c < 2):
                pe.wait_ge(silu_done, b * CHUNKS + c - 1)
            a, o = w1_cols(f, k), w3_cols(f, k)
            three_pass(nc, G[c % 2][:], wh[:, a], wl[:, a], xt_h[:, par, :], xt_l[:, par, :]).then_inc(gate_done, 1)
            if not (first_seq and c < 2):
                pe.wait_ge(hid_done, b * CHUNKS + c - 1)
            three_pass(nc, U[c % 2][:], wh[:, o], wl[:, o], xt_h[:, par, :], xt_l[:, par, :]).then_inc(up_done, 1)

        def pe_down(pe, b, c, par):
            f, k = divmod(c, HC)
            pe.wait_ge(lo_done, b * CHUNKS + c + 1)
            w = w2_cols(f, k)
            three_pass(nc, Y[par][:], wh[:, w], wl[:, w], hid_h[:, c % DEEP, :], hid_l[:, c % DEEP, :],
                       start=(c == 0), stop=(c == CHUNKS - 1)).then_inc(down_done, 1)

        def pe_y_transpose(pe, b):
            pe.wait_ge(y_copied, b + 1)
            for t in range(NT):
                last = nc.tensor.transpose(M[0][:, t * P:(t + 1) * P], yt[:, t * P:(t + 1) * P], ident)
            last.then_inc(yt_done, 1)

        def pe_sequence(pe, b, par, prev, nxt):
            for c in range(CHUNKS):
                pe_gate_up(pe, b, c, par, not prev)
                if c >= 2:
                    pe_down(pe, b, c - 2, par)
                elif prev:
                    pe_down(pe, b - 1, CHUNKS + c - 2, 1 - par)
                if prev and c == 4:
                    pe_y_transpose(pe, b - 1)
                if nxt and c == 8:
                    if prev:
                        pe.wait_ge(x_done, b)
                    pe_norm_transpose(pe, b + 1)
                if nxt and c == 10:
                    pe_logits(pe, b + 1, 1 - par)
                if nxt and c == 14:
                    pe_cw_transpose(pe, b + 1)
                if nxt and c >= 16:
                    pe_cw_broadcast(pe, b + 1, 2 * (c - 16))
                    pe_cw_broadcast(pe, b + 1, 2 * (c - 16) + 1)

        def act_x_hi(act, b, par):
            act.wait_ge(xnt_done, b + 1)
            nc.scalar.copy(xt_h[:, par, :], M[0][:]).then_inc(xh_done, 1)

        def act_cwt(act, b):
            act.wait_ge(cwt_done, b + 1)
            nc.scalar.copy(cwt[:], M[1][:]).then_inc(cwt_copied, 1)

        def act_cwb(act, b, e, par):
            act.wait_ge(cwb_done, b * EXPERTS + e + 1)
            nc.scalar.copy(cwb[:, par, e, :], M[e % 2][:]).then_inc(cwb_copied, 1)

        def act_silu(act, b, c, fresh):
            act.wait_ge(gate_done, b * CHUNKS + c + 1)
            if not fresh:
                act.wait_ge(hid_done, b * CHUNKS + c - DEEP + 1)
            nc.scalar.activation(silu[:, c % DEEP, :], G[c % 2][:], ACT.Silu).then_inc(silu_done, 1)

        def act_hi(act, b, c, fresh):
            act.wait_ge(hid_done, b * CHUNKS + c + 1)
            if not fresh:
                act.wait_ge(down_done, b * CHUNKS + c - DEEP + 1)
            nc.scalar.copy(hid_h[:, c % DEEP, :], hid[:, c % DEEP, :]).then_inc(hi_done, 1)

        def act_y(act, b, par):
            act.wait_ge(down_done, (b + 1) * CHUNKS)
            nc.scalar.copy(yt[:], Y[par][:]).then_inc(y_copied, 1)

        def act_sequence(act, b, par, prev, nxt):
            for c in range(CHUNKS):
                act_silu(act, b, c, not prev and c < DEEP)
                if c >= 1:
                    act_hi(act, b, c - 1, not prev and c - 1 < DEEP)
                elif prev:
                    act_hi(act, b - 1, CHUNKS - 1, False)
                if prev and c == 3:
                    act_y(act, b - 1, 1 - par)
                if nxt and c == 9:
                    act_x_hi(act, b + 1, 1 - par)
                if nxt and c == 15:
                    act_cwt(act, b + 1)
                if nxt and c >= 17:
                    act_cwb(act, b + 1, 2 * (c - 17), 1 - par)
                    act_cwb(act, b + 1, 2 * (c - 17) + 1, 1 - par)
            if nxt:
                act_cwb(act, b + 1, EXPERTS - 2, 1 - par)
                act_cwb(act, b + 1, EXPERTS - 1, 1 - par)

        def pool_rstd(pool, b):
            pool.wait_ge(var_done, b + 1)
            nc.gpsimd.tensor_tensor(rstd[:], var[:], half[:].broadcast_to([P, NT]), ALU.pow).then_inc(rstd_done, 1)

        def pool_exp(pool, b):
            pool.wait_ge(diff_done, b + 1)
            nc.gpsimd.tensor_tensor(ediff[:], euler[:].broadcast_to([P, NT]), diff[:], ALU.pow).then_inc(ediff_done, 1)

        def pool_scale(pool, b, c, par, fresh):
            pool.wait_ge(silu_done, b * CHUNKS + c + 1)
            if c == 0:
                pool.wait_ge(cwb_copied, (b + 1) * EXPERTS)
            if not fresh:
                pool.wait_ge(hid_done, b * CHUNKS + c - DEEP + 1)
            nc.gpsimd.tensor_tensor(scaled[:, c % DEEP, :], silu[:, c % DEEP, :], cwb[:, par, c // HC, :],
                                    ALU.mult).then_inc(scaled_done, 1)

        def pool_sequence(pool, b, par, prev, nxt):
            for c in range(ROUTED):
                pool_scale(pool, b, c, par, not prev and c < DEEP)
                if nxt and c == 5:
                    pool_rstd(pool, b + 1)
                if nxt and c == 12:
                    pool_exp(pool, b + 1)

        def dve_norm(dve, b):
            dve.wait_ge(rstd_done, b + 1)
            for t in range(NT):
                last = nc.vector.tensor_scalar(xn[:, t, :], x[:, bass.ds(b * NT + t, 1), :], mv[:, t, 0:1],
                                               rstd[:, t:t + 1], ALU.subtract, ALU.mult)
            last.then_inc(xn_done, 1)

        def dve_x_lo(dve, b, par):
            dve.wait_ge(xh_done, b + 1)
            nc.vector.tensor_tensor(xt_l[:, par, :], M[0][:], xt_h[:, par, :].bitcast(F32),
                                    ALU.subtract).then_inc(xl_done, 1)

        def dve_pick(s, logits, top, key, onehot):
            wide = [P, NT, EXPERTS]
            s.did(nc.vector.tensor_reduce(top[:], logits[:], AX.X, ALU.max))
            s.settle()
            s.did(nc.vector.tensor_tensor(eq[:], logits[:], top[:].unsqueeze(2).broadcast_to(wide), ALU.is_equal))
            s.settle()
            s.did(nc.vector.tensor_tensor(ranked[:], eq[:], rank.unsqueeze(1).broadcast_to(wide), ALU.mult))
            s.settle()
            s.did(nc.vector.tensor_reduce(key[:], ranked[:], AX.X, ALU.max))
            s.settle()
            return nc.vector.tensor_tensor(onehot[:], ranked[:], key[:].unsqueeze(2).broadcast_to(wide), ALU.is_equal)

        def dve_top_first(dve, s, b):
            dve.wait_ge(logits_done, b + 1)
            s.did(nc.vector.tensor_tensor(lg[:], M[1][:, 0:NT * EXPERTS].rearrange("p (t e) -> p t e", t=NT),
                                          eb[:].unsqueeze(1).broadcast_to([P, NT, EXPERTS]), ALU.add))
            s.settle()
            s.did(dve_pick(s, lg, m1, k1, first))
            s.settle()

        def dve_top_second(dve, s, b):
            s.did(nc.vector.scalar_tensor_tensor(lg2[:], first[:], MASKED, lg[:], ALU.mult, ALU.add))
            s.settle()
            dve_pick(s, lg2, m2, k2, second)
            nc.vector.tensor_tensor(diff[:], m2[:], m1[:], ALU.subtract).then_inc(diff_done, 1)

        def dve_combine(dve, s, b):
            wide = [P, NT, EXPERTS]
            dve.wait_ge(ediff_done, b + 1)
            dve.wait_ge(diff_done, b + 1)
            s.did(nc.vector.tensor_scalar(den[:], ediff[:], 1.0, None, ALU.add))
            s.settle()
            s.did(nc.vector.reciprocal(pr1[:], den[:]))
            s.settle()
            return wide

        def dve_combine_rest(dve, s, b):
            wide = [P, NT, EXPERTS]
            nc.vector.tensor_tensor(eq[:], first[:], pr1[:].unsqueeze(2).broadcast_to(wide), ALU.mult)
            nc.vector.tensor_tensor(pr2[:], ediff[:], pr1[:], ALU.mult).then_inc(pick2, 1)
            dve.wait_ge(pick2, 4 * b + 1)
            nc.vector.tensor_tensor(ranked[:], second[:], pr2[:].unsqueeze(2).broadcast_to(wide), ALU.mult).then_inc(pick2, 1)
            dve.wait_ge(pick2, 4 * b + 2)
            nc.vector.tensor_tensor(cw[:], eq[:], ranked[:], ALU.add).then_inc(pick2, 1)
            dve.wait_ge(pick2, 4 * b + 3)
            nc.vector.tensor_copy(cw_h[:], cw[:]).then_inc(pick2, 1)
            dve.wait_ge(pick2, 4 * b + 4)
            nc.vector.tensor_copy(cwp[:, :, 0:EXPERTS], cw_h[:].bitcast(F32))
            nc.vector.tensor_tensor(cwp[:, :, SLOT:SLOT + EXPERTS], cw[:], cw_h[:].bitcast(F32),
                                    ALU.subtract).then_inc(cw_done, 1)

        pick2 = sem("dve_combine_chain")

        def dve_hidden(dve, b, c, fresh):
            dve.wait_ge(up_done, b * CHUNKS + c + 1)
            if c < ROUTED:
                dve.wait_ge(scaled_done, b * ROUTED + c + 1)
                src = scaled
            else:
                dve.wait_ge(silu_done, b * CHUNKS + c + 1)
                src = silu
            if not fresh:
                dve.wait_ge(lo_done, b * CHUNKS + c - DEEP + 1)
            nc.vector.tensor_tensor(hid[:, c % DEEP, :], src[:, c % DEEP, :], U[c % 2][:], ALU.mult).then_inc(hid_done, 1)

        def dve_lo(dve, b, c, fresh):
            dve.wait_ge(hi_done, b * CHUNKS + c + 1)
            if not fresh:
                dve.wait_ge(down_done, b * CHUNKS + c - DEEP + 1)
            nc.vector.tensor_tensor(hid_l[:, c % DEEP, :], hid[:, c % DEEP, :], hid_h[:, c % DEEP, :].bitcast(F32),
                                    ALU.subtract).then_inc(lo_done, 1)

        def dve_update(dve, b):
            dve.wait_ge(yt_done, b + 1)
            nc.vector.scalar_tensor_tensor(tiles_of(x, b), M[0][:].rearrange("p (t d) -> p t d", t=NT), 0.5,
                                           tiles_of(x, b), ALU.mult, ALU.add).then_inc(x_done, 1)

        def dve_prepare(dve, b, s, part, par):
            if part == 0:
                norm_stats(nc, dve, s, x, stats, mv, var, fence, b, var_done)
            elif part == 1:
                dve_norm(dve, b)
            elif part == 2:
                dve_x_lo(dve, b, par)
            elif part == 3:
                dve_top_first(dve, s, b)
            elif part == 4:
                dve_top_second(dve, s, b)
            elif part == 5:
                dve_combine(dve, s, b)
                dve_combine_rest(dve, s, b)
                assert s.n == CHAIN, s.n

        PARTS = {5: 0, 7: 1, 9: 2, 11: 3, 12: 4, 13: 5}

        def dve_sequence(dve, b, par, prev, nxt):
            s = Steps(dve, chain, (b + 1) * CHAIN)
            for c in range(CHUNKS):
                dve_hidden(dve, b, c, not prev and c < DEEP)
                if c >= 1:
                    dve_lo(dve, b, c - 1, not prev and c - 1 < DEEP)
                elif prev:
                    dve_lo(dve, b - 1, CHUNKS - 1, False)
                if prev and c == 4:
                    dve_update(dve, b - 1)
                if nxt and c in PARTS:
                    dve_prepare(dve, b + 1, s, PARTS[c], 1 - par)

        def every_sequence(eng, body):
            body(eng, 0, 0, False, True)
            with eng.Fori(0, (BATCH - 2) // 2) as i:
                body(eng, 2 * i + 1, 1, True, True)
                body(eng, 2 * i + 2, 0, True, True)
            body(eng, BATCH - 1, 1, True, False)

        END = BATCH - 1
        with nc.Block() as block:
            @block.tensor
            def _(pe):
                pe_norm_transpose(pe, 0)
                pe_logits(pe, 0, 0)
                pe_cw_transpose(pe, 0)
                for e in range(EXPERTS):
                    pe_cw_broadcast(pe, 0, e)
                every_sequence(pe, pe_sequence)
                pe_down(pe, END, CHUNKS - 2, 1)
                pe_down(pe, END, CHUNKS - 1, 1)
                pe_y_transpose(pe, END)

            @block.scalar
            def _(act):
                act_x_hi(act, 0, 0)
                act_cwt(act, 0)
                for e in range(EXPERTS):
                    act_cwb(act, 0, e, 0)
                every_sequence(act, act_sequence)
                act_hi(act, END, CHUNKS - 1, False)
                act_y(act, END, 1)

            @block.gpsimd
            def _(pool):
                pool_rstd(pool, 0)
                pool_exp(pool, 0)
                every_sequence(pool, pool_sequence)

            @block.vector
            def _(dve):
                nc.vector.memset(cwp[:], 0.0)
                s = Steps(dve, chain, 0)
                for part in range(6):
                    dve_prepare(dve, 0, s, part, 0)
                every_sequence(dve, dve_sequence)
                dve_lo(dve, END, CHUNKS - 1, False)
                dve_update(dve, END)
                dve.wait_ge(x_done, BATCH)


def store_stage(nc, sem_of, shared, dram):
    done = sem_of("stored")
    with nc.Block() as block:
        @block.sync
        def _(sp):
            sp.dma_start(dram["out"].rearrange("(n p) d -> p n d", p=P), shared["x"][:]).then_inc(done, 16)
            sp.wait_ge(done, 16)


def attention_stage(nc, sem_of, shared):
    x, wh, wl, cst, qb, ob, half = (shared[k] for k in ("x", "wh", "wl", "cst", "qb", "ob", "half"))
    ident = cst[:, C_ID:C_ID + P]
    cos = cst[:, C_COS:C_COS + NT * HD].rearrange("p (t d) -> p t d", t=NT)
    sin = cst[:, C_SIN:C_SIN + NT * HD].rearrange("p (t f two) -> p t f two", t=NT, two=2)
    GROUPS = HEADS // 4
    GU = 8
    HU = GU // 2
    UNITS = GROUPS * GU
    KT = NT
    SCALE = HD ** -0.5
    QK = 2 * HEADS
    with ExitStack() as ctx:
        def sb(name, shape, dt=F32):
            return ctx.enter_context(nc.sbuf_tensor(f"attn_{name}", shape, dt))

        def pb(name, cols=SEQ):
            return ctx.enter_context(nc.psum_tensor(f"attn_{name}", [P, cols], F32))

        def sem(name):
            return sem_of(f"attn_{name}")

        id16 = sb("id16", [P, P], F16)
        xn = sb("xn", [P, NT, D])
        xt_h = sb("xt_h", [P, SEQ], F32R)
        xt_l = sb("xt_l", [P, SEQ], F32R)
        qk = sb("qk", [P, NT, QK * HD])
        ca = sb("ca", [P, NT, QK, HD])
        sa = sb("sa", [P, NT, QK, HD])
        rot = qk[:].rearrange("p t (h d) -> p t h d", h=QK)
        ss = sb("ss", [P, NT * QK])
        lnss = sb("lnss", [P, NT * QK])
        r0 = sb("r0", [P, NT * QK])
        r1 = sb("r1", [P, NT * QK])
        r2 = sb("r2", [P, NT * QK])
        inv = sb("inv", [P, NT, QK])
        unit = ca[:].rearrange("p t h d -> p (t h d)").rearrange("p (a n d) -> p a n d", a=2, d=HD)
        stack = sb("stack", [P, 2, NT, HEADS, SLOT], F16)
        qkt = sb("qkt", [P, 2, 2 * GROUPS, SEQ], F16)
        ve = sb("ve", [P, 2, KT, HEADS, SLOT])
        pr = sb("pr", [P, 2, 4, 2, SEQ])
        avs = sb("avs", [P, GROUPS, SEQ])
        rs = sb("rs", [P, NT, HEADS])
        on = sb("on", [P, NT, HEADS, HD])
        ot_h, ot_l = xt_h, xt_l
        po = xn
        stats = sb("stats", [P, NT, 6])
        mv = sb("mv", [P, NT, 2])
        var = sb("var", [P, NT])
        rstd = sb("rstd", [P, NT])
        fence = sb("fence", [P, 1])

        S = [pb("scores0", 2 * SEQ), pb("scores1", 2 * SEQ)]
        AV = [pb("av0"), pb("av1")]
        M = [pb("misc0"), pb("misc1")]

        ready_chain, ready, scores_done, exp_done = sem("ready_chain"), sem("ready"), sem("scores_done"), sem("exp_done")
        av_done, av_copied = sem("av_done"), sem("av_copied")
        var_done, rstd_done, xn_done, xnt_done = sem("var_done"), sem("rstd_done"), sem("xn_done"), sem("xnt_done")
        xh_done, xl_done, qkv_done, qkv_copied = sem("xh_done"), sem("xl_done"), sem("qkv_done"), sem("qkv_copied")
        ss_done, ln_done, r0_done, stacked = sem("ss_done"), sem("ln_done"), sem("r0_done"), sem("stacked")
        qkt_done, qkt_copied = sem("qkt_done"), sem("qkt_copied")
        o_done, on_done, ont_done, oh_done, ol_done = (sem("o_done"), sem("on_done"), sem("ont_done"),
                                                       sem("oh_done"), sem("ol_done"))
        po_done, x_done = sem("po_done"), sem("x_done")
        chain_p, chain_e = sem("dve_chain_prepare"), sem("dve_chain_epilogue")
        CHAIN_P, CHAIN_E = 12, NT + 1

        def pe_xnt(pe, b):
            pe.wait_ge(xn_done, b + 1)
            for t in range(NT):
                last = nc.tensor.transpose(M[0][:, t * P:(t + 1) * P], xn[:, t, :], ident)
            last.then_inc(xnt_done, 1)

        def pe_qkv(pe, b, t, prev):
            if t == 0:
                pe.wait_ge(xl_done, b + 1)
            if t < 2 and prev:
                pe.wait_ge(on_done, (b - 2) * NT + t + 3)
            if t >= 2:
                pe.wait_ge(qkv_copied, b * NT + t - 1)
            c = slice(t * P, (t + 1) * P)
            w = slice(QKV0, QKV0 + 3 * D)
            three_pass(nc, M[1 - t % 2][:, 0:3 * D], xt_h[:, c], xt_l[:, c], wh[:, w], wl[:, w]).then_inc(qkv_done, 1)

        def pe_qkt(pe, b, t, prev):
            if t == 0:
                pe.wait_ge(stacked, b + 1)
            if t == 1 and prev:
                pe.wait_ge(x_done, b - 1)
            if t >= 2:
                pe.wait_ge(qkt_copied, b * NT + t - 1)
            bank = M[1 - t % 2][:].bitcast(F16)
            for a in range(2):
                for g in range(GROUPS):
                    n = a * GROUPS + g
                    last = nc.tensor.transpose(bank[:, n * P:(n + 1) * P],
                                               stack[:, a, t, 4 * g:4 * g + 4, :].rearrange("p h s -> p (h s)"), id16[:])
            last.then_inc(qkt_done, 1)

        def pe_scores(pe, b, u, par, fresh):
            g, side, j = u // GU, (u % GU) // HU, u % HU
            if u == 0:
                pe.wait_ge(qkt_copied, (b + 1) * NT)
            if not fresh:
                pe.wait_ge(exp_done, b * UNITS + u - 1)
            rows = slice(SLOT * j, SLOT * (j + 1))
            for n in range(2):
                kt = 2 * side + n
                last = nc.tensor.matmul(S[u % 2][:, n * SEQ:(n + 1) * SEQ],
                                        qkt[rows, par, GROUPS + g, kt * P:(kt + 1) * P],
                                        qkt[rows, par, g, :], start=True, stop=True, tile_position=(SLOT * j, 0))
            last.then_inc(scores_done, 1)

        def pe_av(pe, b, h, n, par, fresh):
            g, kt = h // 2, 2 * (h % 2) + n
            if n == 0:
                pe.wait_ge(exp_done, b * UNITS + (h + 1) * HU)
                if kt == 0 and not fresh:
                    pe.wait_ge(av_copied, b * GROUPS + g - 1)
            for j in range(4):
                last = nc.tensor.matmul(AV[g % 2][SLOT * j:SLOT * (j + 1), :], ve[:, par, kt, 4 * g + j, :],
                                        pr[:, h % 2, j, n, :], start=(kt == 0), stop=(kt == KT - 1),
                                        tile_position=(0, SLOT * j))
            if n == 1:
                last.then_inc(av_done, 1)

        def pe_o(pe, b, t, nxt):
            if t == 0:
                pe.wait_ge(av_copied, (b + 1) * GROUPS)
            if t == 1 and nxt:
                pe.wait_ge(xl_done, b + 3)
            if t >= 2:
                pe.wait_ge(on_done, b * NT + t - 1)
            for g in range(GROUPS):
                last = nc.tensor.transpose(M[1 - t % 2][:, g * P:(g + 1) * P], avs[:, g, t * P:(t + 1) * P], ident)
            last.then_inc(o_done, 1)

        def pe_ont(pe, b, nxt):
            pe.wait_ge(on_done, (b + 1) * NT)
            if nxt:
                pe.wait_ge(qkv_copied, (b + 3) * NT - 1)
            for t in range(NT):
                last = nc.tensor.transpose(M[1][:, t * P:(t + 1) * P], on[:, t, :, :].rearrange("p h d -> p (h d)"), ident)
            last.then_inc(ont_done, 1)

        def pe_project(pe, b, nxt):
            pe.wait_ge(ol_done, b + 1)
            if nxt:
                pe.wait_ge(qkv_copied, (b + 3) * NT)
            w = slice(OUT0, OUT0 + D)
            for t in range(NT):
                c = slice(t * P, (t + 1) * P)
                last = three_pass(nc, M[0][:, t * D:(t + 1) * D], ot_h[:, c], ot_l[:, c], wh[:, w], wl[:, w])
            last.then_inc(po_done, 1)

        def pe_sequence(pe, b, par, prev, nxt):
            for u in range(UNITS):
                pe_scores(pe, b, u, par, not prev and u < 2)
                if u % 2 == 1:
                    n = (u % HU) // 2
                    if u >= HU:
                        h = u // HU - 1
                        pe_av(pe, b, h, n, par, not prev and h < 4)
                    elif prev:
                        pe_av(pe, b - 1, 2 * GROUPS - 1, n, 1 - par, False)
                if nxt and u == 4:
                    pe_xnt(pe, b + 1)
                if nxt and 11 <= u < 15:
                    pe_qkv(pe, b + 1, u - 11, prev)
                if prev and 6 <= u < 10:
                    pe_o(pe, b - 1, u - 6, nxt)
                if prev and u == 17:
                    pe_ont(pe, b - 1, nxt)
                if prev and u == 19:
                    pe_project(pe, b - 1, nxt)
                if nxt and 24 <= u < 28:
                    pe_qkt(pe, b + 1, u - 24, prev)

        def act_exp(act, b, u, fresh):
            h, j = u // HU, u % HU
            act.wait_ge(scores_done, b * UNITS + u + 1)
            if j == 0 and not fresh:
                act.wait_ge(av_done, b * 2 * GROUPS + h - 1)
            nc.scalar.activation(pr[:, h % 2, j, :, :].rearrange("p k q -> p (k q)"),
                                 S[u % 2][:], ACT.Exp, scale=SCALE).then_inc(exp_done, 1)

        def act_x_hi(act, b):
            act.wait_ge(xnt_done, b + 1)
            nc.scalar.copy(xt_h[:], M[0][:]).then_inc(xh_done, 1)

        def act_root(act, b):
            act.wait_ge(ss_done, b + 1)
            nc.scalar.activation(lnss[:], ss[:], ACT.Ln, scale=LN_SCALE).then_inc(ln_done, 1)
            act.wait_ge(ln_done, b + 1)
            nc.scalar.activation(r0[:], lnss[:], ACT.Exp, scale=-0.5).then_inc(r0_done, 1)

        def act_o_hi(act, b):
            act.wait_ge(ont_done, b + 1)
            nc.scalar.copy(ot_h[:], M[1][:]).then_inc(oh_done, 1)

        def act_sequence(act, b, par, prev, nxt):
            for u in range(UNITS):
                act_exp(act, b, u, not prev and u < 2 * GU)
                if nxt and u == 5:
                    act_x_hi(act, b + 1)
                if nxt and u == 19:
                    act_root(act, b + 1)
                if prev and u == 18:
                    act_o_hi(act, b - 1)

        def pool_rstd(pool, b):
            pool.wait_ge(var_done, b + 1)
            nc.gpsimd.tensor_tensor(rstd[:], var[:], half[:].broadcast_to([P, NT]), ALU.pow).then_inc(rstd_done, 1)

        def dve_av_copy(dve, b, g, overwrites):
            dve.wait_ge(av_done, 2 * (b * GROUPS + g + 1))
            if overwrites:
                dve.wait_ge(o_done, b * NT)
            nc.vector.tensor_copy(avs[:, g, :], AV[g % 2][:]).then_inc(av_copied, 1)

        def dve_norm(dve, b):
            dve.wait_ge(rstd_done, b + 1)
            for t in range(NT):
                last = nc.vector.tensor_scalar(xn[:, t, :], x[:, bass.ds(b * NT + t, 1), :], mv[:, t, 0:1],
                                               rstd[:, t:t + 1], ALU.subtract, ALU.mult)
            last.then_inc(xn_done, 1)

        def dve_x_lo(dve, b):
            dve.wait_ge(xh_done, b + 1)
            nc.vector.tensor_tensor(xt_l[:], M[0][:], xt_h[:].bitcast(F32), ALU.subtract).then_inc(xl_done, 1)

        def dve_qkv(dve, b, t, par):
            dve.wait_ge(qkv_done, b * NT + t + 1)
            bank = M[1 - t % 2]
            nc.vector.tensor_tensor(qk[:, t, :], bank[:, 0:2 * D], qb[:, 0:2 * D], ALU.add)
            nc.vector.tensor_tensor(ve[:, par, t, :, 0:HD], bank[:, 2 * D:3 * D].rearrange("p (h d) -> p h d", h=HEADS),
                                    qb[:, 2 * D:3 * D].rearrange("p (h d) -> p h d", h=HEADS), ALU.add).then_inc(qkv_copied, 1)

        def dve_rotate(dve, s, b):
            heads = qk[:].rearrange("p t (h d) -> p t h d", h=QK)
            pairs = qk[:].rearrange("p t (h f two) -> p t h f two", h=QK, two=2)
            spair = sa[:].rearrange("p t h (f two) -> p t h f two", two=2)
            half_wide = [P, NT, QK, HD // 2]
            dve.wait_ge(qkv_copied, (b + 1) * NT)
            nc.vector.tensor_tensor(ca[:], heads, cos.unsqueeze(2).broadcast_to([P, NT, QK, HD]), ALU.mult)
            for i in range(2):
                last = nc.vector.tensor_tensor(spair[:, :, :, :, i], pairs[:, :, :, :, 1 - i],
                                               sin[:, :, :, i].unsqueeze(2).broadcast_to(half_wide), ALU.mult)
            s.did(last)
            s.settle()

        def dve_squares(dve, s, b):
            s.did(nc.vector.tensor_tensor(rot, ca[:], sa[:], ALU.add))
            s.settle()
            s.did(nc.vector.tensor_tensor(sa[:], rot, rot, ALU.mult))
            s.settle()
            s.did(nc.vector.tensor_reduce(r1[:].rearrange("p (t h) -> p t h", t=NT), sa[:], AX.X, ALU.add))
            s.settle()
            nc.vector.tensor_scalar(ss[:], r1[:], NORM_EPS2, None, ALU.max).then_inc(ss_done, 1)

        def dve_refine(dve, s, b):
            dve.wait_ge(r0_done, b + 1)
            s.did(nc.vector.tensor_tensor(r1[:], r0[:], r0[:], ALU.mult))
            s.settle()
            s.did(nc.vector.tensor_tensor(r2[:], r1[:], ss[:], ALU.mult))
            s.settle()
            s.did(nc.vector.tensor_scalar(r1[:], r2[:], -0.5 * LN_SCALE, 1.5, ALU.mult, ALU.add))
            s.settle()
            s.did(nc.vector.scalar_tensor_tensor(inv[:].rearrange("p t h -> p (t h)"), r0[:], LN_SCALE ** 0.5, r1[:],
                                                 ALU.mult, ALU.mult))
            s.settle()

        def dve_unit(dve, s, b):
            for a in range(2):
                hs = slice(a * HEADS, (a + 1) * HEADS)
                last = nc.vector.tensor_tensor(unit[:, a, :, :].rearrange("p (t h) d -> p t h d", t=NT), rot[:, :, hs, :],
                                               inv[:, :, hs].unsqueeze(3).broadcast_to([P, NT, HEADS, HD]), ALU.mult)
            s.did(last)
            s.settle()

        def dve_stack(dve, s, b):
            th = NT * HEADS
            q = stack[:, 0, :, :, :].rearrange("p t h s -> p (t h) s")
            k = stack[:, 1, :, :, :].rearrange("p t h s -> p (t h) s")
            q4 = q.rearrange("p n (c d) -> p n c d", d=HD)
            k4 = k.rearrange("p n (c d) -> p n c d", d=HD)
            nc.vector.tensor_copy(q4[:, :, 0:2, :], unit[:, 0, :, :].unsqueeze(2).broadcast_to([P, th, 2, HD]))
            s.did(nc.vector.tensor_copy(k4[:, :, 0:3:2, :], unit[:, 1, :, :].unsqueeze(2).broadcast_to([P, th, 2, HD])))
            s.settle()
            nc.vector.tensor_tensor(q4[:, :, 2, :], unit[:, 0, :, :], q4[:, :, 0, :], ALU.subtract)
            nc.vector.tensor_tensor(k4[:, :, 1, :], unit[:, 1, :, :], k4[:, :, 0, :], ALU.subtract).then_inc(stacked, 1)

        def dve_qkt(dve, b, t, par):
            dve.wait_ge(qkt_done, b * NT + t + 1)
            nc.vector.tensor_copy(qkt[:, par, :, t * P:(t + 1) * P],
                                  M[1 - t % 2][:].bitcast(F16).rearrange("p (n c) -> p n c", c=P)).then_inc(qkt_copied, 1)

        def dve_o(dve, s, b, t):
            dve.wait_ge(o_done, b * NT + t + 1)
            heads = M[1 - t % 2][:].rearrange("p (h s) -> p h s", h=HEADS)
            s.did(nc.vector.reciprocal(rs[:, t, :], heads[:, :, HD]))
            s.settle()
            nc.vector.tensor_tensor(on[:, t, :, :], heads[:, :, 0:HD], rs[:, t, :].unsqueeze(2).broadcast_to([P, HEADS, HD]),
                                    ALU.mult).then_inc(on_done, 1)

        def dve_o_lo(dve, b):
            dve.wait_ge(oh_done, b + 1)
            nc.vector.tensor_tensor(ot_l[:], M[1][:], ot_h[:].bitcast(F32), ALU.subtract).then_inc(ol_done, 1)

        def dve_update(dve, s, b):
            dve.wait_ge(po_done, b + 1)
            s.did(nc.vector.tensor_tensor(po[:], M[0][:].rearrange("p (t d) -> p t d", t=NT),
                                          ob[:].unsqueeze(1).broadcast_to([P, NT, D]), ALU.add))
            s.settle()
            nc.vector.tensor_tensor(tiles_of(x, b), tiles_of(x, b), po[:], ALU.add).then_inc(x_done, 1)

        def dve_sequence(dve, b, par, prev, nxt):
            p = Steps(dve, chain_p, (b + 1) * CHAIN_P)
            e = Steps(dve, chain_e, (b - 1) * CHAIN_E) if prev else None
            for u in range(UNITS):
                if prev and u == HU:
                    dve_av_copy(dve, b - 1, GROUPS - 1, False)
                if u % GU == HU and u > HU:
                    dve_av_copy(dve, b, u // GU - 1, prev and u < 2 * GU)
                if nxt and u == 0:
                    norm_stats(nc, dve, p, x, stats, mv, var, fence, b + 1, var_done)
                if nxt and u == 2:
                    dve_norm(dve, b + 1)
                if nxt and u == 5:
                    dve_x_lo(dve, b + 1)
                if prev and 7 <= u < 11:
                    dve_o(dve, e, b - 1, u - 7)
                if nxt and 12 <= u < 16:
                    dve_qkv(dve, b + 1, u - 12, 1 - par)
                if nxt and u == 16:
                    dve_rotate(dve, p, b + 1)
                if prev and u == 18:
                    dve_o_lo(dve, b - 1)
                if nxt and u == 18:
                    dve_squares(dve, p, b + 1)
                if prev and u == 20:
                    dve_update(dve, e, b - 1)
                if nxt and u == 21:
                    dve_refine(dve, p, b + 1)
                    dve_unit(dve, p, b + 1)
                if nxt and u == 23:
                    dve_stack(dve, p, b + 1)
                if nxt and 25 <= u < 29:
                    dve_qkt(dve, b + 1, u - 25, 1 - par)
            assert not nxt or p.n == CHAIN_P, p.n
            assert not prev or e.n == CHAIN_E, e.n

        def every_sequence(eng, body):
            body(eng, 0, 0, False, True)
            with eng.Fori(0, (BATCH - 2) // 2) as i:
                body(eng, 2 * i + 1, 1, True, True)
                body(eng, 2 * i + 2, 0, True, True)
            body(eng, BATCH - 1, 1, True, False)

        END = BATCH - 1
        with nc.Block() as block:
            @block.tensor
            def _(pe):
                pe_xnt(pe, 0)
                pe.wait_ge(ready, 1)
                for t in range(NT):
                    pe_qkv(pe, 0, t, False)
                for t in range(NT):
                    pe_qkt(pe, 0, t, False)
                every_sequence(pe, pe_sequence)
                for n in range(2):
                    pe_av(pe, END, 2 * GROUPS - 1, n, 1, False)
                for t in range(NT):
                    pe_o(pe, END, t, False)
                pe_ont(pe, END, False)
                pe_project(pe, END, False)

            @block.scalar
            def _(act):
                nc.scalar.preload_act_table_set("natural_log_exp_and_others")
                act_x_hi(act, 0)
                act_root(act, 0)
                every_sequence(act, act_sequence)
                act_o_hi(act, END)

            @block.gpsimd
            def _(pool):
                pool_rstd(pool, 0)
                pool_rstd(pool, 1)
                with pool.Fori(2, BATCH) as b:
                    pool_rstd(pool, b)

            @block.vector
            def _(dve):
                nc.vector.memset(ve[:], 0.0).then_inc(ready_chain, 1)
                nc.vector.memset(stack[:], 0.0)
                nc.vector.tensor_copy(id16[:], ident)
                dve.wait_ge(ready_chain, 1)
                nc.vector.memset(ve[:, :, :, :, HD:HD + 1], 1.0).then_inc(ready, 1)
                dve.wait_ge(ready, 1)
                p = Steps(dve, chain_p, 0)
                norm_stats(nc, dve, p, x, stats, mv, var, fence, 0, var_done)
                dve_norm(dve, 0)
                dve_x_lo(dve, 0)
                for t in range(NT):
                    dve_qkv(dve, 0, t, 0)
                dve_rotate(dve, p, 0)
                dve_squares(dve, p, 0)
                dve_refine(dve, p, 0)
                dve_unit(dve, p, 0)
                dve_stack(dve, p, 0)
                assert p.n == CHAIN_P, p.n
                for t in range(NT):
                    dve_qkt(dve, 0, t, 0)
                every_sequence(dve, dve_sequence)
                e = Steps(dve, chain_e, END * CHAIN_E)
                dve_av_copy(dve, END, GROUPS - 1, False)
                for t in range(NT):
                    dve_o(dve, e, END, t)
                dve_o_lo(dve, END)
                dve_update(dve, e, END)
                dve.wait_ge(x_done, BATCH)



def macaron_block(nc, x, weights, router, expert_bias, qkv_b, out_b, consts, selectors, out, stages=("ffn1", "attn", "ffn2")):
    dram = dict(x=x, weights=weights, router=router, expert_bias=expert_bias, qkv_b=qkv_b, out_b=out_b,
                consts=consts, selectors=selectors, out=out)
    with ExitStack() as ctx:
        def sb(name, shape, dt=F32):
            return ctx.enter_context(nc.sbuf_tensor(name, shape, dt))

        def sem(name):
            return ctx.enter_context(nc.semaphore(name))

        shared = dict(
            x=sb("x_res", [P, TILES, D]), wh=sb("w_hi", [P, WCOLS], F32R), wl=sb("w_lo", [P, WCOLS], F32R),
            cst=sb("cst", [P, C_ALL]), sel=sb("sel", [P, EXPERTS, P], F32R),
            rwh=sb("rw_hi", [P, EXPERTS], F32R), rwl=sb("rw_lo", [P, EXPERTS], F32R),
            eb=sb("expert_bias_row", [P, EXPERTS]), qb=sb("qkv_bias_row", [P, 3 * D]), ob=sb("out_bias_row", [P, D]),
            half=sb("minus_half", [P, 1]), euler=sb("euler", [P, 1]))
        load_stage(nc, sem, shared, dram)
        if "ffn1" in stages:
            ffn_stage(nc, sem, shared, "ffn1")
        if "attn" in stages:
            attention_stage(nc, sem, shared)
        if "ffn2" in stages:
            ffn_stage(nc, sem, shared, "ffn2")
        store_stage(nc, sem, shared, dram)


def constant_table():
    c = np.zeros((P, C_ALL), np.float32)
    c[:, C_ID:C_ID + P] = np.eye(P, dtype=np.float32)
    c[:, C_RANK:C_RANK + EXPERTS] = EXPERTS - np.arange(EXPERTS)
    freqs = np.arange(HD // 2, dtype=np.float32)
    inv = (np.float32(1.0) / np.float32(1250) ** (freqs / np.float32(HD // 2))).astype(np.float32)
    theta = (np.arange(SEQ, dtype=np.float32)[:, None] * inv[None, :]).astype(np.float32)
    cos = np.repeat(np.cos(theta), 2, axis=1).reshape(NT, P, HD).transpose(1, 0, 2)
    sin = np.stack([-np.sin(theta), np.sin(theta)], axis=-1).reshape(NT, P, HD).transpose(1, 0, 2)
    c[:, C_COS:C_COS + NT * HD] = cos.reshape(P, NT * HD)
    c[:, C_SIN:C_SIN + NT * HD] = sin.reshape(P, NT * HD)
    return c


def selector_table():
    c = np.zeros((P, EXPERTS, P), np.float32)
    for e in range(EXPERTS):
        c[[e, SLOT + e], e, :] = 1.0
    return c


def kernel(**inputs):
    import concourse.bacc as bacc
    from concourse.bass_utils import run_bass_kernel_spmd

    g = {k.removeprefix("L0_"): np.asarray(v) for k, v in inputs.items()}
    cat = np.concatenate
    w1 = cat([g["ffn_w1"], g["ffn_sw1"]]).transpose(2, 0, 1)
    w3 = cat([g["ffn_w3"], g["ffn_sw3"]]).transpose(2, 0, 1)
    w2 = cat([g["ffn_w2"], g["ffn_sw2"]]).transpose(2, 0, 1)
    w2 = w2.reshape(HC, P, FFNS, D).transpose(1, 2, 0, 3).reshape(P, FFNS, HC * D)
    ffn = cat([w1, w3, w2], axis=2).reshape(P, QKV0)
    arrays = {
        "x": g["attn_tokens"].reshape(BATCH * SEQ, D),
        "weights": cat([ffn, g["attn_qkv_w"].T, g["attn_out_w"].T], axis=1),
        "router": g["ffn_router_w"].T,
        "expert_bias": g["ffn_expert_bias"].reshape(1, EXPERTS),
        "qkv_b": g["attn_qkv_b"].reshape(1, 3 * D),
        "out_b": g["attn_out_b"].reshape(1, D),
        "consts": constant_table(),
        "selectors": selector_table(),
    }
    arrays = {k: np.ascontiguousarray(v) for k, v in arrays.items()}
    nc = bacc.Bacc("TRN2", target_bir_lowering=False, num_devices=1)
    args = [nc.dram_tensor(f"in_{k}", a.shape, mybir.dt.from_np(a.dtype), kind="ExternalInput").ap()
            for k, a in arrays.items()]
    args.append(nc.dram_tensor("out", (BATCH * SEQ, D), F32, kind="ExternalOutput").ap())
    macaron_block(nc, *args)
    r = run_bass_kernel_spmd(nc, [{f"in_{k}": a for k, a in arrays.items()}], core_ids=[0])
    return r.results[0]["out"].reshape(BATCH, SEQ, D)
```

```python
from contextlib import ExitStack, contextmanager

import numpy as np
import concourse.bass as bass
from concourse import mybir

F32 = mybir.dt.float32
F32R = mybir.dt.float32r
F16 = mybir.dt.float16
I32 = mybir.dt.int32
ALU = mybir.AluOpType
ACT = mybir.ActivationFunctionType
AX = mybir.AxisListType

P = 128
D = 128
BATCH, SEQ = 16, 512
NT = SEQ // P
TILES = BATCH * NT
HEADS, HD = 16, 8
HID = 256
EXPERTS, SHARED = 8, 2
FFNS = EXPERTS + SHARED
HC = HID // P
HALVES = 2
GROUP = BATCH // HALVES
HTILES = TILES // HALVES
BLOCKS = 2 * HTILES + EXPERTS
PAIRS = BLOCKS // 2
ZERO_PARTS = 8
FW = 3 * HID
QKV0 = FFNS * FW
OUT0 = QKV0 + 3 * D
WCOLS = OUT0 + D
STAGE = 1024
LN_EPS = 1e-5
NORM_EPS2 = 1e-24
MASKED = -3.0e38
LN_SCALE = 2.0 ** 16
SLOT = 32

C_ID, C_RANK = 0, P
C_COS = C_RANK + EXPERTS
C_SIN = C_COS + NT * HD
C_TRI = C_SIN + NT * HD
C_BLOCK = C_TRI + P
C_RESTART = C_BLOCK + BLOCKS
C_ALL = C_RESTART + TILES * EXPERTS


def w1_cols(f, k):
    return slice(f * FW + k * P, f * FW + (k + 1) * P)


def w3_cols(f, k):
    return slice(f * FW + HID + k * P, f * FW + HID + (k + 1) * P)


def w2_cols(f, k):
    return slice(f * FW + 2 * HID + k * D, f * FW + 2 * HID + (k + 1) * D)


def tiles_of(x, b):
    return x[:, bass.ds(b * NT, NT), :]


class Steps:

    def __init__(self, eng, sem, base):
        self.eng, self.sem, self.base, self.n = eng, sem, base, 0

    def did(self, instruction):
        self.n += 1
        return instruction.then_inc(self.sem, 1)

    def settle(self):
        self.eng.wait_ge(self.sem, self.base + self.n)


@contextmanager
def stage_semaphores(nc):
    used = []

    def sem(name):
        used.append(nc.alloc_semaphore(name=name))
        return used[-1]

    yield sem
    nc.all_engine_barrier()
    nc.clear_and_free_semaphores(used)
    nc.all_engine_barrier()


def load_stage(nc, sem, shared, dram):
    x, wh, wl, cst, rwh, rwl, eb, qb, ob, half, euler, ones16, tri16 = (shared[k] for k in (
        "x", "wh", "wl", "cst", "rwh", "rwl", "eb", "qb", "ob", "half", "euler", "ones16", "tri16"))
    pieces = WCOLS // STAGE
    with ExitStack() as ctx:
        stage = ctx.enter_context(nc.sbuf_tensor("w_stage", [P, pieces, STAGE], F32))
        rw = ctx.enter_context(nc.sbuf_tensor("rw_stage", [P, EXPERTS], F32))
        zeros = ctx.enter_context(nc.sbuf_tensor("zeros", [P, BLOCKS // ZERO_PARTS, D], F32))
        zeros_set = sem("load_zeros")
        w_in = [sem(f"load_w{n}") for n in range(pieces)]
        c_in, x_in, w_hi, c_hi, split, ones_set = (sem(n) for n in (
            "load_c", "load_x", "load_hi", "load_chi", "load_split", "load_const"))
        with nc.Block() as block:
            @block.sync
            def _(sp):
                sp.dma_start(cst[:], dram["consts"][:, :]).then_inc(c_in, 16)
                sp.dma_start(rw[:], dram["router"][:, :]).then_inc(c_in, 16)
                for n in range(pieces):
                    sp.dma_start(stage[:, n, :], dram["weights"][:, n * STAGE:(n + 1) * STAGE]).then_inc(w_in[n], 16)
                sp.wait_ge(c_in, 32)

            @block.gpsimd
            def _(pool):
                nc.gpsimd.memset(half[:], -0.5)
                nc.gpsimd.memset(ones16[:], 1.0)
                nc.gpsimd.memset(euler[:], float(np.float32(np.e))).then_inc(ones_set, 1)
                pool.wait_ge(ones_set, 1)
                pool.wait_ge(zeros_set, 1)
                w = BLOCKS // ZERO_PARTS
                for h in range(HALVES):
                    slots = dram["x_slots"][h].rearrange("(n p) d -> p n d", p=P)
                    for n in range(ZERO_PARTS):
                        nc.gpsimd.dma_start(slots[:, n * w:(n + 1) * w, :], zeros[:]).then_inc(shared["zeroed"], 16)
                pool.wait_ge(shared["zeroed"], HALVES * 16 * ZERO_PARTS)

            @block.scalar
            def _(act):
                act.dma_start(x[:], dram["x"].rearrange("(n p) d -> p n d", p=P)).then_inc(x_in, 16)
                act.dma_start(eb[:], dram["expert_bias"].broadcast_to([P, EXPERTS])).then_inc(x_in, 16)
                act.dma_start(qb[:], dram["qkv_b"].broadcast_to([P, 3 * D])).then_inc(x_in, 16)
                act.dma_start(ob[:], dram["out_b"].broadcast_to([P, D])).then_inc(x_in, 16)
                act.wait_ge(c_in, 32)
                nc.scalar.copy(tri16[:], cst[:, C_TRI:C_TRI + P])
                nc.scalar.copy(rwh[:], rw[:]).then_inc(c_hi, 1)
                for n in range(pieces):
                    act.wait_ge(w_in[n], 16)
                    nc.scalar.copy(wh[:, n * STAGE:(n + 1) * STAGE], stage[:, n, :]).then_inc(w_hi, 1)
                act.wait_ge(x_in, 64)

            @block.vector
            def _(dve):
                nc.vector.memset(zeros[:], 0.0).then_inc(zeros_set, 1)
                dve.wait_ge(c_hi, 1)
                nc.vector.tensor_tensor(rwl[:], rw[:], rwh[:].bitcast(F32), ALU.subtract)
                for n in range(pieces):
                    dve.wait_ge(w_hi, n + 1)
                    part = slice(n * STAGE, (n + 1) * STAGE)
                    last = nc.vector.tensor_tensor(wl[:, part], stage[:, n, :], wh[:, part].bitcast(F32), ALU.subtract)
                last.then_inc(split, 1)
                dve.wait_ge(split, 1)


def three_pass(nc, out, ah, al, bh, bl, start=True, stop=True):
    nc.tensor.matmul(out, ah, bh, start=start, stop=False)
    nc.tensor.matmul(out, ah, bl, start=False, stop=False)
    return nc.tensor.matmul(out, al, bh, start=False, stop=stop)


def norm_stats(nc, dve, s, x, stats, mv, var, fence, b, var_done):
    for t in range(NT):
        last = nc.vector.bn_stats(stats[:, t, :], x[:, bass.ds(b * NT + t, 1), :])
    s.did(last)
    s.settle()
    nc.vector.memset(fence[:], 0.0)
    for t in range(NT):
        last = nc.vector.bn_aggr(mv[:, t, :], stats[:, t, :])
    s.did(last)
    s.settle()
    nc.vector.tensor_scalar(var[:], mv[:, :, 1], LN_EPS, None, ALU.add).then_inc(var_done, 1)

def norm_route_stage(nc, sem_of, shared, ffn, tag):
    x, cst, rwh, rwl, eb, half = (shared[k] for k in ("x", "cst", "rwh", "rwl", "eb", "half"))
    xn_all, lg = ffn["xn_all"], ffn["lg"]
    ident = cst[:, C_ID:C_ID + P]
    with ExitStack() as ctx:
        def sb(name, shape, dt=F32):
            return ctx.enter_context(nc.sbuf_tensor(f"{tag}_{name}", shape, dt))

        def sem(name):
            return sem_of(f"{tag}_{name}")

        xn = sb("xn", [P, 2, NT, D])
        xt_h = sb("xt_h", [P, 2, SEQ], F32R)
        xt_l = sb("xt_l", [P, 2, SEQ], F32R)
        stats = sb("stats", [P, NT, 6])
        mv = sb("mv", [P, NT, 2])
        var = sb("var", [P, NT])
        rstd = sb("rstd", [P, NT])
        fence = sb("fence", [P, 1])
        T = [ctx.enter_context(nc.psum_tensor(f"{tag}_xt{i}", [P, SEQ], F32)) for i in range(2)]
        L = [ctx.enter_context(nc.psum_tensor(f"{tag}_lg{i}", [P, SEQ], F32)) for i in range(2)]
        var_done, rstd_done, xn_done, xnt_done = sem("var_done"), sem("rstd_done"), sem("xn_done"), sem("xnt_done")
        xh_done, xl_done, logits_done, kept = sem("xh_done"), sem("xl_done"), sem("logits_done"), sem("kept")
        chain = sem("chain")
        CHAIN = 3

        def pe_sequence(pe, b, par, prev, nxt):
            pe.wait_ge(xn_done, b + 1)
            for t in range(NT):
                last = nc.tensor.transpose(T[par][:, t * P:(t + 1) * P], xn[:, par, t, :], ident)
            last.then_inc(xnt_done, 1)
            pe.wait_ge(xl_done, b + 1)
            for t in range(NT):
                c = slice(t * P, (t + 1) * P)
                last = three_pass(nc, L[par][:, t * EXPERTS:(t + 1) * EXPERTS],
                                  xt_h[:, par, c], xt_l[:, par, c], rwh[:], rwl[:])
            last.then_inc(logits_done, 1)

        def act_sequence(act, b, par, prev, nxt):
            act.wait_ge(xnt_done, b + 1)
            nc.scalar.copy(xt_h[:, par, :], T[par][:]).then_inc(xh_done, 1)

        def pool_rstd(pool, b):
            pool.wait_ge(var_done, b + 1)
            nc.gpsimd.tensor_tensor(rstd[:], var[:], half[:].broadcast_to([P, NT]), ALU.pow).then_inc(rstd_done, 1)

        def dve_norm(dve, s, b, par):
            dve.wait_ge(rstd_done, b + 1)
            for t in range(NT):
                last = nc.vector.tensor_scalar(xn[:, par, t, :], x[:, bass.ds(b * NT + t, 1), :], mv[:, t, 0:1],
                                               rstd[:, t:t + 1], ALU.subtract, ALU.mult)
            last.then_inc(xn_done, 1)
            dve.wait_ge(xn_done, b + 1)
            s.did(nc.vector.tensor_copy(tiles_of(xn_all, b), xn[:, par, :, :]))

        def dve_sequence(dve, b, par, prev, nxt):
            s = Steps(dve, chain, (b + 1) * CHAIN)
            if nxt:
                norm_stats(nc, dve, s, x, stats, mv, var, fence, b + 1, var_done)
            dve.wait_ge(xh_done, b + 1)
            nc.vector.tensor_tensor(xt_l[:, par, :], T[par][:], xt_h[:, par, :].bitcast(F32), ALU.subtract).then_inc(xl_done, 1)
            if nxt:
                dve_norm(dve, s, b + 1, 1 - par)
            dve.wait_ge(logits_done, b + 1)
            nc.vector.tensor_tensor(tiles_of(lg, b), L[par][:, 0:NT * EXPERTS].rearrange("p (t e) -> p t e", t=NT),
                                    eb[:].unsqueeze(1).broadcast_to([P, NT, EXPERTS]), ALU.add).then_inc(kept, 1)

        with nc.Block() as block:
            @block.tensor
            def _(pe):
                in_pairs(pe, pe_sequence)

            @block.scalar
            def _(act):
                in_pairs(act, act_sequence)

            @block.gpsimd
            def _(pool):
                pool_rstd(pool, 0)
                with pool.Fori(1, BATCH) as b:
                    pool_rstd(pool, b)

            @block.vector
            def _(dve):
                s = Steps(dve, chain, 0)
                norm_stats(nc, dve, s, x, stats, mv, var, fence, 0, var_done)
                dve_norm(dve, s, 0, 0)
                assert s.n == CHAIN, s.n
                in_pairs(dve, dve_sequence)
                dve.wait_ge(kept, BATCH)
                dve.wait_ge(chain, BATCH * CHAIN)


def in_pairs(eng, body):
    body(eng, 0, 0, False, True)
    with eng.Fori(0, (BATCH - 2) // 2) as i:
        body(eng, 2 * i + 1, 1, True, True)
        body(eng, 2 * i + 2, 0, True, True)
    body(eng, BATCH - 1, 1, True, False)


def assign_stage(nc, sem_of, shared, ffn, tag):
    cst, ones16, tri16 = shared["cst"], shared["ones16"], shared["tri16"]
    lg, slots, block_expert, diff = ffn["lg"], ffn["slots"], ffn["block_expert"], ffn["diff"]
    TE = TILES * EXPERTS
    rank = cst[:, C_RANK:C_RANK + EXPERTS]
    restart = cst[:, C_RESTART:C_RESTART + TE]
    numbers = cst[:, C_BLOCK:C_BLOCK + BLOCKS]
    with ExitStack() as ctx:
        def sb(name, shape, dt=F32):
            return ctx.enter_context(nc.sbuf_tensor(f"{tag}_{name}", shape, dt))

        def sem(name):
            return sem_of(f"{tag}_{name}")

        wide = [P, TILES, EXPERTS]
        eq, ranked, first, second, lg2, scratch = (sb(n, wide) for n in ("eq", "ranked", "first", "second", "lg2", "tmp"))
        mask16 = sb("mask16", wide, F16)
        m1, m2, k1, k2 = (sb(n, [P, TILES]) for n in ("m1", "m2", "k1", "k2"))
        tot = sb("tot", [P, EXPERTS, TILES])
        cum = sb("cum", [P, EXPERTS, TILES])
        before = sb("before", [P, EXPERTS, TILES])
        place = sb("place", wide)
        rounded = sb("rounded", [P, HALVES, EXPERTS], I32)
        shifted = sb("shifted", [P, HALVES, EXPERTS], I32)
        nblk, last_blk, base = (sb(n, [P, HALVES, EXPERTS]) for n in ("nblk", "last_blk", "base"))
        unit8 = sb("unit8", [P, EXPERTS])
        ge = sb("ge", [P, HALVES, BLOCKS, EXPERTS])
        which = sb("which", [P, HALVES, BLOCKS])
        picked = sb("picked", [P, TILES])
        PRE = ctx.enter_context(nc.psum_tensor(f"{tag}_pre_ps", [P, TE], F32))
        TOT = ctx.enter_context(nc.psum_tensor(f"{tag}_tot_ps", [P, TE], F32))
        chain, mask_done, sums_done = sem("chain"), sem("mask_done"), sem("sums_done")

        with nc.Block() as block:
            @block.tensor
            def _(pe):
                flat = mask16[:].rearrange("p t e -> p (t e)")
                pe.wait_ge(mask_done, 1)
                nc.tensor.matmul(TOT[:], ones16[:], flat, start=True, stop=True)
                nc.tensor.matmul(PRE[:], tri16[:], flat, start=True, stop=True).then_inc(sums_done, 1)

            @block.vector
            def _(dve):
                s = Steps(dve, chain, 0)

                def step(instruction):
                    s.did(instruction)
                    s.settle()

                def pick(logits, top, key, onehot):
                    step(nc.vector.tensor_reduce(top[:], logits[:], AX.X, ALU.max))
                    step(nc.vector.tensor_tensor(eq[:], logits[:], top[:].unsqueeze(2).broadcast_to(wide), ALU.is_equal))
                    step(nc.vector.tensor_tensor(ranked[:], eq[:], rank.unsqueeze(1).broadcast_to(wide), ALU.mult))
                    step(nc.vector.tensor_reduce(key[:], ranked[:], AX.X, ALU.max))
                    step(nc.vector.tensor_tensor(onehot[:], ranked[:], key[:].unsqueeze(2).broadcast_to(wide), ALU.is_equal))

                step(nc.vector.memset(unit8[:], 1.0))
                pick(lg, m1, k1, first)
                step(nc.vector.scalar_tensor_tensor(lg2[:], first[:], MASKED, lg[:], ALU.mult, ALU.add))
                pick(lg2, m2, k2, second)
                step(nc.vector.tensor_tensor(diff[:], m2[:], m1[:], ALU.subtract))
                nc.vector.tensor_tensor(mask16[:], first[:], second[:], ALU.add).then_inc(mask_done, 1)
                dve.wait_ge(sums_done, 1)
                step(nc.vector.tensor_copy(tot[:], TOT[:].rearrange("p (t e) -> p e t", e=EXPERTS)))
                step(nc.vector.tensor_tensor_scan(cum[:].rearrange("p e t -> p (e t)"), restart,
                                                  tot[:].rearrange("p e t -> p (e t)"), 0.0, ALU.mult, ALU.add))
                step(nc.vector.tensor_tensor(before[:], cum[:], tot[:], ALU.subtract))
                step(nc.vector.tensor_scalar(rounded[:], cum[:].rearrange("p e (h t) -> p h e t", h=HALVES)[:, :, :, HTILES - 1], float(P - 1), None, ALU.add))
                step(nc.vector.tensor_scalar(shifted[:], rounded[:], P.bit_length() - 1, None, ALU.arith_shift_right))
                step(nc.vector.tensor_copy(nblk[:], shifted[:]))
                for h in range(HALVES):
                    step(nc.vector.tensor_tensor_scan(last_blk[:, h, :], unit8[:], nblk[:, h, :], 0.0, ALU.mult, ALU.add))
                step(nc.vector.tensor_tensor(base[:], last_blk[:], nblk[:], ALU.subtract))
                step(nc.vector.tensor_tensor(place[:], PRE[:].rearrange("p (t e) -> p t e", e=EXPERTS),
                                             before[:].rearrange("p e t -> p t e"), ALU.add))
                step(nc.vector.tensor_scalar(nblk[:], base[:], float(P), None, ALU.mult))
                halved = place[:].rearrange("p (h t) e -> p h t e", h=HALVES)
                step(nc.vector.tensor_tensor(halved, halved, nblk[:].unsqueeze(2).broadcast_to([P, HALVES, HTILES, EXPERTS]), ALU.add))
                for k, onehot in enumerate((first, second)):
                    step(nc.vector.tensor_tensor(scratch[:], onehot[:], place[:], ALU.mult))
                    step(nc.vector.tensor_reduce(picked[:], scratch[:], AX.X, ALU.add))
                    step(nc.vector.tensor_copy(slots[:, k, :], picked[:]))
                for h in range(HALVES):
                    step(nc.vector.tensor_tensor(ge[:, h, :, :], numbers.unsqueeze(2).broadcast_to([P, BLOCKS, EXPERTS]),
                                                 last_blk[:, h, :].unsqueeze(1).broadcast_to([P, BLOCKS, EXPERTS]), ALU.is_ge))
                step(nc.vector.tensor_reduce(which[:], ge[:], AX.X, ALU.add))
                step(nc.vector.tensor_scalar(block_expert[:], which[:], float(EXPERTS - 1), None, ALU.min))


RG = NT


def pool_scatter(nc, pool, ffn, dram, h, scattered):
    for t in range(h * HTILES, (h + 1) * HTILES):
        for k in range(2):
            nc.gpsimd.indirect_dma_start(
                out=dram["x_slots"][h], out_offset=bass.IndirectOffsetOnAxis(ffn["slots"][:, k, t:t + 1], 0),
                in_=ffn["xn_all"][:, t, :], in_offset=None).then_inc(scattered, 16)


def pool_gather(nc, pool, ffn, dram, h, got, gathered, combined):
    for n in range(HTILES):
        t = h * HTILES + n
        if n >= RG:
            pool.wait_ge(combined, 2 * (n - RG + 1))
        for k in range(2):
            nc.gpsimd.indirect_dma_start(
                out=got[:, n % RG, k, :], out_offset=None, in_=dram["y_slots"][h],
                in_offset=bass.IndirectOffsetOnAxis(ffn["slots"][:, k, t:t + 1], 0)).then_inc(gathered[n % RG], 16)


def dve_combine(nc, dve, x, wt, h, i, q, got, gathered, combined):
    n = q * RG + i
    t = n + h * HTILES
    dve.wait_ge(gathered[i], 32 * q + 32)
    for k in range(2):
        nc.vector.scalar_tensor_tensor(x[:, bass.ds(t, 1), :], got[:, i, k:k + 1, :], wt[:, k, bass.ds(t, 1)],
                                       x[:, bass.ds(t, 1), :], ALU.mult, ALU.add).then_inc(combined, 1)
        dve.wait_ge(combined, 2 * n + k + 1)


def shared_stage(nc, sem_of, shared, ffn, dram, tag, h, first_ffn, store):
    x, wh, wl, cst, half, euler = (shared[k] for k in ("x", "wh", "wl", "cst", "half", "euler"))
    xn_all, slots, diff, wt = ffn["xn_all"], ffn["slots"], ffn["diff"], ffn["wt"]
    ident = cst[:, C_ID:C_ID + P]
    SC = SHARED * HC
    DEEP, LAG = SC, 3
    B0 = h * GROUP
    with ExitStack() as ctx:
        def sb(name, shape, dt=F32):
            return ctx.enter_context(nc.sbuf_tensor(f"{tag}_{name}", shape, dt))

        def pb(name):
            return ctx.enter_context(nc.psum_tensor(f"{tag}_{name}", [P, SEQ], F32))

        def sem(name):
            return sem_of(f"{tag}_{name}")

        xn = sb("xn", [P, NT, D])
        silu = sb("silu", [P, DEEP, SEQ])
        hid = sb("hid", [P, DEEP, SEQ])
        hid_h = sb("hid_h", [P, DEEP, SEQ], F32R)
        hid_l = sb("hid_l", [P, DEEP, SEQ], F32R)
        xt_h = sb("xt_h", [P, 2, SEQ], F32R)
        xt_l = sb("xt_l", [P, 2, SEQ], F32R)
        yt = sb("yt", [P, SEQ])
        ediff = sb("ediff", [P, TILES])
        den = sb("den", [P, TILES])
        got = sb("got", [P, RG, 2, D])
        G = [pb("gate0"), pb("gate1")]
        U = [pb("up0"), pb("up1")]
        Y = [pb("y0"), pb("y1")]
        M = [pb("misc0"), pb("misc1")]
        gate_done, up_done, down_done = sem("gate_done"), sem("up_done"), sem("down_done")
        silu_done, hid_done, hi_done, lo_done = sem("silu_done"), sem("hid_done"), sem("hi_done"), sem("lo_done")
        xn_done, xnt_done, xh_done, xl_done = sem("xn_done"), sem("xnt_done"), sem("xh_done"), sem("xl_done")
        y_copied, yt_done, x_done = sem("y_copied"), sem("yt_done"), sem("x_done")
        ediff_done, scattered, weights_done = sem("ediff_done"), sem("scattered"), sem("weights_done")
        gathered, combined, stored = [sem(f"gathered{i}") for i in range(RG)], sem("combined"), sem("stored")

        def pe_xnt(pe, b):
            pe.wait_ge(xn_done, b + 1)
            for t in range(NT):
                last = nc.tensor.transpose(M[1][:, t * P:(t + 1) * P], xn[:, t, :], ident)
            last.then_inc(xnt_done, 1)

        def pe_gate_up(pe, b, c, par, fresh):
            f, k = EXPERTS + c // HC, c % HC
            if c == 0:
                pe.wait_ge(xl_done, b + 1)
            if not fresh:
                pe.wait_ge(silu_done, b * SC + c - 1)
            a, o = w1_cols(f, k), w3_cols(f, k)
            three_pass(nc, G[c % 2][:], wh[:, a], wl[:, a], xt_h[:, par, :], xt_l[:, par, :]).then_inc(gate_done, 1)
            if not fresh:
                pe.wait_ge(hid_done, b * SC + c - 1)
            three_pass(nc, U[c % 2][:], wh[:, o], wl[:, o], xt_h[:, par, :], xt_l[:, par, :]).then_inc(up_done, 1)

        def pe_down(pe, b, c, par):
            f, k = EXPERTS + c // HC, c % HC
            pe.wait_ge(lo_done, b * SC + c + 1)
            w = w2_cols(f, k)
            three_pass(nc, Y[par][:], wh[:, w], wl[:, w], hid_h[:, c, :], hid_l[:, c, :],
                       start=(c == 0), stop=(c == SC - 1)).then_inc(down_done, 1)

        def pe_y_transpose(pe, b):
            pe.wait_ge(y_copied, b + 1)
            for t in range(NT):
                last = nc.tensor.transpose(M[0][:, t * P:(t + 1) * P], yt[:, t * P:(t + 1) * P], ident)
            last.then_inc(yt_done, 1)

        def pe_sequence(pe, b, par, prev, prev2, nxt):
            for c in range(SC):
                pe_gate_up(pe, b, c, par, not prev and c < 2)
                if c == 1 and prev2:
                    pe_y_transpose(pe, b - 2)
                if c >= LAG:
                    pe_down(pe, b, c - LAG, par)
                elif prev:
                    pe_down(pe, b - 1, SC + c - LAG, 1 - par)
                if c == 2 and nxt:
                    pe_xnt(pe, b + 1)

        def act_x_hi(act, b, par):
            act.wait_ge(xnt_done, b + 1)
            nc.scalar.copy(xt_h[:, par, :], M[1][:]).then_inc(xh_done, 1)

        def act_hi(act, b, c, fresh):
            act.wait_ge(hid_done, b * SC + c + 1)
            if not fresh:
                act.wait_ge(down_done, (b - 1) * SC + c + 1)
            nc.scalar.copy(hid_h[:, c, :], hid[:, c, :]).then_inc(hi_done, 1)

        def act_y(act, b, par):
            act.wait_ge(down_done, (b + 1) * SC)
            nc.scalar.copy(yt[:], Y[par][:]).then_inc(y_copied, 1)

        def act_sequence(act, b, par, prev, prev2, nxt):
            for c in range(SC):
                act.wait_ge(gate_done, b * SC + c + 1)
                if prev:
                    act.wait_ge(hid_done, (b - 1) * SC + c + 1)
                nc.scalar.activation(silu[:, c, :], G[c % 2][:], ACT.Silu).then_inc(silu_done, 1)
                if c >= 1:
                    act_hi(act, b, c - 1, not prev)
                elif prev:
                    act_hi(act, b - 1, SC - 1, not prev2)
                if c == 3 and prev:
                    act_y(act, b - 1, 1 - par)
                if c == 3 and nxt:
                    act_x_hi(act, b + 1, 1 - par)

        def dve_xn(dve, b):
            if type(b) is not int or b > 0:
                dve.wait_ge(xnt_done, b)
            nc.vector.tensor_copy(xn[:], tiles_of(xn_all, B0 + b)).then_inc(xn_done, 1)

        def dve_x_lo(dve, b, par):
            dve.wait_ge(xh_done, b + 1)
            nc.vector.tensor_tensor(xt_l[:, par, :], M[1][:], xt_h[:, par, :].bitcast(F32), ALU.subtract).then_inc(xl_done, 1)

        def dve_lo(dve, b, c, fresh):
            dve.wait_ge(hi_done, b * SC + c + 1)
            if not fresh:
                dve.wait_ge(down_done, (b - 1) * SC + c + 1)
            nc.vector.tensor_tensor(hid_l[:, c, :], hid[:, c, :], hid_h[:, c, :].bitcast(F32), ALU.subtract).then_inc(lo_done, 1)

        def dve_update(dve, b):
            dve.wait_ge(yt_done, b + 1)
            if h == 1:
                dve.wait_ge(combined, 2 * NT * (b + 1))
            nc.vector.scalar_tensor_tensor(tiles_of(x, B0 + b), M[0][:].rearrange("p (t d) -> p t d", t=NT), 0.5,
                                           tiles_of(x, B0 + b), ALU.mult, ALU.add).then_inc(x_done, 1)

        def dve_sequence(dve, b, par, prev, prev2, nxt):
            for c in range(SC):
                if c >= 1:
                    dve_lo(dve, b, c - 1, not prev)
                elif prev:
                    dve_lo(dve, b - 1, SC - 1, not prev2)
                dve.wait_ge(up_done, b * SC + c + 1)
                dve.wait_ge(silu_done, b * SC + c + 1)
                if prev:
                    dve.wait_ge(lo_done, (b - 1) * SC + c + 1)
                nc.vector.tensor_tensor(hid[:, c, :], silu[:, c, :], U[c % 2][:], ALU.mult).then_inc(hid_done, 1)
                if c == 1 and nxt:
                    dve_xn(dve, b + 1)
                if c == 2 and prev2:
                    dve_update(dve, b - 2)
                if c == 3 and nxt:
                    dve_x_lo(dve, b + 1, 1 - par)
                if h == 1:
                    dve_combine(nc, dve, x, wt, h, c, b, got, gathered, combined)

        def every_sequence(eng, body):
            body(eng, 0, 0, False, False, True)
            body(eng, 1, 1, True, False, True)
            with eng.Fori(0, (GROUP - 4) // 2) as i:
                body(eng, 2 * i + 2, 0, True, True, True)
                body(eng, 2 * i + 3, 1, True, True, True)
            body(eng, GROUP - 2, 0, True, True, True)
            body(eng, GROUP - 1, 1, True, True, False)

        END = GROUP - 1
        with nc.Block() as block:
            @block.tensor
            def _(pe):
                pe_xnt(pe, 0)
                every_sequence(pe, pe_sequence)
                pe.wait_ge(x_done, END - 1)
                pe_y_transpose(pe, END - 1)
                for c in range(SC - LAG, SC):
                    pe_down(pe, END, c, 1)
                pe.wait_ge(x_done, END)
                pe_y_transpose(pe, END)

            @block.scalar
            def _(act):
                act_x_hi(act, 0, 0)
                every_sequence(act, act_sequence)
                act_hi(act, END, SC - 1, False)
                act.wait_ge(yt_done, END)
                act_y(act, END, 1)

            @block.gpsimd
            def _(pool):
                if h == 0:
                    if first_ffn:
                        pool.wait_ge(shared["zeroed"], HALVES * 16 * ZERO_PARTS)
                    pool_scatter(nc, pool, ffn, dram, h, scattered)
                    nc.gpsimd.tensor_tensor(ediff[:], euler[:].broadcast_to([P, TILES]), diff[:], ALU.pow).then_inc(ediff_done, 1)
                    pool.wait_ge(scattered, 2 * HTILES * 16)
                else:
                    pool_gather(nc, pool, ffn, dram, h, got, gathered, combined)

            @block.sync
            def _(sp):
                if store:
                    out = dram["out"].rearrange("(n p) d -> p n d", p=P)
                    sp.dma_start(out[:, 0:HTILES, :], x[:, 0:HTILES, :]).then_inc(stored, 16)
                    for b in range(GROUP):
                        sp.wait_ge(x_done, b + 1)
                        tiles = slice((B0 + b) * NT, (B0 + b + 1) * NT)
                        sp.dma_start(out[:, tiles, :], x[:, tiles, :]).then_inc(stored, 16)
                    sp.wait_ge(stored, 16 * (GROUP + 1))

            @block.vector
            def _(dve):
                dve_xn(dve, 0)
                dve_x_lo(dve, 0, 0)
                every_sequence(dve, dve_sequence)
                dve_update(dve, END - 1)
                dve_lo(dve, END, SC - 1, False)
                dve_update(dve, END)
                if h == 0:
                    dve.wait_ge(ediff_done, 1)
                    nc.vector.tensor_scalar(den[:], ediff[:], 2.0, 2.0, ALU.mult, ALU.add).then_inc(weights_done, 1)
                    dve.wait_ge(weights_done, 1)
                    nc.vector.reciprocal(wt[:, 0, :], den[:]).then_inc(weights_done, 1)
                    dve.wait_ge(weights_done, 2)
                    nc.vector.tensor_tensor(wt[:, 1, :], ediff[:], wt[:, 0, :], ALU.mult).then_inc(weights_done, 1)
                    dve.wait_ge(weights_done, 3)
                dve.wait_ge(x_done, GROUP)


def expert_stage(nc, sem_of, shared, ffn, dram, tag, h):
    x, w, cst, wt = shared["x"], shared["w"], shared["cst"], ffn["wt"]
    block_expert = ffn["block_expert"]
    ident = cst[:, C_ID:C_ID + P]
    w_of = w[:, :, 0:QKV0].rearrange("p s (f w) -> p s f w", f=FFNS)
    x_in = dram["x_slots"][h].rearrange("(n p) d -> p n d", p=P)
    y_out = dram["y_slots"][h].rearrange("(n p) d -> p n d", p=P)
    R = 4
    with ExitStack() as ctx:
        def sb(name, shape, dt=F32):
            return ctx.enter_context(nc.sbuf_tensor(f"{tag}_{name}", shape, dt))

        def sem(name):
            return sem_of(f"{tag}_{name}")

        xg = sb("xg", [P, R, 2, D])
        xt_h = sb("xt_h", [P, R, 2, P], F32R)
        xt_l = sb("xt_l", [P, R, 2, P], F32R)
        silu = sb("silu", [P, R, 2, HID])
        hid = sb("hid", [P, R, 2, HID])
        ht_h = sb("ht_h", [P, R, 2 * HC, P], F32R)
        ht_l = sb("ht_l", [P, R, 2 * HC, P], F32R)
        y_lo = sb("y_lo", [P, 2, D])
        ys = sb("ys", [P, R, 2, D])
        got = sb("got", [P, RG, 2, D])
        GU = [ctx.enter_context(nc.psum_tensor(f"{tag}_gu{i}", [P, 2, 2 * HID], F32)) for i in range(2)]
        XT = ctx.enter_context(nc.psum_tensor(f"{tag}_xt", [P, 2, P], F32))
        HT = [ctx.enter_context(nc.psum_tensor(f"{tag}_ht{i}", [P, 2 * HC, P], F32)) for i in range(2)]
        Y = ctx.enter_context(nc.psum_tensor(f"{tag}_y", [P, 2, 2, D], F32))
        loaded = [sem(f"loaded{r}") for r in range(R)]
        stored = [sem(f"stored{r}") for r in range(R)]
        xt_done, xh_done, xl_done, gu_done = sem("xt_done"), sem("xh_done"), sem("xl_done"), sem("gu_done")
        silu_done, hid_done, ht_done, hh_done, hl_done = (sem("silu_done"), sem("hid_done"), sem("ht_done"),
                                                         sem("hh_done"), sem("hl_done"))
        y_done, y_copied, y_summed = sem("y_done"), sem("y_copied"), sem("y_summed")

        scattered, combined = sem("scattered"), sem("combined")
        gathered = [sem(f"gathered{i}") for i in range(RG)]

        def pe_xt(pe, p, i, q, fresh):
            pe.wait_ge(loaded[i], 16 * (q + 1))
            if not fresh:
                pe.wait_ge(xl_done, p)
            for n in range(2):
                last = nc.tensor.transpose(XT[:, n, :], xg[:, i, n, :], ident)
            last.then_inc(xt_done, 1)

        expert_regs = [[nc.tensor.alloc_register(f"{tag}_expert{i}_{n}") for n in range(2)] for i in range(R)]

        def experts_of(pe, i):
            return [pe.snap(r, min_val=0, max_val=EXPERTS - 1) for r in expert_regs[i]]

        def pe_gate_up(pe, p, i, fresh):
            pe.reg_load(expert_regs[i], block_expert[0:1, h, bass.ds(2 * p, 2)])
            pe.wait_ge(xl_done, p + 1)
            if not fresh:
                pe.wait_ge(hid_done, p - 1)
            for n, e in enumerate(experts_of(pe, i)):
                w_hi, w_lo = (w_of[:, part, bass.ds(e, 1), 0:2 * HID] for part in range(2))
                last = three_pass_moving(nc, GU[i % 2][:, n, :], xt_h[:, i, n, :], xt_l[:, i, n, :], w_hi, w_lo)
            last.then_inc(gu_done, 1)

        def pe_ht(pe, p, i, fresh):
            pe.wait_ge(hid_done, p + 1)
            if not fresh:
                pe.wait_ge(hl_done, p - 1)
            for n in range(2):
                for k in range(HC):
                    last = nc.tensor.transpose(HT[i % 2][:, n * HC + k, :], hid[:, i, n, k * P:(k + 1) * P], ident)
            last.then_inc(ht_done, 1)

        def pe_down(pe, p, i, fresh):
            pe.wait_ge(hl_done, p + 1)
            if not fresh:
                pe.wait_ge(y_summed, p)
            for n, e in enumerate(experts_of(pe, i)):
                for k in range(HC):
                    cols = slice(2 * HID + k * D, 2 * HID + (k + 1) * D)
                    both = lambda: nc.tensor.matmul(Y[:, n, :, :], ht_h[:, i, n * HC + k, :], w_of[:, :, bass.ds(e, 1), cols],
                                                    start=(k == 0), stop=(k == HC - 1))
                    if k == 0:
                        both()
                    last = nc.tensor.matmul(Y[:, n, 0, :], ht_l[:, i, n * HC + k, :], w_of[:, 0, bass.ds(e, 1), cols],
                                            start=False, stop=False)
                    if k > 0:
                        last = both()
            last.then_inc(y_done, 1)

        def pe_pair(pe, p, i, q, first, last):
            pe_gate_up(pe, p, i, first and i < 2)
            if not (last and i >= 2):
                pe_xt(pe, p + 2, (i + 2) % R, q + (i + 2) // R, False)
            if not (first and i < 3):
                pe_down(pe, p - 3, (i - 3) % R, first and i == 3)
            if not (first and i < 1):
                pe_ht(pe, p - 1, (i - 1) % R, first and i < 3)

        def act_x_hi(act, p, i):
            act.wait_ge(xt_done, p + 1)
            nc.scalar.copy(xt_h[:, i, :, :], XT[:]).then_inc(xh_done, 1)

        def act_h_hi(act, p, i):
            act.wait_ge(ht_done, p + 1)
            if not (type(p) is int and p < R):
                act.wait_ge(y_done, p - R + 1)
            nc.scalar.copy(ht_h[:, i, :, :], HT[i % 2][:]).then_inc(hh_done, 1)

        def act_y(act, p, i):
            act.wait_ge(y_done, p + 1)
            nc.scalar.copy(y_lo[:], Y[:, :, 1, :]).then_inc(y_copied, 1)

        def act_pair(act, p, i, q, first, last):
            act.wait_ge(gu_done, p + 1)
            if not first:
                act.wait_ge(hid_done, p - R + 1)
            nc.scalar.activation(silu[:, i, :, :], GU[i % 2][:, :, 0:HID], ACT.Silu).then_inc(silu_done, 1)
            if not (last and i >= 2):
                act_x_hi(act, p + 2, (i + 2) % R)
            if not (first and i < 3):
                act_y(act, p - 3, (i - 3) % R)
            if not (first and i < 1):
                act_h_hi(act, p - 1, (i - 1) % R)

        def dve_x_lo(dve, p, i):
            dve.wait_ge(xh_done, p + 1)
            nc.vector.tensor_tensor(xt_l[:, i, :, :], XT[:], xt_h[:, i, :, :].bitcast(F32), ALU.subtract).then_inc(xl_done, 1)

        def dve_h_lo(dve, p, i):
            dve.wait_ge(hh_done, p + 1)
            nc.vector.tensor_tensor(ht_l[:, i, :, :], HT[i % 2][:], ht_h[:, i, :, :].bitcast(F32), ALU.subtract).then_inc(hl_done, 1)

        def dve_y(dve, p, i, q, fresh):
            dve.wait_ge(y_copied, p + 1)
            if not fresh:
                dve.wait_ge(stored[i], 16 * q)
            nc.vector.tensor_tensor(ys[:, i, :, :], Y[:, :, 0, :], y_lo[:], ALU.add).then_inc(y_summed, 1)

        def dve_pair(dve, p, i, q, first, last):
            dve.wait_ge(silu_done, p + 1)
            if not first:
                dve.wait_ge(ht_done, p - R + 1)
            nc.vector.tensor_tensor(hid[:, i, :, :], silu[:, i, :, :], GU[i % 2][:, :, HID:2 * HID], ALU.mult).then_inc(hid_done, 1)
            if not (last and i >= 2):
                dve_x_lo(dve, p + 2, (i + 2) % R)
            if not (first and i < 3):
                dve_y(dve, p - 3, (i - 3) % R, q - (i < 3), first)
            if not (first and i < 1):
                dve_h_lo(dve, p - 1, (i - 1) % R)
            if h == 1 and not first:
                dve_combine(nc, dve, x, wt, 0, i, q - 1, got, gathered, combined)

        def sp_load(sp, p, i, fresh):
            if not fresh:
                sp.wait_ge(xt_done, p - R + 1)
            sp.dma_start(xg[:, i, :, :], x_in[:, bass.ds(2 * p, 2), :]).then_inc(loaded[i], 16)

        def sp_pair(sp, p, i, q, first, last):
            if not last:
                sp_load(sp, p + R, i, False)
            if not (first and i < 3):
                sp_store(sp, p - 3, (i - 3) % R)

        def sp_store(sp, p, i):
            sp.wait_ge(y_summed, p + 1)
            sp.dma_start(y_out[:, bass.ds(2 * p, 2), :], ys[:, i, :, :]).then_inc(stored[i], 16)

        def every_pair(eng, body):
            for i in range(R):
                body(eng, i, i, 0, True, False)
            with eng.Fori(1, PAIRS // R - 1) as q:
                for i in range(R):
                    body(eng, q * R + i, i, q, False, False)
            for i in range(R):
                body(eng, PAIRS - R + i, i, PAIRS // R - 1, False, True)

        N = PAIRS
        with nc.Block() as block:
            @block.sync
            def _(sp):
                for p in range(R):
                    sp_load(sp, p, p, True)
                every_pair(sp, sp_pair)
                for p in range(N - 3, N):
                    sp_store(sp, p, p % R)
                for r in range(R):
                    sp.wait_ge(stored[r], 16 * (N // R))

            @block.gpsimd
            def _(pool):
                if h == 0:
                    pool_scatter(nc, pool, ffn, dram, 1, scattered)
                    pool.wait_ge(scattered, 2 * HTILES * 16)
                else:
                    pool_gather(nc, pool, ffn, dram, 0, got, gathered, combined)

            @block.tensor
            def _(pe):
                pe_xt(pe, 0, 0, 0, True)
                pe_xt(pe, 1, 1, 0, False)
                every_pair(pe, pe_pair)
                pe_down(pe, N - 3, (N - 3) % R, False)
                pe_ht(pe, N - 1, (N - 1) % R, False)
                pe_down(pe, N - 2, (N - 2) % R, False)
                pe_down(pe, N - 1, (N - 1) % R, False)

            @block.scalar
            def _(act):
                act_x_hi(act, 0, 0)
                act_x_hi(act, 1, 1)
                every_pair(act, act_pair)
                act_y(act, N - 3, (N - 3) % R)
                act_h_hi(act, N - 1, (N - 1) % R)
                act_y(act, N - 2, (N - 2) % R)
                act_y(act, N - 1, (N - 1) % R)

            @block.vector
            def _(dve):
                dve_x_lo(dve, 0, 0)
                dve_x_lo(dve, 1, 1)
                every_pair(dve, dve_pair)
                dve_y(dve, N - 3, (N - 3) % R, N // R - 1, False)
                dve_h_lo(dve, N - 1, (N - 1) % R)
                dve_y(dve, N - 2, (N - 2) % R, N // R - 1, False)
                dve_y(dve, N - 1, (N - 1) % R, N // R - 1, False)


def three_pass_moving(nc, out, ah, al, bh, bl, start=True, stop=True):
    nc.tensor.matmul(out, ah, bh, start=start, stop=False)
    nc.tensor.matmul(out, ah, bl, start=False, stop=False)
    return nc.tensor.matmul(out, al, bh, start=False, stop=stop)


def ffn_stage(nc, sem_of, shared, dram, tag, first_ffn, store):
    with ExitStack() as ctx:
        def sb(name, shape, dt=F32):
            return ctx.enter_context(nc.sbuf_tensor(f"{tag}_{name}", shape, dt))

        ffn = dict(slots=sb("slots", [P, 2, TILES], I32), block_expert=sb("block_expert", [P, HALVES, BLOCKS], I32),
                   diff=sb("diff", [P, TILES]), wt=sb("wt", [P, 2, TILES]), xn_all=sb("xn_all", [P, TILES, D]))
        with ExitStack() as routing:
            ffn["lg"] = routing.enter_context(nc.sbuf_tensor(f"{tag}_lg", [P, TILES, EXPERTS], F32))
            norm_route_stage(nc, sem_of, shared, ffn, f"{tag}_norm")
            assign_stage(nc, sem_of, shared, ffn, f"{tag}_assign")
        shared_stage(nc, sem_of, shared, ffn, dram, f"{tag}_shared0", 0, first_ffn, False)
        expert_stage(nc, sem_of, shared, ffn, dram, f"{tag}_expert0", 0)
        expert_stage(nc, sem_of, shared, ffn, dram, f"{tag}_expert1", 1)
        shared_stage(nc, sem_of, shared, ffn, dram, f"{tag}_shared1", 1, first_ffn, store)


def attention_stage(nc, sem_of, shared):
    x, wh, wl, cst, qb, ob, half = (shared[k] for k in ("x", "wh", "wl", "cst", "qb", "ob", "half"))
    ident = cst[:, C_ID:C_ID + P]
    cos = cst[:, C_COS:C_COS + NT * HD].rearrange("p (t d) -> p t d", t=NT)
    sin = cst[:, C_SIN:C_SIN + NT * HD].rearrange("p (t f two) -> p t f two", t=NT, two=2)
    GROUPS = HEADS // 4
    GU = 8
    HU = GU // 2
    UNITS = GROUPS * GU
    KT = NT
    SCALE = HD ** -0.5
    QK = 2 * HEADS
    with ExitStack() as ctx:
        def sb(name, shape, dt=F32):
            return ctx.enter_context(nc.sbuf_tensor(f"attn_{name}", shape, dt))

        def pb(name, cols=SEQ):
            return ctx.enter_context(nc.psum_tensor(f"attn_{name}", [P, cols], F32))

        def sem(name):
            return sem_of(f"attn_{name}")

        id16 = sb("id16", [P, P], F16)
        xn = sb("xn", [P, NT, D])
        xt_h = sb("xt_h", [P, SEQ], F32R)
        xt_l = sb("xt_l", [P, SEQ], F32R)
        qk = sb("qk", [P, NT, QK * HD])
        ca = sb("ca", [P, NT, QK, HD])
        sa = sb("sa", [P, NT, QK, HD])
        rot = qk[:].rearrange("p t (h d) -> p t h d", h=QK)
        ss = sb("ss", [P, NT * QK])
        lnss = sb("lnss", [P, NT * QK])
        r0 = sb("r0", [P, NT * QK])
        r1 = sb("r1", [P, NT * QK])
        r2 = sb("r2", [P, NT * QK])
        inv = sb("inv", [P, NT, QK])
        unit = ca[:].rearrange("p t h d -> p (t h d)").rearrange("p (a n d) -> p a n d", a=2, d=HD)
        stack = sb("stack", [P, 2, NT, HEADS, SLOT], F16)
        qkt = sb("qkt", [P, 2, 2 * GROUPS, SEQ], F16)
        ve = sb("ve", [P, 2, KT, HEADS, SLOT])
        pr = sb("pr", [P, 2, 4, 2, SEQ])
        avs = sb("avs", [P, GROUPS, SEQ])
        rs = sb("rs", [P, NT, HEADS])
        on = sb("on", [P, NT, HEADS, HD])
        ot_h, ot_l = xt_h, xt_l
        po = xn
        stats = sb("stats", [P, NT, 6])
        mv = sb("mv", [P, NT, 2])
        var = sb("var", [P, NT])
        rstd = sb("rstd", [P, NT])
        fence = sb("fence", [P, 1])

        S = [pb("scores0", 2 * SEQ), pb("scores1", 2 * SEQ)]
        AV = [pb("av0"), pb("av1")]
        M = [pb("misc0"), pb("misc1")]

        ready_chain, ready, scores_done, exp_done = sem("ready_chain"), sem("ready"), sem("scores_done"), sem("exp_done")
        av_done, av_copied = sem("av_done"), sem("av_copied")
        var_done, rstd_done, xn_done, xnt_done = sem("var_done"), sem("rstd_done"), sem("xn_done"), sem("xnt_done")
        xh_done, xl_done, qkv_done, qkv_copied = sem("xh_done"), sem("xl_done"), sem("qkv_done"), sem("qkv_copied")
        ss_done, ln_done, r0_done, stacked = sem("ss_done"), sem("ln_done"), sem("r0_done"), sem("stacked")
        qkt_done, qkt_copied = sem("qkt_done"), sem("qkt_copied")
        o_done, on_done, ont_done, oh_done, ol_done = (sem("o_done"), sem("on_done"), sem("ont_done"),
                                                       sem("oh_done"), sem("ol_done"))
        po_done, x_done = sem("po_done"), sem("x_done")
        chain_p, chain_e = sem("dve_chain_prepare"), sem("dve_chain_epilogue")
        CHAIN_P, CHAIN_E = 12, NT + 1

        def pe_xnt(pe, b):
            pe.wait_ge(xn_done, b + 1)
            for t in range(NT):
                last = nc.tensor.transpose(M[0][:, t * P:(t + 1) * P], xn[:, t, :], ident)
            last.then_inc(xnt_done, 1)

        def pe_qkv(pe, b, t, prev):
            if t == 0:
                pe.wait_ge(xl_done, b + 1)
            if t < 2 and prev:
                pe.wait_ge(on_done, (b - 2) * NT + t + 3)
            if t >= 2:
                pe.wait_ge(qkv_copied, b * NT + t - 1)
            c = slice(t * P, (t + 1) * P)
            w = slice(QKV0, QKV0 + 3 * D)
            three_pass(nc, M[1 - t % 2][:, 0:3 * D], xt_h[:, c], xt_l[:, c], wh[:, w], wl[:, w]).then_inc(qkv_done, 1)

        def pe_qkt(pe, b, t, prev):
            if t == 0:
                pe.wait_ge(stacked, b + 1)
            if t == 1 and prev:
                pe.wait_ge(x_done, b - 1)
            if t >= 2:
                pe.wait_ge(qkt_copied, b * NT + t - 1)
            bank = M[1 - t % 2][:].bitcast(F16)
            for a in range(2):
                for g in range(GROUPS):
                    n = a * GROUPS + g
                    last = nc.tensor.transpose(bank[:, n * P:(n + 1) * P],
                                               stack[:, a, t, 4 * g:4 * g + 4, :].rearrange("p h s -> p (h s)"), id16[:])
            last.then_inc(qkt_done, 1)

        def pe_scores(pe, b, u, par, fresh):
            g, side, j = u // GU, (u % GU) // HU, u % HU
            if u == 0:
                pe.wait_ge(qkt_copied, (b + 1) * NT)
            if not fresh:
                pe.wait_ge(exp_done, b * UNITS + u - 1)
            rows = slice(SLOT * j, SLOT * (j + 1))
            for n in range(2):
                kt = 2 * side + n
                last = nc.tensor.matmul(S[u % 2][:, n * SEQ:(n + 1) * SEQ],
                                        qkt[rows, par, GROUPS + g, kt * P:(kt + 1) * P],
                                        qkt[rows, par, g, :], start=True, stop=True, tile_position=(SLOT * j, 0))
            last.then_inc(scores_done, 1)

        def pe_av(pe, b, h, n, par, fresh):
            g, kt = h // 2, 2 * (h % 2) + n
            if n == 0:
                pe.wait_ge(exp_done, b * UNITS + (h + 1) * HU)
                if kt == 0 and not fresh:
                    pe.wait_ge(av_copied, b * GROUPS + g - 1)
            for j in range(4):
                last = nc.tensor.matmul(AV[g % 2][SLOT * j:SLOT * (j + 1), :], ve[:, par, kt, 4 * g + j, :],
                                        pr[:, h % 2, j, n, :], start=(kt == 0), stop=(kt == KT - 1),
                                        tile_position=(0, SLOT * j))
            if n == 1:
                last.then_inc(av_done, 1)

        def pe_o(pe, b, t, nxt):
            if t == 0:
                pe.wait_ge(av_copied, (b + 1) * GROUPS)
            if t == 1 and nxt:
                pe.wait_ge(xl_done, b + 3)
            if t >= 2:
                pe.wait_ge(on_done, b * NT + t - 1)
            for g in range(GROUPS):
                last = nc.tensor.transpose(M[1 - t % 2][:, g * P:(g + 1) * P], avs[:, g, t * P:(t + 1) * P], ident)
            last.then_inc(o_done, 1)

        def pe_ont(pe, b, nxt):
            pe.wait_ge(on_done, (b + 1) * NT)
            if nxt:
                pe.wait_ge(qkv_copied, (b + 3) * NT - 1)
            for t in range(NT):
                last = nc.tensor.transpose(M[1][:, t * P:(t + 1) * P], on[:, t, :, :].rearrange("p h d -> p (h d)"), ident)
            last.then_inc(ont_done, 1)

        def pe_project(pe, b, nxt):
            pe.wait_ge(ol_done, b + 1)
            if nxt:
                pe.wait_ge(qkv_copied, (b + 3) * NT)
            w = slice(OUT0, OUT0 + D)
            for t in range(NT):
                c = slice(t * P, (t + 1) * P)
                last = three_pass(nc, M[0][:, t * D:(t + 1) * D], ot_h[:, c], ot_l[:, c], wh[:, w], wl[:, w])
            last.then_inc(po_done, 1)

        def pe_sequence(pe, b, par, prev, nxt):
            for u in range(UNITS):
                pe_scores(pe, b, u, par, not prev and u < 2)
                if u % 2 == 1:
                    n = (u % HU) // 2
                    if u >= HU:
                        h = u // HU - 1
                        pe_av(pe, b, h, n, par, not prev and h < 4)
                    elif prev:
                        pe_av(pe, b - 1, 2 * GROUPS - 1, n, 1 - par, False)
                if nxt and u == 4:
                    pe_xnt(pe, b + 1)
                if nxt and 11 <= u < 15:
                    pe_qkv(pe, b + 1, u - 11, prev)
                if prev and 6 <= u < 10:
                    pe_o(pe, b - 1, u - 6, nxt)
                if prev and u == 17:
                    pe_ont(pe, b - 1, nxt)
                if prev and u == 19:
                    pe_project(pe, b - 1, nxt)
                if nxt and 24 <= u < 28:
                    pe_qkt(pe, b + 1, u - 24, prev)

        def act_exp(act, b, u, fresh):
            h, j = u // HU, u % HU
            act.wait_ge(scores_done, b * UNITS + u + 1)
            if j == 0 and not fresh:
                act.wait_ge(av_done, b * 2 * GROUPS + h - 1)
            nc.scalar.activation(pr[:, h % 2, j, :, :].rearrange("p k q -> p (k q)"),
                                 S[u % 2][:], ACT.Exp, scale=SCALE).then_inc(exp_done, 1)

        def act_x_hi(act, b):
            act.wait_ge(xnt_done, b + 1)
            nc.scalar.copy(xt_h[:], M[0][:]).then_inc(xh_done, 1)

        def act_root(act, b):
            act.wait_ge(ss_done, b + 1)
            nc.scalar.activation(lnss[:], ss[:], ACT.Ln, scale=LN_SCALE).then_inc(ln_done, 1)
            act.wait_ge(ln_done, b + 1)
            nc.scalar.activation(r0[:], lnss[:], ACT.Exp, scale=-0.5).then_inc(r0_done, 1)

        def act_o_hi(act, b):
            act.wait_ge(ont_done, b + 1)
            nc.scalar.copy(ot_h[:], M[1][:]).then_inc(oh_done, 1)

        def act_sequence(act, b, par, prev, nxt):
            for u in range(UNITS):
                act_exp(act, b, u, not prev and u < 2 * GU)
                if nxt and u == 5:
                    act_x_hi(act, b + 1)
                if nxt and u == 19:
                    act_root(act, b + 1)
                if prev and u == 18:
                    act_o_hi(act, b - 1)

        def pool_rstd(pool, b):
            pool.wait_ge(var_done, b + 1)
            nc.gpsimd.tensor_tensor(rstd[:], var[:], half[:].broadcast_to([P, NT]), ALU.pow).then_inc(rstd_done, 1)

        def dve_av_copy(dve, b, g, overwrites):
            dve.wait_ge(av_done, 2 * (b * GROUPS + g + 1))
            if overwrites:
                dve.wait_ge(o_done, b * NT)
            nc.vector.tensor_copy(avs[:, g, :], AV[g % 2][:]).then_inc(av_copied, 1)

        def dve_norm(dve, b):
            dve.wait_ge(rstd_done, b + 1)
            for t in range(NT):
                last = nc.vector.tensor_scalar(xn[:, t, :], x[:, bass.ds(b * NT + t, 1), :], mv[:, t, 0:1],
                                               rstd[:, t:t + 1], ALU.subtract, ALU.mult)
            last.then_inc(xn_done, 1)

        def dve_x_lo(dve, b):
            dve.wait_ge(xh_done, b + 1)
            nc.vector.tensor_tensor(xt_l[:], M[0][:], xt_h[:].bitcast(F32), ALU.subtract).then_inc(xl_done, 1)

        def dve_qkv(dve, b, t, par):
            dve.wait_ge(qkv_done, b * NT + t + 1)
            bank = M[1 - t % 2]
            nc.vector.tensor_tensor(qk[:, t, :], bank[:, 0:2 * D], qb[:, 0:2 * D], ALU.add)
            nc.vector.tensor_tensor(ve[:, par, t, :, 0:HD], bank[:, 2 * D:3 * D].rearrange("p (h d) -> p h d", h=HEADS),
                                    qb[:, 2 * D:3 * D].rearrange("p (h d) -> p h d", h=HEADS), ALU.add).then_inc(qkv_copied, 1)

        def dve_rotate(dve, s, b):
            heads = qk[:].rearrange("p t (h d) -> p t h d", h=QK)
            pairs = qk[:].rearrange("p t (h f two) -> p t h f two", h=QK, two=2)
            spair = sa[:].rearrange("p t h (f two) -> p t h f two", two=2)
            half_wide = [P, NT, QK, HD // 2]
            dve.wait_ge(qkv_copied, (b + 1) * NT)
            nc.vector.tensor_tensor(ca[:], heads, cos.unsqueeze(2).broadcast_to([P, NT, QK, HD]), ALU.mult)
            for i in range(2):
                last = nc.vector.tensor_tensor(spair[:, :, :, :, i], pairs[:, :, :, :, 1 - i],
                                               sin[:, :, :, i].unsqueeze(2).broadcast_to(half_wide), ALU.mult)
            s.did(last)
            s.settle()

        def dve_squares(dve, s, b):
            s.did(nc.vector.tensor_tensor(rot, ca[:], sa[:], ALU.add))
            s.settle()
            s.did(nc.vector.tensor_tensor(sa[:], rot, rot, ALU.mult))
            s.settle()
            s.did(nc.vector.tensor_reduce(r1[:].rearrange("p (t h) -> p t h", t=NT), sa[:], AX.X, ALU.add))
            s.settle()
            nc.vector.tensor_scalar(ss[:], r1[:], NORM_EPS2, None, ALU.max).then_inc(ss_done, 1)

        def dve_refine(dve, s, b):
            dve.wait_ge(r0_done, b + 1)
            s.did(nc.vector.tensor_tensor(r1[:], r0[:], r0[:], ALU.mult))
            s.settle()
            s.did(nc.vector.tensor_tensor(r2[:], r1[:], ss[:], ALU.mult))
            s.settle()
            s.did(nc.vector.tensor_scalar(r1[:], r2[:], -0.5 * LN_SCALE, 1.5, ALU.mult, ALU.add))
            s.settle()
            s.did(nc.vector.scalar_tensor_tensor(inv[:].rearrange("p t h -> p (t h)"), r0[:], LN_SCALE ** 0.5, r1[:],
                                                 ALU.mult, ALU.mult))
            s.settle()

        def dve_unit(dve, s, b):
            for a in range(2):
                hs = slice(a * HEADS, (a + 1) * HEADS)
                last = nc.vector.tensor_tensor(unit[:, a, :, :].rearrange("p (t h) d -> p t h d", t=NT), rot[:, :, hs, :],
                                               inv[:, :, hs].unsqueeze(3).broadcast_to([P, NT, HEADS, HD]), ALU.mult)
            s.did(last)
            s.settle()

        def dve_stack(dve, s, b):
            th = NT * HEADS
            q = stack[:, 0, :, :, :].rearrange("p t h s -> p (t h) s")
            k = stack[:, 1, :, :, :].rearrange("p t h s -> p (t h) s")
            q4 = q.rearrange("p n (c d) -> p n c d", d=HD)
            k4 = k.rearrange("p n (c d) -> p n c d", d=HD)
            nc.vector.tensor_copy(q4[:, :, 0:2, :], unit[:, 0, :, :].unsqueeze(2).broadcast_to([P, th, 2, HD]))
            s.did(nc.vector.tensor_copy(k4[:, :, 0:3:2, :], unit[:, 1, :, :].unsqueeze(2).broadcast_to([P, th, 2, HD])))
            s.settle()
            nc.vector.tensor_tensor(q4[:, :, 2, :], unit[:, 0, :, :], q4[:, :, 0, :], ALU.subtract)
            nc.vector.tensor_tensor(k4[:, :, 1, :], unit[:, 1, :, :], k4[:, :, 0, :], ALU.subtract).then_inc(stacked, 1)

        def dve_qkt(dve, b, t, par):
            dve.wait_ge(qkt_done, b * NT + t + 1)
            nc.vector.tensor_copy(qkt[:, par, :, t * P:(t + 1) * P],
                                  M[1 - t % 2][:].bitcast(F16).rearrange("p (n c) -> p n c", c=P)).then_inc(qkt_copied, 1)

        def dve_o(dve, s, b, t):
            dve.wait_ge(o_done, b * NT + t + 1)
            heads = M[1 - t % 2][:].rearrange("p (h s) -> p h s", h=HEADS)
            s.did(nc.vector.reciprocal(rs[:, t, :], heads[:, :, HD]))
            s.settle()
            nc.vector.tensor_tensor(on[:, t, :, :], heads[:, :, 0:HD], rs[:, t, :].unsqueeze(2).broadcast_to([P, HEADS, HD]),
                                    ALU.mult).then_inc(on_done, 1)

        def dve_o_lo(dve, b):
            dve.wait_ge(oh_done, b + 1)
            nc.vector.tensor_tensor(ot_l[:], M[1][:], ot_h[:].bitcast(F32), ALU.subtract).then_inc(ol_done, 1)

        def dve_update(dve, s, b):
            dve.wait_ge(po_done, b + 1)
            s.did(nc.vector.tensor_tensor(po[:], M[0][:].rearrange("p (t d) -> p t d", t=NT),
                                          ob[:].unsqueeze(1).broadcast_to([P, NT, D]), ALU.add))
            s.settle()
            nc.vector.tensor_tensor(tiles_of(x, b), tiles_of(x, b), po[:], ALU.add).then_inc(x_done, 1)

        def dve_sequence(dve, b, par, prev, nxt):
            p = Steps(dve, chain_p, (b + 1) * CHAIN_P)
            e = Steps(dve, chain_e, (b - 1) * CHAIN_E) if prev else None
            for u in range(UNITS):
                if prev and u == HU:
                    dve_av_copy(dve, b - 1, GROUPS - 1, False)
                if u % GU == HU and u > HU:
                    dve_av_copy(dve, b, u // GU - 1, prev and u < 2 * GU)
                if nxt and u == 0:
                    norm_stats(nc, dve, p, x, stats, mv, var, fence, b + 1, var_done)
                if nxt and u == 2:
                    dve_norm(dve, b + 1)
                if nxt and u == 5:
                    dve_x_lo(dve, b + 1)
                if prev and 7 <= u < 11:
                    dve_o(dve, e, b - 1, u - 7)
                if nxt and 12 <= u < 16:
                    dve_qkv(dve, b + 1, u - 12, 1 - par)
                if nxt and u == 16:
                    dve_rotate(dve, p, b + 1)
                if prev and u == 18:
                    dve_o_lo(dve, b - 1)
                if nxt and u == 18:
                    dve_squares(dve, p, b + 1)
                if prev and u == 20:
                    dve_update(dve, e, b - 1)
                if nxt and u == 21:
                    dve_refine(dve, p, b + 1)
                    dve_unit(dve, p, b + 1)
                if nxt and u == 23:
                    dve_stack(dve, p, b + 1)
                if nxt and 25 <= u < 29:
                    dve_qkt(dve, b + 1, u - 25, 1 - par)
            assert not nxt or p.n == CHAIN_P, p.n
            assert not prev or e.n == CHAIN_E, e.n

        def every_sequence(eng, body):
            body(eng, 0, 0, False, True)
            with eng.Fori(0, (BATCH - 2) // 2) as i:
                body(eng, 2 * i + 1, 1, True, True)
                body(eng, 2 * i + 2, 0, True, True)
            body(eng, BATCH - 1, 1, True, False)

        END = BATCH - 1
        with nc.Block() as block:
            @block.tensor
            def _(pe):
                pe_xnt(pe, 0)
                pe.wait_ge(ready, 1)
                for t in range(NT):
                    pe_qkv(pe, 0, t, False)
                for t in range(NT):
                    pe_qkt(pe, 0, t, False)
                every_sequence(pe, pe_sequence)
                for n in range(2):
                    pe_av(pe, END, 2 * GROUPS - 1, n, 1, False)
                for t in range(NT):
                    pe_o(pe, END, t, False)
                pe_ont(pe, END, False)
                pe_project(pe, END, False)

            @block.scalar
            def _(act):
                nc.scalar.preload_act_table_set("natural_log_exp_and_others")
                act_x_hi(act, 0)
                act_root(act, 0)
                every_sequence(act, act_sequence)
                act_o_hi(act, END)

            @block.gpsimd
            def _(pool):
                pool_rstd(pool, 0)
                pool_rstd(pool, 1)
                with pool.Fori(2, BATCH) as b:
                    pool_rstd(pool, b)

            @block.vector
            def _(dve):
                nc.vector.memset(ve[:], 0.0).then_inc(ready_chain, 1)
                nc.vector.memset(stack[:], 0.0)
                nc.vector.tensor_copy(id16[:], ident)
                dve.wait_ge(ready_chain, 1)
                nc.vector.memset(ve[:, :, :, :, HD:HD + 1], 1.0).then_inc(ready, 1)
                dve.wait_ge(ready, 1)
                p = Steps(dve, chain_p, 0)
                norm_stats(nc, dve, p, x, stats, mv, var, fence, 0, var_done)
                dve_norm(dve, 0)
                dve_x_lo(dve, 0)
                for t in range(NT):
                    dve_qkv(dve, 0, t, 0)
                dve_rotate(dve, p, 0)
                dve_squares(dve, p, 0)
                dve_refine(dve, p, 0)
                dve_unit(dve, p, 0)
                dve_stack(dve, p, 0)
                assert p.n == CHAIN_P, p.n
                for t in range(NT):
                    dve_qkt(dve, 0, t, 0)
                every_sequence(dve, dve_sequence)
                e = Steps(dve, chain_e, END * CHAIN_E)
                dve_av_copy(dve, END, GROUPS - 1, False)
                for t in range(NT):
                    dve_o(dve, e, END, t)
                dve_o_lo(dve, END)
                dve_update(dve, e, END)
                dve.wait_ge(x_done, BATCH)



def macaron_block(nc, x, weights, router, expert_bias, qkv_b, out_b, consts, out, stages=("ffn1", "attn", "ffn2")):
    dram = dict(x=x, weights=weights, router=router, expert_bias=expert_bias, qkv_b=qkv_b, out_b=out_b,
                consts=consts, out=out,
                **{f"{kind}_slots": [nc.dram_tensor(f"{kind}_slots{h}", (BLOCKS * P, D), F32).ap() for h in range(HALVES)]
                   for kind in "xy"})
    with ExitStack() as ctx:
        def sb(name, shape, dt=F32):
            return ctx.enter_context(nc.sbuf_tensor(name, shape, dt))

        def sem(name):
            return ctx.enter_context(nc.semaphore(name))

        w = sb("w_split", [P, 2, WCOLS], F32R)
        shared = dict(
            x=sb("x_res", [P, TILES, D]), w=w, wh=w[:, 0, :], wl=w[:, 1, :],
            cst=sb("cst", [P, C_ALL]), ones16=sb("ones16", [P, P], F16), tri16=sb("tri16", [P, P], F16), zeroed=sem("slots_zeroed"),
            rwh=sb("rw_hi", [P, EXPERTS], F32R), rwl=sb("rw_lo", [P, EXPERTS], F32R),
            eb=sb("expert_bias_row", [P, EXPERTS]), qb=sb("qkv_bias_row", [P, 3 * D]), ob=sb("out_bias_row", [P, D]),
            half=sb("minus_half", [P, 1]), euler=sb("euler", [P, 1]))
        load_stage(nc, sem, shared, dram)
        if "ffn1" in stages:
            with stage_semaphores(nc) as stage_sem:
                ffn_stage(nc, stage_sem, shared, dram, "ffn1", True, "ffn2" not in stages and "attn" not in stages)
        if "attn" in stages:
            attention_stage(nc, sem, shared)
        if "ffn2" in stages:
            ffn_stage(nc, sem, shared, dram, "ffn2", False, True)


def constant_table():
    c = np.zeros((P, C_ALL), np.float32)
    c[:, C_ID:C_ID + P] = np.eye(P, dtype=np.float32)
    c[:, C_RANK:C_RANK + EXPERTS] = EXPERTS - np.arange(EXPERTS)
    freqs = np.arange(HD // 2, dtype=np.float32)
    inv = (np.float32(1.0) / np.float32(1250) ** (freqs / np.float32(HD // 2))).astype(np.float32)
    theta = (np.arange(SEQ, dtype=np.float32)[:, None] * inv[None, :]).astype(np.float32)
    cos = np.repeat(np.cos(theta), 2, axis=1).reshape(NT, P, HD).transpose(1, 0, 2)
    sin = np.stack([-np.sin(theta), np.sin(theta)], axis=-1).reshape(NT, P, HD).transpose(1, 0, 2)
    c[:, C_COS:C_COS + NT * HD] = cos.reshape(P, NT * HD)
    c[:, C_SIN:C_SIN + NT * HD] = sin.reshape(P, NT * HD)
    c[:, C_TRI:C_TRI + P] = np.triu(np.ones((P, P), np.float32), 1)
    c[:, C_BLOCK:C_BLOCK + BLOCKS] = np.arange(BLOCKS)
    c[:, C_RESTART:C_RESTART + TILES * EXPERTS] = np.arange(TILES * EXPERTS) % HTILES != 0
    return c


def kernel(**inputs):
    import concourse.bacc as bacc
    from concourse.bass_utils import run_bass_kernel_spmd

    g = {k.removeprefix("L0_"): np.asarray(v) for k, v in inputs.items()}
    cat = np.concatenate
    w1 = cat([g["ffn_w1"], g["ffn_sw1"]]).transpose(2, 0, 1)
    w3 = cat([g["ffn_w3"], g["ffn_sw3"]]).transpose(2, 0, 1)
    w2 = cat([g["ffn_w2"], g["ffn_sw2"]]).transpose(2, 0, 1)
    w2 = w2.reshape(HC, P, FFNS, D).transpose(1, 2, 0, 3).reshape(P, FFNS, HC * D)
    ffn = cat([w1, w3, w2], axis=2).reshape(P, QKV0)
    arrays = {
        "x": g["attn_tokens"].reshape(BATCH * SEQ, D),
        "weights": cat([ffn, g["attn_qkv_w"].T, g["attn_out_w"].T], axis=1),
        "router": g["ffn_router_w"].T,
        "expert_bias": g["ffn_expert_bias"].reshape(1, EXPERTS),
        "qkv_b": g["attn_qkv_b"].reshape(1, 3 * D),
        "out_b": g["attn_out_b"].reshape(1, D),
        "consts": constant_table(),
    }
    arrays = {k: np.ascontiguousarray(v) for k, v in arrays.items()}
    nc = bacc.Bacc("TRN2", target_bir_lowering=False, num_devices=1)
    args = [nc.dram_tensor(f"in_{k}", a.shape, mybir.dt.from_np(a.dtype), kind="ExternalInput").ap()
            for k, a in arrays.items()]
    args.append(nc.dram_tensor("out", (BATCH * SEQ, D), F32, kind="ExternalOutput").ap())
    macaron_block(nc, *args)
    r = run_bass_kernel_spmd(nc, [{f"in_{k}": a for k, a in arrays.items()}], core_ids=[0])
    return r.results[0]["out"].reshape(BATCH, SEQ, D)
```

```python
from contextlib import ExitStack, contextmanager

import numpy as np
import concourse.bass as bass
from concourse import mybir

F32 = mybir.dt.float32
F32R = mybir.dt.float32r
F16 = mybir.dt.float16
I32 = mybir.dt.int32
ALU = mybir.AluOpType
ACT = mybir.ActivationFunctionType
AX = mybir.AxisListType

P = 128
D = 128
BATCH, SEQ = 16, 512
NT = SEQ // P
TILES = BATCH * NT
HEADS, HD = 16, 8
HID = 256
EXPERTS, SHARED = 8, 2
FFNS = EXPERTS + SHARED
HC = HID // P
HALVES = 2
GROUP = BATCH // HALVES
HTILES = TILES // HALVES
BLOCKS = 2 * HTILES + EXPERTS
PAIRS = BLOCKS // 2
FW = 3 * HID
QKV0 = FFNS * FW
OUT0 = QKV0 + 3 * D
WCOLS = OUT0 + D
STAGE = 1024
LN_EPS = 1e-5
NORM_EPS2 = 1e-24
MASKED = -3.0e38
LN_SCALE = 2.0 ** 16
SLOT = 32

C_ID, C_RANK = 0, P
C_COS = C_RANK + EXPERTS
C_SIN = C_COS + NT * HD
C_TRI = C_SIN + NT * HD
C_BLOCK = C_TRI + P
C_RESTART = C_BLOCK + BLOCKS
C_ALL = C_RESTART + TILES * EXPERTS


def w1_cols(f, k):
    return slice(f * FW + k * P, f * FW + (k + 1) * P)


def w3_cols(f, k):
    return slice(f * FW + HID + k * P, f * FW + HID + (k + 1) * P)


def w2_cols(f, k):
    return slice(f * FW + 2 * HID + k * D, f * FW + 2 * HID + (k + 1) * D)


def tiles_of(x, b):
    return x[:, bass.ds(b * NT, NT), :]


class Steps:

    def __init__(self, eng, sem, base):
        self.eng, self.sem, self.base, self.n = eng, sem, base, 0

    def did(self, instruction):
        self.n += 1
        return instruction.then_inc(self.sem, 1)

    def settle(self):
        self.eng.wait_ge(self.sem, self.base + self.n)


@contextmanager
def stage_semaphores(nc):
    used = []

    def sem(name):
        used.append(nc.alloc_semaphore(name=name))
        return used[-1]

    yield sem
    nc.all_engine_barrier()
    nc.clear_and_free_semaphores(used)
    nc.all_engine_barrier()


def load_stage(nc, sem_of, shared, dram, w_stage, tag):
    x, cst, zeros, loads = (shared[k] for k in ("x", "cst", "zeros", "loads"))
    zeros_set, tri_set = sem_of(f"{tag}_zeros_set"), sem_of(f"{tag}_tri_set")
    with nc.Block() as block:
        @block.sync
        def _(sp):
            x_in = dram["x"].rearrange("(n p) d -> p n d", p=P)
            sp.dma_start(x[:, 0:4 * NT, :], x_in[:, 0:4 * NT, :]).then_inc(loads["first"], 16)
            sp.dma_start(cst[:], dram["consts"][:, :]).then_inc(loads["first"], 16)
            sp.dma_start(shared["rw"][:], dram["router"][:, :]).then_inc(loads["first"], 16)
            sp.dma_start(shared["eb"][:], dram["expert_bias"].broadcast_to([P, EXPERTS])).then_inc(loads["first"], 16)
            sp.dma_start(x[:, 4 * NT:, :], x_in[:, 4 * NT:, :]).then_inc(loads["x"], 16)
            sp.dma_start(w_stage[:], dram["weights"][:, :]).then_inc(loads["w"], 16)
            sp.wait_ge(zeros_set, 1)
            for h in range(HALVES):
                slots = dram["x_slots"][h].rearrange("(n p) d -> p n d", p=P)
                sp.dma_start(slots, zeros[:].unsqueeze(1).broadcast_to([P, BLOCKS, D])).then_inc(loads["zeros"][h], 16)
            sp.dma_start(shared["qb"][:], dram["qkv_b"].broadcast_to([P, 3 * D])).then_inc(loads["bias"], 16)
            sp.dma_start(shared["ob"][:], dram["out_b"].broadcast_to([P, D])).then_inc(loads["bias"], 16)

        @block.gpsimd
        def _(pool):
            nc.gpsimd.memset(zeros[:], 0.0).then_inc(zeros_set, 1)
            nc.gpsimd.memset(shared["half"][:], -0.5)
            nc.gpsimd.memset(shared["ones16"][:], 1.0)
            nc.gpsimd.memset(shared["euler"][:], float(np.float32(np.e)))

        @block.scalar
        def _(act):
            act.wait_ge(loads["first"], 64)
            nc.scalar.copy(shared["tri16"][:], cst[:, C_TRI:C_TRI + P]).then_inc(tri_set, 1)
            act.wait_ge(tri_set, 1)


def three_pass(nc, out, ah, al, bh, bl, start=True, stop=True):
    nc.tensor.matmul(out, ah, bh, start=start, stop=False)
    nc.tensor.matmul(out, ah, bl, start=False, stop=False)
    return nc.tensor.matmul(out, al, bh, start=False, stop=stop)


def norm_stats(nc, dve, s, x, stats, mv, var, fence, b, var_done):
    for t in range(NT):
        last = nc.vector.bn_stats(stats[:, t, :], x[:, bass.ds(b * NT + t, 1), :])
    s.did(last)
    s.settle()
    nc.vector.memset(fence[:], 0.0)
    for t in range(NT):
        last = nc.vector.bn_aggr(mv[:, t, :], stats[:, t, :])
    s.did(last)
    s.settle()
    nc.vector.tensor_scalar(var[:], mv[:, :, 1], LN_EPS, None, ALU.add).then_inc(var_done, 1)

def norm_route_stage(nc, sem_of, shared, ffn, tag, first_ffn):
    x, cst, rw, eb, half, loads = (shared[k] for k in ("x", "cst", "rw", "eb", "half", "loads"))
    xn_all, lg = ffn["xn_all"], ffn["lg"]
    ident = cst[:, C_ID:C_ID + P]
    with ExitStack() as ctx:
        def sb(name, shape, dt=F32):
            return ctx.enter_context(nc.sbuf_tensor(f"{tag}_{name}", shape, dt))

        def sem(name):
            return sem_of(f"{tag}_{name}")

        xn = sb("xn", [P, 2, NT, D])
        xt = sb("xt", [P, 2, SEQ])
        stats = sb("stats", [P, NT, 6])
        mv = sb("mv", [P, 2, NT, 2])
        var = sb("var", [P, 2, NT])
        rstd = sb("rstd", [P, 2, NT])
        fence = sb("fence", [P, 1])
        T = [ctx.enter_context(nc.psum_tensor(f"{tag}_xt{i}", [P, SEQ], F32)) for i in range(2)]
        L = [ctx.enter_context(nc.psum_tensor(f"{tag}_lg{i}", [P, SEQ], F32)) for i in range(2)]
        stats_done, mean_done, var_done, rstd_done = sem("stats_done"), sem("mean_done"), sem("var_done"), sem("rstd_done")
        xn_done, xn_kept, xnt_done, xt_copied = sem("xn_done"), sem("xn_kept"), sem("xnt_done"), sem("xt_copied")
        logits_done, logits_kept = sem("logits_done"), sem("logits_kept")

        def pe_transpose(pe, b, par, old):
            pe.wait_ge(xn_done, b + 1)
            if old:
                pe.wait_ge(xt_copied, b - 1)
            for t in range(NT):
                last = nc.tensor.transpose(T[par][:, t * P:(t + 1) * P], xn[:, par, t, :], ident)
            last.then_inc(xnt_done, 1)

        def pe_logits(pe, b, par, old):
            pe.wait_ge(xt_copied, b + 1)
            if old:
                pe.wait_ge(logits_kept, b - 1)
            for t in range(NT):
                last = nc.tensor.matmul(L[par][:, t * EXPERTS:(t + 1) * EXPERTS], xt[:, par, t * P:(t + 1) * P], rw[:],
                                        start=True, stop=True)
            last.then_inc(logits_done, 1)

        def pe_step(pe, b, par):
            fixed = type(b) is int
            pe_transpose(pe, b, par, not (fixed and b < 2))
            if not (fixed and b < 1):
                pe_logits(pe, b - 1, 1 - par, not (fixed and b < 3))

        def act_step(act, b, par):
            old = not (type(b) is int and b < 2)
            act.wait_ge(xn_done, b + 1)
            nc.scalar.copy(tiles_of(xn_all, b), xn[:, par, :, :]).then_inc(xn_kept, 1)
            act.wait_ge(xnt_done, b + 1)
            if old:
                act.wait_ge(logits_done, b - 1)
            nc.scalar.copy(xt[:, par, :], T[par][:]).then_inc(xt_copied, 1)

        def pool_step(pool, b, par):
            pool.wait_ge(var_done, b + 1)
            nc.gpsimd.tensor_tensor(rstd[:, par, :], var[:, par, :], half[:].broadcast_to([P, NT]), ALU.pow).then_inc(rstd_done, 1)

        def dve_stats(dve, b):
            for t in range(NT):
                last = nc.vector.bn_stats(stats[:, t, :], x[:, bass.ds(b * NT + t, 1), :])
            last.then_inc(stats_done, 1)

        def dve_mean(dve, b, par, old):
            if old:
                dve.wait_ge(xn_done, b - 1)
            dve.wait_ge(stats_done, b + 1)
            nc.vector.memset(fence[:], 0.0)
            for t in range(NT):
                last = nc.vector.bn_aggr(mv[:, par, t, :], stats[:, t, :])
            last.then_inc(mean_done, 1)

        def dve_var(dve, b, par):
            dve.wait_ge(mean_done, b + 1)
            nc.vector.tensor_scalar(var[:, par, :], mv[:, par, :, 1], LN_EPS, None, ALU.add).then_inc(var_done, 1)

        def dve_norm(dve, b, par, old):
            dve.wait_ge(rstd_done, b + 1)
            if old:
                dve.wait_ge(xnt_done, b - 1)
                dve.wait_ge(xn_kept, b - 1)
            for t in range(NT):
                last = nc.vector.tensor_scalar(xn[:, par, t, :], x[:, bass.ds(b * NT + t, 1), :], mv[:, par, t, 0:1],
                                               rstd[:, par, t:t + 1], ALU.subtract, ALU.mult)
            last.then_inc(xn_done, 1)

        def dve_logits(dve, b, par):
            dve.wait_ge(logits_done, b + 1)
            nc.vector.tensor_tensor(tiles_of(lg, b), L[par][:, 0:NT * EXPERTS].rearrange("p (t e) -> p t e", t=NT),
                                    eb[:].unsqueeze(1).broadcast_to([P, NT, EXPERTS]), ALU.add).then_inc(logits_kept, 1)

        def dve_step(dve, b, par):
            fixed = type(b) is int
            more = not (fixed and b + 2 >= BATCH)
            if more:
                dve_stats(dve, b + 2)
            if not (fixed and b + 1 >= BATCH):
                dve_norm(dve, b + 1, 1 - par, not (fixed and b < 1))
            if more:
                dve_mean(dve, b + 2, par, True)
            if not (fixed and b < 1):
                dve_logits(dve, b - 1, 1 - par)
            if more:
                dve_var(dve, b + 2, par)

        def every_step(eng, body, loop_needs=None):
            for b in (0, 1):
                body(eng, b, b)
            if loop_needs:
                eng.wait_ge(loop_needs, 16)
            with eng.Fori(1, BATCH // 2 - 1) as i:
                body(eng, 2 * i, 0)
                body(eng, 2 * i + 1, 1)
            for b in (BATCH - 2, BATCH - 1):
                body(eng, b, b % 2)

        with nc.Block() as block:
            @block.tensor
            def _(pe):
                every_step(pe, pe_step)
                pe_logits(pe, BATCH - 1, 1, True)

            @block.scalar
            def _(act):
                every_step(act, act_step)

            @block.gpsimd
            def _(pool):
                every_step(pool, pool_step)

            @block.vector
            def _(dve):
                for b in range(2):
                    dve_stats(dve, b)
                    dve_mean(dve, b, b, False)
                    dve_var(dve, b, b)
                dve_norm(dve, 0, 0, False)
                every_step(dve, dve_step, loads["x"] if first_ffn else None)
                dve_logits(dve, BATCH - 1, 1)
                dve.wait_ge(logits_kept, BATCH)


def assign_stage(nc, sem_of, shared, ffn, w_stage, tag, first_ffn):
    cst, ones16, tri16 = shared["cst"], shared["ones16"], shared["tri16"]
    lg, slots, block_expert, diff = ffn["lg"], ffn["slots"], ffn["block_expert"], ffn["diff"]
    TE = TILES * EXPERTS
    rank = cst[:, C_RANK:C_RANK + EXPERTS]
    restart = cst[:, C_RESTART:C_RESTART + TE]
    numbers = cst[:, C_BLOCK:C_BLOCK + BLOCKS]
    with ExitStack() as ctx:
        def sb(name, shape, dt=F32):
            return ctx.enter_context(nc.sbuf_tensor(f"{tag}_{name}", shape, dt))

        def sem(name):
            return sem_of(f"{tag}_{name}")

        wide = [P, TILES, EXPERTS]
        eq, ranked, first, second, lg2, scratch = (sb(n, wide) for n in ("eq", "ranked", "first", "second", "lg2", "tmp"))
        mask16 = sb("mask16", wide, F16)
        m1, m2, k1, k2 = (sb(n, [P, TILES]) for n in ("m1", "m2", "k1", "k2"))
        tot = sb("tot", [P, EXPERTS, TILES])
        cum = sb("cum", [P, EXPERTS, TILES])
        before = sb("before", [P, EXPERTS, TILES])
        place = sb("place", wide)
        rounded = sb("rounded", [P, HALVES, EXPERTS], I32)
        shifted = sb("shifted", [P, HALVES, EXPERTS], I32)
        nblk, last_blk, base = (sb(n, [P, HALVES, EXPERTS]) for n in ("nblk", "last_blk", "base"))
        unit8 = sb("unit8", [P, EXPERTS])
        ge = sb("ge", [P, HALVES, BLOCKS, EXPERTS])
        which = sb("which", [P, HALVES, BLOCKS])
        picked = sb("picked", [P, TILES])
        PRE = ctx.enter_context(nc.psum_tensor(f"{tag}_pre_ps", [P, TE], F32))
        TOT = ctx.enter_context(nc.psum_tensor(f"{tag}_tot_ps", [P, TE], F32))
        chain, mask_done, sums_done = sem("chain"), sem("mask_done"), sem("sums_done")
        w_hi_done, w_lo_done = sem("w_hi_done"), sem("w_lo_done")
        w = shared["w"]
        parts = [slice(n * STAGE, (n + 1) * STAGE) for n in range(WCOLS // STAGE)]

        with nc.Block() as block:
            @block.scalar
            def _(act):
                if first_ffn:
                    act.wait_ge(shared["loads"]["w"], 16)
                    for part in parts:
                        nc.scalar.copy(w[:, 0, part], w_stage[:, part]).then_inc(w_hi_done, 1)

            @block.gpsimd
            def _(pool):
                if first_ffn:
                    for n, part in enumerate(parts):
                        pool.wait_ge(w_hi_done, n + 1)
                        nc.gpsimd.tensor_tensor(w[:, 1, part], w_stage[:, part], w[:, 0, part].bitcast(F32),
                                                ALU.subtract).then_inc(w_lo_done, 1)
                    pool.wait_ge(w_lo_done, len(parts))

            @block.tensor
            def _(pe):
                flat = mask16[:].rearrange("p t e -> p (t e)")
                pe.wait_ge(mask_done, 1)
                nc.tensor.matmul(TOT[:], ones16[:], flat, start=True, stop=True)
                nc.tensor.matmul(PRE[:], tri16[:], flat, start=True, stop=True).then_inc(sums_done, 1)

            @block.vector
            def _(dve):
                s = Steps(dve, chain, 0)

                def step(instruction):
                    s.did(instruction)
                    s.settle()

                def pick(logits, top, key, onehot):
                    step(nc.vector.tensor_reduce(top[:], logits[:], AX.X, ALU.max))
                    step(nc.vector.tensor_tensor(eq[:], logits[:], top[:].unsqueeze(2).broadcast_to(wide), ALU.is_equal))
                    step(nc.vector.tensor_tensor(ranked[:], eq[:], rank.unsqueeze(1).broadcast_to(wide), ALU.mult))
                    step(nc.vector.tensor_reduce(key[:], ranked[:], AX.X, ALU.max))
                    step(nc.vector.tensor_tensor(onehot[:], ranked[:], key[:].unsqueeze(2).broadcast_to(wide), ALU.is_equal))

                step(nc.vector.memset(unit8[:], 1.0))
                pick(lg, m1, k1, first)
                step(nc.vector.scalar_tensor_tensor(lg2[:], first[:], MASKED, lg[:], ALU.mult, ALU.add))
                pick(lg2, m2, k2, second)
                step(nc.vector.tensor_tensor(diff[:], m2[:], m1[:], ALU.subtract))
                nc.vector.tensor_tensor(mask16[:], first[:], second[:], ALU.add).then_inc(mask_done, 1)
                dve.wait_ge(sums_done, 1)
                step(nc.vector.tensor_copy(tot[:], TOT[:].rearrange("p (t e) -> p e t", e=EXPERTS)))
                step(nc.vector.tensor_tensor_scan(cum[:].rearrange("p e t -> p (e t)"), restart,
                                                  tot[:].rearrange("p e t -> p (e t)"), 0.0, ALU.mult, ALU.add))
                step(nc.vector.tensor_tensor(before[:], cum[:], tot[:], ALU.subtract))
                step(nc.vector.tensor_scalar(rounded[:], cum[:].rearrange("p e (h t) -> p h e t", h=HALVES)[:, :, :, HTILES - 1], float(P - 1), None, ALU.add))
                step(nc.vector.tensor_scalar(shifted[:], rounded[:], P.bit_length() - 1, None, ALU.arith_shift_right))
                step(nc.vector.tensor_copy(nblk[:], shifted[:]))
                for h in range(HALVES):
                    step(nc.vector.tensor_tensor_scan(last_blk[:, h, :], unit8[:], nblk[:, h, :], 0.0, ALU.mult, ALU.add))
                step(nc.vector.tensor_tensor(base[:], last_blk[:], nblk[:], ALU.subtract))
                step(nc.vector.tensor_tensor(place[:], PRE[:].rearrange("p (t e) -> p t e", e=EXPERTS),
                                             before[:].rearrange("p e t -> p t e"), ALU.add))
                step(nc.vector.tensor_scalar(nblk[:], base[:], float(P), None, ALU.mult))
                halved = place[:].rearrange("p (h t) e -> p h t e", h=HALVES)
                step(nc.vector.tensor_tensor(halved, halved, nblk[:].unsqueeze(2).broadcast_to([P, HALVES, HTILES, EXPERTS]), ALU.add))
                for k, onehot in enumerate((first, second)):
                    step(nc.vector.tensor_tensor(scratch[:], onehot[:], place[:], ALU.mult))
                    step(nc.vector.tensor_reduce(picked[:], scratch[:], AX.X, ALU.add))
                    step(nc.vector.tensor_copy(slots[:, k, :], picked[:]))
                for h in range(HALVES):
                    step(nc.vector.tensor_tensor(ge[:, h, :, :], numbers.unsqueeze(2).broadcast_to([P, BLOCKS, EXPERTS]),
                                                 last_blk[:, h, :].unsqueeze(1).broadcast_to([P, BLOCKS, EXPERTS]), ALU.is_ge))
                step(nc.vector.tensor_reduce(which[:], ge[:], AX.X, ALU.add))
                step(nc.vector.tensor_scalar(block_expert[:], which[:], float(EXPERTS - 1), None, ALU.min))


RG = NT


def pool_scatter(nc, pool, ffn, dram, h, scattered):
    for t in range(h * HTILES, (h + 1) * HTILES):
        for k in range(2):
            nc.gpsimd.indirect_dma_start(
                out=dram["x_slots"][h], out_offset=bass.IndirectOffsetOnAxis(ffn["slots"][:, k, t:t + 1], 0),
                in_=ffn["xn_all"][:, t, :], in_offset=None).then_inc(scattered, 16)


def pool_gather(nc, pool, ffn, dram, h, got, gathered, combined):
    for n in range(HTILES):
        t = h * HTILES + n
        if n >= RG:
            pool.wait_ge(combined, 2 * (n - RG + 1))
        for k in range(2):
            nc.gpsimd.indirect_dma_start(
                out=got[:, n % RG, k, :], out_offset=None, in_=dram["y_slots"][h],
                in_offset=bass.IndirectOffsetOnAxis(ffn["slots"][:, k, t:t + 1], 0)).then_inc(gathered[n % RG], 16)


def dve_combine(nc, dve, x, wt, h, i, q, got, gathered, combined):
    n = q * RG + i
    t = n + h * HTILES
    dve.wait_ge(gathered[i], 32 * q + 32)
    for k in range(2):
        nc.vector.scalar_tensor_tensor(x[:, bass.ds(t, 1), :], got[:, i, k:k + 1, :], wt[:, k, bass.ds(t, 1)],
                                       x[:, bass.ds(t, 1), :], ALU.mult, ALU.add).then_inc(combined, 1)
        dve.wait_ge(combined, 2 * n + k + 1)


def shared_stage(nc, sem_of, shared, ffn, dram, tag, h, first_ffn, store):
    x, wh, wl, cst = (shared[k] for k in ("x", "wh", "wl", "cst"))
    xn_all, wt = ffn["xn_all"], ffn["wt"]
    ident = cst[:, C_ID:C_ID + P]
    SC = SHARED * HC
    DEEP, LAG = SC, 3
    B0 = h * GROUP
    with ExitStack() as ctx:
        def sb(name, shape, dt=F32):
            return ctx.enter_context(nc.sbuf_tensor(f"{tag}_{name}", shape, dt))

        def pb(name):
            return ctx.enter_context(nc.psum_tensor(f"{tag}_{name}", [P, SEQ], F32))

        def sem(name):
            return sem_of(f"{tag}_{name}")

        xn = sb("xn", [P, NT, D])
        silu = sb("silu", [P, DEEP, SEQ])
        hid = sb("hid", [P, DEEP, SEQ])
        hid_h = sb("hid_h", [P, DEEP, SEQ], F32R)
        hid_l = sb("hid_l", [P, DEEP, SEQ], F32R)
        xt_h = sb("xt_h", [P, 2, SEQ], F32R)
        xt_l = sb("xt_l", [P, 2, SEQ], F32R)
        yt = sb("yt", [P, SEQ])
        got = sb("got", [P, RG, 2, D])
        G = [pb("gate0"), pb("gate1")]
        U = [pb("up0"), pb("up1")]
        Y = [pb("y0"), pb("y1")]
        M = [pb("misc0"), pb("misc1")]
        gate_done, up_done, down_done = sem("gate_done"), sem("up_done"), sem("down_done")
        silu_done, hid_done, hi_done, lo_done = sem("silu_done"), sem("hid_done"), sem("hi_done"), sem("lo_done")
        xn_done, xnt_done, xh_done, xl_done = sem("xn_done"), sem("xnt_done"), sem("xh_done"), sem("xl_done")
        y_copied, yt_done, x_done = sem("y_copied"), sem("yt_done"), sem("x_done")
        scattered = sem("scattered")
        gathered, combined, stored = [sem(f"gathered{i}") for i in range(RG)], sem("combined"), sem("stored")

        def pe_xnt(pe, b):
            pe.wait_ge(xn_done, b + 1)
            for t in range(NT):
                last = nc.tensor.transpose(M[1][:, t * P:(t + 1) * P], xn[:, t, :], ident)
            last.then_inc(xnt_done, 1)

        def pe_gate_up(pe, b, c, par, fresh):
            f, k = EXPERTS + c // HC, c % HC
            if c == 0:
                pe.wait_ge(xl_done, b + 1)
            if not fresh:
                pe.wait_ge(silu_done, b * SC + c - 1)
            a, o = w1_cols(f, k), w3_cols(f, k)
            three_pass(nc, G[c % 2][:], wh[:, a], wl[:, a], xt_h[:, par, :], xt_l[:, par, :]).then_inc(gate_done, 1)
            if not fresh:
                pe.wait_ge(hid_done, b * SC + c - 1)
            three_pass(nc, U[c % 2][:], wh[:, o], wl[:, o], xt_h[:, par, :], xt_l[:, par, :]).then_inc(up_done, 1)

        def pe_down(pe, b, c, par):
            f, k = EXPERTS + c // HC, c % HC
            pe.wait_ge(lo_done, b * SC + c + 1)
            w = w2_cols(f, k)
            three_pass(nc, Y[par][:], wh[:, w], wl[:, w], hid_h[:, c, :], hid_l[:, c, :],
                       start=(c == 0), stop=(c == SC - 1)).then_inc(down_done, 1)

        def pe_y_transpose(pe, b):
            pe.wait_ge(y_copied, b + 1)
            for t in range(NT):
                last = nc.tensor.transpose(M[0][:, t * P:(t + 1) * P], yt[:, t * P:(t + 1) * P], ident)
            last.then_inc(yt_done, 1)

        def pe_sequence(pe, b, par, prev, prev2, nxt):
            for c in range(SC):
                pe_gate_up(pe, b, c, par, not prev and c < 2)
                if c == 1 and prev2:
                    if type(b) is not int or b > 2:
                        pe.wait_ge(x_done, b - 2)
                    pe_y_transpose(pe, b - 2)
                if c >= LAG:
                    pe_down(pe, b, c - LAG, par)
                elif prev:
                    pe_down(pe, b - 1, SC + c - LAG, 1 - par)
                if c == 1 and nxt:
                    pe_xnt(pe, b + 1)

        def act_xn(act, b):
            if type(b) is not int or b > 0:
                act.wait_ge(xnt_done, b)
            nc.scalar.copy(xn[:], tiles_of(xn_all, B0 + b)).then_inc(xn_done, 1)

        def act_x_hi(act, b, par):
            act.wait_ge(xnt_done, b + 1)
            nc.scalar.copy(xt_h[:, par, :], M[1][:]).then_inc(xh_done, 1)

        def act_hi(act, b, c, fresh):
            act.wait_ge(hid_done, b * SC + c + 1)
            if not fresh:
                act.wait_ge(down_done, (b - 1) * SC + c + 1)
            nc.scalar.copy(hid_h[:, c, :], hid[:, c, :]).then_inc(hi_done, 1)

        def act_y(act, b, par):
            act.wait_ge(down_done, (b + 1) * SC)
            nc.scalar.copy(yt[:], Y[par][:]).then_inc(y_copied, 1)

        def act_sequence(act, b, par, prev, prev2, nxt):
            for c in range(SC):
                act.wait_ge(gate_done, b * SC + c + 1)
                if prev:
                    act.wait_ge(hid_done, (b - 1) * SC + c + 1)
                nc.scalar.activation(silu[:, c, :], G[c % 2][:], ACT.Silu).then_inc(silu_done, 1)
                if c >= 1:
                    act_hi(act, b, c - 1, not prev)
                elif prev:
                    act_hi(act, b - 1, SC - 1, not prev2)
                if c == 0 and nxt:
                    act_xn(act, b + 1)
                if c == 3 and prev:
                    act_y(act, b - 1, 1 - par)
                if c == 2 and nxt:
                    act_x_hi(act, b + 1, 1 - par)

        def dve_x_lo(dve, b, par):
            dve.wait_ge(xh_done, b + 1)
            nc.vector.tensor_tensor(xt_l[:, par, :], M[1][:], xt_h[:, par, :].bitcast(F32), ALU.subtract).then_inc(xl_done, 1)

        def dve_lo(dve, b, c, fresh):
            dve.wait_ge(hi_done, b * SC + c + 1)
            if not fresh:
                dve.wait_ge(down_done, (b - 1) * SC + c + 1)
            nc.vector.tensor_tensor(hid_l[:, c, :], hid[:, c, :], hid_h[:, c, :].bitcast(F32), ALU.subtract).then_inc(lo_done, 1)

        def dve_update(dve, b):
            dve.wait_ge(yt_done, b + 1)
            if h == 1:
                dve.wait_ge(combined, 2 * NT * (b + 1))
            nc.vector.scalar_tensor_tensor(tiles_of(x, B0 + b), M[0][:].rearrange("p (t d) -> p t d", t=NT), 0.5,
                                           tiles_of(x, B0 + b), ALU.mult, ALU.add).then_inc(x_done, 1)

        def dve_sequence(dve, b, par, prev, prev2, nxt):
            for c in range(SC):
                if c >= 1:
                    dve_lo(dve, b, c - 1, not prev)
                elif prev:
                    dve_lo(dve, b - 1, SC - 1, not prev2)
                dve.wait_ge(up_done, b * SC + c + 1)
                dve.wait_ge(silu_done, b * SC + c + 1)
                if prev:
                    dve.wait_ge(lo_done, (b - 1) * SC + c + 1)
                nc.vector.tensor_tensor(hid[:, c, :], silu[:, c, :], U[c % 2][:], ALU.mult).then_inc(hid_done, 1)
                if c == 2 and nxt:
                    dve_x_lo(dve, b + 1, 1 - par)
                if c == 2 and prev2:
                    dve_update(dve, b - 2)
                if h == 1:
                    dve_combine(nc, dve, x, wt, h, c, b, got, gathered, combined)

        def every_sequence(eng, body):
            body(eng, 0, 0, False, False, True)
            body(eng, 1, 1, True, False, True)
            with eng.Fori(0, (GROUP - 4) // 2) as i:
                body(eng, 2 * i + 2, 0, True, True, True)
                body(eng, 2 * i + 3, 1, True, True, True)
            body(eng, GROUP - 2, 0, True, True, True)
            body(eng, GROUP - 1, 1, True, True, False)

        END = GROUP - 1
        with nc.Block() as block:
            @block.tensor
            def _(pe):
                pe_xnt(pe, 0)
                every_sequence(pe, pe_sequence)
                pe.wait_ge(x_done, END - 1)
                pe_y_transpose(pe, END - 1)
                for c in range(SC - LAG, SC):
                    pe_down(pe, END, c, 1)
                pe.wait_ge(x_done, END)
                pe_y_transpose(pe, END)

            @block.scalar
            def _(act):
                act_xn(act, 0)
                act_x_hi(act, 0, 0)
                every_sequence(act, act_sequence)
                act_hi(act, END, SC - 1, False)
                act.wait_ge(yt_done, END)
                act_y(act, END, 1)

            @block.gpsimd
            def _(pool):
                if h == 0:
                    if first_ffn:
                        pool.wait_ge(shared["loads"]["zeros"][h], 16)
                    pool_scatter(nc, pool, ffn, dram, h, scattered)
                    pool.wait_ge(scattered, 2 * HTILES * 16)
                else:
                    pool_gather(nc, pool, ffn, dram, h, got, gathered, combined)

            @block.sync
            def _(sp):
                if store:
                    out = dram["out"].rearrange("(n p) d -> p n d", p=P)
                    sp.dma_start(out[:, 0:HTILES, :], x[:, 0:HTILES, :]).then_inc(stored, 16)
                    for b in range(GROUP):
                        sp.wait_ge(x_done, b + 1)
                        tiles = slice((B0 + b) * NT, (B0 + b + 1) * NT)
                        sp.dma_start(out[:, tiles, :], x[:, tiles, :]).then_inc(stored, 16)
                    sp.wait_ge(stored, 16 * (GROUP + 1))

            @block.vector
            def _(dve):
                dve_x_lo(dve, 0, 0)
                every_sequence(dve, dve_sequence)
                dve_update(dve, END - 1)
                dve_lo(dve, END, SC - 1, False)
                dve_update(dve, END)
                dve.wait_ge(x_done, GROUP)


def expert_stage(nc, sem_of, shared, ffn, dram, tag, first_ffn):
    x, w, cst, wt, euler = shared["x"], shared["w"], shared["cst"], ffn["wt"], shared["euler"]
    block_expert = ffn["block_expert"][:].rearrange("p h n -> p (h n)")
    ident = cst[:, C_ID:C_ID + P]
    w_of = w[:, :, 0:QKV0].rearrange("p s (f w) -> p s f w", f=FFNS)
    x_in = [dram["x_slots"][h].rearrange("(n p) d -> p n d", p=P) for h in range(HALVES)]
    y_out = [dram["y_slots"][h].rearrange("(n p) d -> p n d", p=P) for h in range(HALVES)]
    R = 4
    with ExitStack() as ctx:
        def sb(name, shape, dt=F32):
            return ctx.enter_context(nc.sbuf_tensor(f"{tag}_{name}", shape, dt))

        def sem(name):
            return sem_of(f"{tag}_{name}")

        xg = sb("xg", [P, R, 2, D])
        xt_h = sb("xt_h", [P, R, 2, P], F32R)
        xt_l = sb("xt_l", [P, R, 2, P], F32R)
        silu = sb("silu", [P, R, 2, HID])
        hid = sb("hid", [P, R, 2, HID])
        ht_h = sb("ht_h", [P, R, 2 * HC, P], F32R)
        ht_l = sb("ht_l", [P, R, 2 * HC, P], F32R)
        y_lo = sb("y_lo", [P, 2, D])
        ys = sb("ys", [P, R, 2, D])
        got = sb("got", [P, RG, 2, D])
        GU = [ctx.enter_context(nc.psum_tensor(f"{tag}_gu{i}", [P, 2, 2 * HID], F32)) for i in range(2)]
        XT = ctx.enter_context(nc.psum_tensor(f"{tag}_xt", [P, 2, P], F32))
        HT = [ctx.enter_context(nc.psum_tensor(f"{tag}_ht{i}", [P, 2 * HC, P], F32)) for i in range(2)]
        Y = ctx.enter_context(nc.psum_tensor(f"{tag}_y", [P, 2, 2, D], F32))
        loaded = [sem(f"loaded{r}") for r in range(R)]
        stored = [sem(f"stored{r}") for r in range(R)]
        xt_done, xh_done, xl_done, gu_done = sem("xt_done"), sem("xh_done"), sem("xl_done"), sem("gu_done")
        silu_done, hid_done, ht_done, hh_done, hl_done = (sem("silu_done"), sem("hid_done"), sem("ht_done"),
                                                         sem("hh_done"), sem("hl_done"))
        y_done, y_copied, y_summed = sem("y_done"), sem("y_copied"), sem("y_summed")

        ediff = sb("ediff", [P, TILES])
        den = sb("den", [P, TILES])
        ediff_done, weights_done = sem("ediff_done"), sem("weights_done")
        scattered, combined = sem("scattered"), sem("combined")
        gathered = [sem(f"gathered{i}") for i in range(RG)]

        N = HALVES * PAIRS
        QH = PAIRS // R
        def pe_xt(pe, p, i, q, fresh):
            pe.wait_ge(loaded[i], 16 * (q + 1))
            if not fresh:
                pe.wait_ge(xl_done, p)
            for n in range(2):
                last = nc.tensor.transpose(XT[:, n, :], xg[:, i, n, :], ident)
            last.then_inc(xt_done, 1)

        expert_regs = [[nc.tensor.alloc_register(f"{tag}_expert{i}_{n}") for n in range(2)] for i in range(R)]

        def experts_of(pe, i):
            return [pe.snap(r, min_val=0, max_val=EXPERTS - 1) for r in expert_regs[i]]

        def pe_gate_up(pe, p, i, fresh):
            pe.reg_load(expert_regs[i], block_expert[0:1, bass.ds(2 * p, 2)])
            pe.wait_ge(xl_done, p + 1)
            if not fresh:
                pe.wait_ge(hid_done, p - 1)
            for n, e in enumerate(experts_of(pe, i)):
                w_hi, w_lo = (w_of[:, part, bass.ds(e, 1), 0:2 * HID] for part in range(2))
                last = three_pass_moving(nc, GU[i % 2][:, n, :], xt_h[:, i, n, :], xt_l[:, i, n, :], w_hi, w_lo)
            last.then_inc(gu_done, 1)

        def pe_ht(pe, p, i, fresh):
            pe.wait_ge(hid_done, p + 1)
            if not fresh:
                pe.wait_ge(hl_done, p - 1)
            for n in range(2):
                for k in range(HC):
                    last = nc.tensor.transpose(HT[i % 2][:, n * HC + k, :], hid[:, i, n, k * P:(k + 1) * P], ident)
            last.then_inc(ht_done, 1)

        def pe_down(pe, p, i, fresh):
            pe.wait_ge(hl_done, p + 1)
            if not fresh:
                pe.wait_ge(y_summed, p)
            for n, e in enumerate(experts_of(pe, i)):
                for k in range(HC):
                    cols = slice(2 * HID + k * D, 2 * HID + (k + 1) * D)
                    both = lambda: nc.tensor.matmul(Y[:, n, :, :], ht_h[:, i, n * HC + k, :], w_of[:, :, bass.ds(e, 1), cols],
                                                    start=(k == 0), stop=(k == HC - 1))
                    if k == 0:
                        both()
                    last = nc.tensor.matmul(Y[:, n, 0, :], ht_l[:, i, n * HC + k, :], w_of[:, 0, bass.ds(e, 1), cols],
                                            start=False, stop=False)
                    if k > 0:
                        last = both()
            last.then_inc(y_done, 1)

        def pe_pair(pe, p, i, q, first, last, zone):
            pe_gate_up(pe, p, i, first and i < 2)
            if not (last and i >= 2):
                pe_xt(pe, p + 2, (i + 2) % R, q + (i + 2) // R, False)
            if not (first and i < 3):
                pe_down(pe, p - 3, (i - 3) % R, first and i == 3)
            if not (first and i < 1):
                pe_ht(pe, p - 1, (i - 1) % R, first and i < 3)

        def act_x_hi(act, p, i):
            act.wait_ge(xt_done, p + 1)
            nc.scalar.copy(xt_h[:, i, :, :], XT[:]).then_inc(xh_done, 1)

        def act_h_hi(act, p, i):
            act.wait_ge(ht_done, p + 1)
            if not (type(p) is int and p < R):
                act.wait_ge(y_done, p - R + 1)
            nc.scalar.copy(ht_h[:, i, :, :], HT[i % 2][:]).then_inc(hh_done, 1)

        def act_y(act, p, i):
            act.wait_ge(y_done, p + 1)
            nc.scalar.copy(y_lo[:], Y[:, :, 1, :]).then_inc(y_copied, 1)

        def act_pair(act, p, i, q, first, last, zone):
            act.wait_ge(gu_done, p + 1)
            if not first:
                act.wait_ge(hid_done, p - R + 1)
            nc.scalar.activation(silu[:, i, :, :], GU[i % 2][:, :, 0:HID], ACT.Silu).then_inc(silu_done, 1)
            if not (last and i >= 2):
                act_x_hi(act, p + 2, (i + 2) % R)
            if not (first and i < 3):
                act_y(act, p - 3, (i - 3) % R)
            if not (first and i < 1):
                act_h_hi(act, p - 1, (i - 1) % R)

        def dve_x_lo(dve, p, i):
            dve.wait_ge(xh_done, p + 1)
            nc.vector.tensor_tensor(xt_l[:, i, :, :], XT[:], xt_h[:, i, :, :].bitcast(F32), ALU.subtract).then_inc(xl_done, 1)

        def dve_h_lo(dve, p, i):
            dve.wait_ge(hh_done, p + 1)
            nc.vector.tensor_tensor(ht_l[:, i, :, :], HT[i % 2][:], ht_h[:, i, :, :].bitcast(F32), ALU.subtract).then_inc(hl_done, 1)

        def dve_y(dve, p, i, q, fresh):
            dve.wait_ge(y_copied, p + 1)
            if not fresh:
                dve.wait_ge(stored[i], 16 * q)
            nc.vector.tensor_tensor(ys[:, i, :, :], Y[:, :, 0, :], y_lo[:], ALU.add).then_inc(y_summed, 1)

        def dve_pair(dve, p, i, q, first, last, zone):
            dve.wait_ge(silu_done, p + 1)
            if not first:
                dve.wait_ge(ht_done, p - R + 1)
            nc.vector.tensor_tensor(hid[:, i, :, :], silu[:, i, :, :], GU[i % 2][:, :, HID:2 * HID], ALU.mult).then_inc(hid_done, 1)
            if not (last and i >= 2):
                dve_x_lo(dve, p + 2, (i + 2) % R)
            if not (first and i < 3):
                dve_y(dve, p - 3, (i - 3) % R, q - (i < 3), first)
            if not (first and i < 1):
                dve_h_lo(dve, p - 1, (i - 1) % R)
            if zone == "turn" and i == 0:
                dve_weights(dve)
            if zone in ("second", "last"):
                dve_combine(nc, dve, x, wt, 0, i, q - (QH + 1), got, gathered, combined)

        def dve_weights(dve):
            dve.wait_ge(ediff_done, 1)
            nc.vector.tensor_scalar(den[:], ediff[:], 2.0, 2.0, ALU.mult, ALU.add).then_inc(weights_done, 1)
            dve.wait_ge(weights_done, 1)
            nc.vector.reciprocal(wt[:, 0, :], den[:]).then_inc(weights_done, 1)
            dve.wait_ge(weights_done, 2)
            nc.vector.tensor_tensor(wt[:, 1, :], ediff[:], wt[:, 0, :], ALU.mult).then_inc(weights_done, 1)
            dve.wait_ge(weights_done, 3)

        def sp_load(sp, p, i, h, fresh):
            if not fresh:
                sp.wait_ge(xt_done, p - R + 1)
            sp.dma_start(xg[:, i, :, :], x_in[h][:, bass.ds(2 * (p - h * PAIRS), 2), :]).then_inc(loaded[i], 16)

        def sp_store(sp, p, i, h):
            sp.wait_ge(y_summed, p + 1)
            sp.dma_start(y_out[h][:, bass.ds(2 * (p - h * PAIRS), 2), :], ys[:, i, :, :]).then_inc(stored[i], 16)

        def sp_pair(sp, p, i, q, first, last, zone):
            if zone == "end of first" and i == 0:
                sp.wait_ge(scattered, 2 * HTILES * 16)
            if not last:
                sp_load(sp, p + R, i, int(zone not in ("start", "first")), False)
            if not (first and i < 3):
                sp_store(sp, p - 3, (i - 3) % R, int(zone in ("second", "last") or (zone == "turn" and i >= 3)))

        def every_pair(eng, body):
            def steps(q, zone):
                for i in range(R):
                    body(eng, q * R + i, i, q, zone == "start", zone == "last", zone)

            steps(0, "start")
            with eng.Fori(1, QH - 1) as q:
                steps(q, "first")
            steps(QH - 1, "end of first")
            steps(QH, "turn")
            with eng.Fori(QH + 1, 2 * QH - 1) as q:
                steps(q, "second")
            steps(2 * QH - 1, "last")

        with nc.Block() as block:
            @block.sync
            def _(sp):
                for p in range(R):
                    sp_load(sp, p, p, 0, True)
                every_pair(sp, sp_pair)
                for p in range(N - 3, N):
                    sp_store(sp, p, p % R, 1)
                for r in range(R):
                    sp.wait_ge(stored[r], 16 * (N // R))

            @block.gpsimd
            def _(pool):
                if first_ffn:
                    pool.wait_ge(shared["loads"]["zeros"][1], 16)
                pool_scatter(nc, pool, ffn, dram, 1, scattered)
                nc.gpsimd.tensor_tensor(ediff[:], euler[:].broadcast_to([P, TILES]), ffn["diff"][:], ALU.pow).then_inc(ediff_done, 1)
                for r in range(R):
                    pool.wait_ge(stored[r], 16 * QH)
                pool_gather(nc, pool, ffn, dram, 0, got, gathered, combined)

            @block.tensor
            def _(pe):
                pe_xt(pe, 0, 0, 0, True)
                pe_xt(pe, 1, 1, 0, False)
                every_pair(pe, pe_pair)
                pe_down(pe, N - 3, (N - 3) % R, False)
                pe_ht(pe, N - 1, (N - 1) % R, False)
                pe_down(pe, N - 2, (N - 2) % R, False)
                pe_down(pe, N - 1, (N - 1) % R, False)

            @block.scalar
            def _(act):
                act_x_hi(act, 0, 0)
                act_x_hi(act, 1, 1)
                every_pair(act, act_pair)
                act_y(act, N - 3, (N - 3) % R)
                act_h_hi(act, N - 1, (N - 1) % R)
                act_y(act, N - 2, (N - 2) % R)
                act_y(act, N - 1, (N - 1) % R)

            @block.vector
            def _(dve):
                dve_x_lo(dve, 0, 0)
                dve_x_lo(dve, 1, 1)
                every_pair(dve, dve_pair)
                dve_y(dve, N - 3, (N - 3) % R, N // R - 1, False)
                dve_h_lo(dve, N - 1, (N - 1) % R)
                dve_y(dve, N - 2, (N - 2) % R, N // R - 1, False)
                dve_y(dve, N - 1, (N - 1) % R, N // R - 1, False)


def three_pass_moving(nc, out, ah, al, bh, bl, start=True, stop=True):
    nc.tensor.matmul(out, ah, bh, start=start, stop=False)
    nc.tensor.matmul(out, ah, bl, start=False, stop=False)
    return nc.tensor.matmul(out, al, bh, start=False, stop=stop)


def ffn_stage(nc, sem_of, shared, dram, tag, first_ffn, store):
    with ExitStack() as ctx:
        def sb(name, shape, dt=F32):
            return ctx.enter_context(nc.sbuf_tensor(f"{tag}_{name}", shape, dt))

        ffn = dict(slots=sb("slots", [P, 2, TILES], I32), block_expert=sb("block_expert", [P, HALVES, BLOCKS], I32),
                   diff=sb("diff", [P, TILES]), wt=sb("wt", [P, 2, TILES]), xn_all=sb("xn_all", [P, TILES, D]))
        with ExitStack() as routing:
            ffn["lg"] = routing.enter_context(nc.sbuf_tensor(f"{tag}_lg", [P, TILES, EXPERTS], F32))
            w_stage = None
            if first_ffn:
                w_stage = routing.enter_context(nc.sbuf_tensor("w_stage", [P, WCOLS], F32))
                load_stage(nc, sem_of, shared, dram, w_stage, "load")
            norm_route_stage(nc, sem_of, shared, ffn, f"{tag}_norm", first_ffn)
            assign_stage(nc, sem_of, shared, ffn, w_stage, f"{tag}_assign", first_ffn)
        shared_stage(nc, sem_of, shared, ffn, dram, f"{tag}_shared0", 0, first_ffn, False)
        expert_stage(nc, sem_of, shared, ffn, dram, f"{tag}_expert", first_ffn)
        shared_stage(nc, sem_of, shared, ffn, dram, f"{tag}_shared1", 1, first_ffn, store)


def attention_stage(nc, sem_of, shared):
    x, wh, wl, cst, qb, ob, half = (shared[k] for k in ("x", "wh", "wl", "cst", "qb", "ob", "half"))
    ident = cst[:, C_ID:C_ID + P]
    cos = cst[:, C_COS:C_COS + NT * HD].rearrange("p (t d) -> p t d", t=NT)
    sin = cst[:, C_SIN:C_SIN + NT * HD].rearrange("p (t f two) -> p t f two", t=NT, two=2)
    GROUPS = HEADS // 4
    GU = 8
    HU = GU // 2
    UNITS = GROUPS * GU
    KT = NT
    SCALE = HD ** -0.5
    QK = 2 * HEADS
    with ExitStack() as ctx:
        def sb(name, shape, dt=F32):
            return ctx.enter_context(nc.sbuf_tensor(f"attn_{name}", shape, dt))

        def pb(name, cols=SEQ):
            return ctx.enter_context(nc.psum_tensor(f"attn_{name}", [P, cols], F32))

        def sem(name):
            return sem_of(f"attn_{name}")

        id16 = sb("id16", [P, P], F16)
        xn = sb("xn", [P, NT, D])
        xt_h = sb("xt_h", [P, SEQ], F32R)
        xt_l = sb("xt_l", [P, SEQ], F32R)
        qk = sb("qk", [P, NT, QK * HD])
        ca = sb("ca", [P, NT, QK, HD])
        sa = sb("sa", [P, NT, QK, HD])
        rot = qk[:].rearrange("p t (h d) -> p t h d", h=QK)
        ss = sb("ss", [P, NT * QK])
        lnss = sb("lnss", [P, NT * QK])
        r0 = sb("r0", [P, NT * QK])
        r1 = sb("r1", [P, NT * QK])
        r2 = sb("r2", [P, NT * QK])
        inv = sb("inv", [P, NT, QK])
        unit = ca[:].rearrange("p t h d -> p (t h d)").rearrange("p (a n d) -> p a n d", a=2, d=HD)
        stack = sb("stack", [P, 2, NT, HEADS, SLOT], F16)
        qkt = sb("qkt", [P, 2, 2 * GROUPS, SEQ], F16)
        ve = sb("ve", [P, 2, KT, HEADS, SLOT])
        pr = sb("pr", [P, 2, 4, 2, SEQ])
        avs = sb("avs", [P, GROUPS, SEQ])
        rs = sb("rs", [P, NT, HEADS])
        on = sb("on", [P, NT, HEADS, HD])
        ot_h, ot_l = xt_h, xt_l
        po = xn
        stats = sb("stats", [P, NT, 6])
        mv = sb("mv", [P, NT, 2])
        var = sb("var", [P, NT])
        rstd = sb("rstd", [P, NT])
        fence = sb("fence", [P, 1])

        S = [pb("scores0", 2 * SEQ), pb("scores1", 2 * SEQ)]
        AV = [pb("av0"), pb("av1")]
        M = [pb("misc0"), pb("misc1")]

        ready_chain, ready, scores_done, exp_done = sem("ready_chain"), sem("ready"), sem("scores_done"), sem("exp_done")
        av_done, av_copied = sem("av_done"), sem("av_copied")
        var_done, rstd_done, xn_done, xnt_done = sem("var_done"), sem("rstd_done"), sem("xn_done"), sem("xnt_done")
        xh_done, xl_done, qkv_done, qkv_copied = sem("xh_done"), sem("xl_done"), sem("qkv_done"), sem("qkv_copied")
        ss_done, ln_done, r0_done, stacked = sem("ss_done"), sem("ln_done"), sem("r0_done"), sem("stacked")
        qkt_done, qkt_copied = sem("qkt_done"), sem("qkt_copied")
        o_done, on_done, ont_done, oh_done, ol_done = (sem("o_done"), sem("on_done"), sem("ont_done"),
                                                       sem("oh_done"), sem("ol_done"))
        po_done, x_done, id16_done = sem("po_done"), sem("x_done"), sem("id16_done")
        chain_p, chain_e = sem("dve_chain_prepare"), sem("dve_chain_epilogue")
        CHAIN_P, CHAIN_E = 12, NT + 1

        def pe_xnt(pe, b):
            pe.wait_ge(xn_done, b + 1)
            for t in range(NT):
                last = nc.tensor.transpose(M[0][:, t * P:(t + 1) * P], xn[:, t, :], ident)
            last.then_inc(xnt_done, 1)

        def pe_qkv(pe, b, t, prev):
            if t == 0:
                pe.wait_ge(xl_done, b + 1)
            if t < 2 and prev:
                pe.wait_ge(on_done, (b - 2) * NT + t + 3)
            if t >= 2:
                pe.wait_ge(qkv_copied, b * NT + t - 1)
            c = slice(t * P, (t + 1) * P)
            w = slice(QKV0, QKV0 + 3 * D)
            three_pass(nc, M[1 - t % 2][:, 0:3 * D], xt_h[:, c], xt_l[:, c], wh[:, w], wl[:, w]).then_inc(qkv_done, 1)

        def pe_qkt(pe, b, t, prev):
            if t == 0:
                pe.wait_ge(stacked, b + 1)
            if t == 1 and prev:
                pe.wait_ge(x_done, b - 1)
            if t >= 2:
                pe.wait_ge(qkt_copied, b * NT + t - 1)
            bank = M[1 - t % 2][:].bitcast(F16)
            for a in range(2):
                for g in range(GROUPS):
                    n = a * GROUPS + g
                    last = nc.tensor.transpose(bank[:, n * P:(n + 1) * P],
                                               stack[:, a, t, 4 * g:4 * g + 4, :].rearrange("p h s -> p (h s)"), id16[:])
            last.then_inc(qkt_done, 1)

        def pe_scores(pe, b, u, par, fresh):
            g, side, j = u // GU, (u % GU) // HU, u % HU
            if u == 0:
                pe.wait_ge(qkt_copied, (b + 1) * NT)
            if not fresh:
                pe.wait_ge(exp_done, b * UNITS + u - 1)
            rows = slice(SLOT * j, SLOT * (j + 1))
            for n in range(2):
                kt = 2 * side + n
                last = nc.tensor.matmul(S[u % 2][:, n * SEQ:(n + 1) * SEQ],
                                        qkt[rows, par, GROUPS + g, kt * P:(kt + 1) * P],
                                        qkt[rows, par, g, :], start=True, stop=True, tile_position=(SLOT * j, 0))
            last.then_inc(scores_done, 1)

        def pe_av(pe, b, h, n, par, fresh):
            g, kt = h // 2, 2 * (h % 2) + n
            if n == 0:
                pe.wait_ge(exp_done, b * UNITS + (h + 1) * HU)
                if kt == 0 and not fresh:
                    pe.wait_ge(av_copied, b * GROUPS + g - 1)
            for j in range(4):
                last = nc.tensor.matmul(AV[g % 2][SLOT * j:SLOT * (j + 1), :], ve[:, par, kt, 4 * g + j, :],
                                        pr[:, h % 2, j, n, :], start=(kt == 0), stop=(kt == KT - 1),
                                        tile_position=(0, SLOT * j))
            if n == 1:
                last.then_inc(av_done, 1)

        def pe_o(pe, b, t, nxt):
            if t == 0:
                pe.wait_ge(av_copied, (b + 1) * GROUPS)
            if t == 1 and nxt:
                pe.wait_ge(xl_done, b + 3)
            if t >= 2:
                pe.wait_ge(on_done, b * NT + t - 1)
            for g in range(GROUPS):
                last = nc.tensor.transpose(M[1 - t % 2][:, g * P:(g + 1) * P], avs[:, g, t * P:(t + 1) * P], ident)
            last.then_inc(o_done, 1)

        def pe_ont(pe, b, nxt):
            pe.wait_ge(on_done, (b + 1) * NT)
            if nxt:
                pe.wait_ge(qkv_copied, (b + 3) * NT - 1)
            for t in range(NT):
                last = nc.tensor.transpose(M[1][:, t * P:(t + 1) * P], on[:, t, :, :].rearrange("p h d -> p (h d)"), ident)
            last.then_inc(ont_done, 1)

        def pe_project(pe, b, nxt):
            pe.wait_ge(ol_done, b + 1)
            if nxt:
                pe.wait_ge(qkv_copied, (b + 3) * NT)
            w = slice(OUT0, OUT0 + D)
            for t in range(NT):
                c = slice(t * P, (t + 1) * P)
                last = three_pass(nc, M[0][:, t * D:(t + 1) * D], ot_h[:, c], ot_l[:, c], wh[:, w], wl[:, w])
            last.then_inc(po_done, 1)

        def pe_sequence(pe, b, par, prev, nxt):
            for u in range(UNITS):
                pe_scores(pe, b, u, par, not prev and u < 2)
                if u % 2 == 1:
                    n = (u % HU) // 2
                    if u >= HU:
                        h = u // HU - 1
                        pe_av(pe, b, h, n, par, not prev and h < 4)
                    elif prev:
                        pe_av(pe, b - 1, 2 * GROUPS - 1, n, 1 - par, False)
                if nxt and u == 4:
                    pe_xnt(pe, b + 1)
                if nxt and 11 <= u < 15:
                    pe_qkv(pe, b + 1, u - 11, prev)
                if prev and 6 <= u < 10:
                    pe_o(pe, b - 1, u - 6, nxt)
                if prev and u == 17:
                    pe_ont(pe, b - 1, nxt)
                if prev and u == 23:
                    pe_project(pe, b - 1, nxt)
                if nxt and 27 <= u < 31:
                    pe_qkt(pe, b + 1, u - 27, prev)

        def act_exp(act, b, u, fresh):
            h, j = u // HU, u % HU
            act.wait_ge(scores_done, b * UNITS + u + 1)
            if j == 0 and not fresh:
                act.wait_ge(av_done, b * 2 * GROUPS + h - 1)
            nc.scalar.activation(pr[:, h % 2, j, :, :].rearrange("p k q -> p (k q)"),
                                 S[u % 2][:], ACT.Exp, scale=SCALE).then_inc(exp_done, 1)

        def act_x_hi(act, b):
            act.wait_ge(xnt_done, b + 1)
            nc.scalar.copy(xt_h[:], M[0][:]).then_inc(xh_done, 1)

        def act_root(act, b):
            act.wait_ge(ss_done, b + 1)
            nc.scalar.activation(lnss[:], ss[:], ACT.Ln, scale=LN_SCALE).then_inc(ln_done, 1)
            act.wait_ge(ln_done, b + 1)
            nc.scalar.activation(r0[:], lnss[:], ACT.Exp, scale=-0.5).then_inc(r0_done, 1)

        def act_o_hi(act, b):
            act.wait_ge(ont_done, b + 1)
            nc.scalar.copy(ot_h[:], M[1][:]).then_inc(oh_done, 1)

        def act_sequence(act, b, par, prev, nxt):
            for u in range(UNITS):
                act_exp(act, b, u, not prev and u < 2 * GU)
                if nxt and u == 5:
                    act_x_hi(act, b + 1)
                if nxt and u == 22:
                    act_root(act, b + 1)
                if prev and u == 18:
                    act_o_hi(act, b - 1)

        def pool_rstd(pool, b):
            pool.wait_ge(var_done, b + 1)
            nc.gpsimd.tensor_tensor(rstd[:], var[:], half[:].broadcast_to([P, NT]), ALU.pow).then_inc(rstd_done, 1)

        def dve_av_copy(dve, b, g, overwrites):
            dve.wait_ge(av_done, 2 * (b * GROUPS + g + 1))
            if overwrites:
                dve.wait_ge(o_done, b * NT)
            nc.vector.tensor_copy(avs[:, g, :], AV[g % 2][:]).then_inc(av_copied, 1)

        def dve_norm(dve, b):
            dve.wait_ge(rstd_done, b + 1)
            for t in range(NT):
                last = nc.vector.tensor_scalar(xn[:, t, :], x[:, bass.ds(b * NT + t, 1), :], mv[:, t, 0:1],
                                               rstd[:, t:t + 1], ALU.subtract, ALU.mult)
            last.then_inc(xn_done, 1)

        def dve_x_lo(dve, b):
            dve.wait_ge(xh_done, b + 1)
            nc.vector.tensor_tensor(xt_l[:], M[0][:], xt_h[:].bitcast(F32), ALU.subtract).then_inc(xl_done, 1)

        def dve_qkv(dve, b, t, par):
            dve.wait_ge(qkv_done, b * NT + t + 1)
            bank = M[1 - t % 2]
            nc.vector.tensor_tensor(qk[:, t, :], bank[:, 0:2 * D], qb[:, 0:2 * D], ALU.add)
            nc.vector.tensor_tensor(ve[:, par, t, :, 0:HD], bank[:, 2 * D:3 * D].rearrange("p (h d) -> p h d", h=HEADS),
                                    qb[:, 2 * D:3 * D].rearrange("p (h d) -> p h d", h=HEADS), ALU.add).then_inc(qkv_copied, 1)

        def dve_rotate(dve, s, b):
            heads = qk[:].rearrange("p t (h d) -> p t h d", h=QK)
            pairs = qk[:].rearrange("p t (h f two) -> p t h f two", h=QK, two=2)
            spair = sa[:].rearrange("p t h (f two) -> p t h f two", two=2)
            half_wide = [P, NT, QK, HD // 2]
            dve.wait_ge(qkv_copied, (b + 1) * NT)
            nc.vector.tensor_tensor(ca[:], heads, cos.unsqueeze(2).broadcast_to([P, NT, QK, HD]), ALU.mult)
            for i in range(2):
                last = nc.vector.tensor_tensor(spair[:, :, :, :, i], pairs[:, :, :, :, 1 - i],
                                               sin[:, :, :, i].unsqueeze(2).broadcast_to(half_wide), ALU.mult)
            s.did(last)
            s.settle()

        def dve_squares(dve, s, b):
            s.did(nc.vector.tensor_tensor(rot, ca[:], sa[:], ALU.add))
            s.settle()
            s.did(nc.vector.tensor_tensor(sa[:], rot, rot, ALU.mult))
            s.settle()
            s.did(nc.vector.tensor_reduce(r1[:].rearrange("p (t h) -> p t h", t=NT), sa[:], AX.X, ALU.add))
            s.settle()
            nc.vector.tensor_scalar(ss[:], r1[:], NORM_EPS2, None, ALU.max).then_inc(ss_done, 1)

        def dve_refine(dve, s, b):
            dve.wait_ge(r0_done, b + 1)
            s.did(nc.vector.tensor_tensor(r1[:], r0[:], r0[:], ALU.mult))
            s.settle()
            s.did(nc.vector.tensor_tensor(r2[:], r1[:], ss[:], ALU.mult))
            s.settle()
            s.did(nc.vector.tensor_scalar(r1[:], r2[:], -0.5 * LN_SCALE, 1.5, ALU.mult, ALU.add))
            s.settle()
            s.did(nc.vector.scalar_tensor_tensor(inv[:].rearrange("p t h -> p (t h)"), r0[:], LN_SCALE ** 0.5, r1[:],
                                                 ALU.mult, ALU.mult))
            s.settle()

        def dve_unit(dve, s, b):
            for a in range(2):
                hs = slice(a * HEADS, (a + 1) * HEADS)
                last = nc.vector.tensor_tensor(unit[:, a, :, :].rearrange("p (t h) d -> p t h d", t=NT), rot[:, :, hs, :],
                                               inv[:, :, hs].unsqueeze(3).broadcast_to([P, NT, HEADS, HD]), ALU.mult)
            s.did(last)
            s.settle()

        def dve_stack(dve, s, b):
            th = NT * HEADS
            q = stack[:, 0, :, :, :].rearrange("p t h s -> p (t h) s")
            k = stack[:, 1, :, :, :].rearrange("p t h s -> p (t h) s")
            q4 = q.rearrange("p n (c d) -> p n c d", d=HD)
            k4 = k.rearrange("p n (c d) -> p n c d", d=HD)
            nc.vector.tensor_copy(q4[:, :, 0:2, :], unit[:, 0, :, :].unsqueeze(2).broadcast_to([P, th, 2, HD]))
            s.did(nc.vector.tensor_copy(k4[:, :, 0:3:2, :], unit[:, 1, :, :].unsqueeze(2).broadcast_to([P, th, 2, HD])))
            s.settle()
            nc.vector.tensor_tensor(q4[:, :, 2, :], unit[:, 0, :, :], q4[:, :, 0, :], ALU.subtract)
            nc.vector.tensor_tensor(k4[:, :, 1, :], unit[:, 1, :, :], k4[:, :, 0, :], ALU.subtract).then_inc(stacked, 1)

        def dve_qkt(dve, b, t, par):
            dve.wait_ge(qkt_done, b * NT + t + 1)
            nc.vector.tensor_copy(qkt[:, par, :, t * P:(t + 1) * P],
                                  M[1 - t % 2][:].bitcast(F16).rearrange("p (n c) -> p n c", c=P)).then_inc(qkt_copied, 1)

        def dve_o(dve, s, b, t):
            dve.wait_ge(o_done, b * NT + t + 1)
            heads = M[1 - t % 2][:].rearrange("p (h s) -> p h s", h=HEADS)
            s.did(nc.vector.reciprocal(rs[:, t, :], heads[:, :, HD]))
            s.settle()
            nc.vector.tensor_tensor(on[:, t, :, :], heads[:, :, 0:HD], rs[:, t, :].unsqueeze(2).broadcast_to([P, HEADS, HD]),
                                    ALU.mult).then_inc(on_done, 1)

        def dve_o_lo(dve, b):
            dve.wait_ge(oh_done, b + 1)
            nc.vector.tensor_tensor(ot_l[:], M[1][:], ot_h[:].bitcast(F32), ALU.subtract).then_inc(ol_done, 1)

        def dve_update(dve, s, b):
            dve.wait_ge(po_done, b + 1)
            s.did(nc.vector.tensor_tensor(po[:], M[0][:].rearrange("p (t d) -> p t d", t=NT),
                                          ob[:].unsqueeze(1).broadcast_to([P, NT, D]), ALU.add))
            s.settle()
            nc.vector.tensor_tensor(tiles_of(x, b), tiles_of(x, b), po[:], ALU.add).then_inc(x_done, 1)

        def dve_sequence(dve, b, par, prev, nxt):
            p = Steps(dve, chain_p, (b + 1) * CHAIN_P)
            e = Steps(dve, chain_e, (b - 1) * CHAIN_E) if prev else None
            for u in range(UNITS):
                if prev and u == HU:
                    dve_av_copy(dve, b - 1, GROUPS - 1, False)
                if u % GU == HU and u > HU:
                    dve_av_copy(dve, b, u // GU - 1, prev and u < 2 * GU)
                if nxt and u == 0:
                    norm_stats(nc, dve, p, x, stats, mv, var, fence, b + 1, var_done)
                if nxt and u == 2:
                    dve_norm(dve, b + 1)
                if nxt and u == 5:
                    dve_x_lo(dve, b + 1)
                if prev and 7 <= u < 11:
                    dve_o(dve, e, b - 1, u - 7)
                if nxt and 12 <= u < 16:
                    dve_qkv(dve, b + 1, u - 12, 1 - par)
                if nxt and u == 16:
                    dve_rotate(dve, p, b + 1)
                if nxt and u == 17:
                    dve_squares(dve, p, b + 1)
                if prev and u == 19:
                    dve_o_lo(dve, b - 1)
                if nxt and u == 22:
                    dve_refine(dve, p, b + 1)
                    dve_unit(dve, p, b + 1)
                if nxt and u == 24:
                    dve_stack(dve, p, b + 1)
                if prev and u == 25:
                    dve_update(dve, e, b - 1)
                if nxt and 28 <= u < 32:
                    dve_qkt(dve, b + 1, u - 28, 1 - par)
            assert not nxt or p.n == CHAIN_P, p.n
            assert not prev or e.n == CHAIN_E, e.n

        def every_sequence(eng, body):
            body(eng, 0, 0, False, True)
            with eng.Fori(0, (BATCH - 2) // 2) as i:
                body(eng, 2 * i + 1, 1, True, True)
                body(eng, 2 * i + 2, 0, True, True)
            body(eng, BATCH - 1, 1, True, False)

        END = BATCH - 1
        with nc.Block() as block:
            @block.tensor
            def _(pe):
                pe_xnt(pe, 0)
                for t in range(NT):
                    pe_qkv(pe, 0, t, False)
                pe.wait_ge(id16_done, 1)
                for t in range(NT):
                    pe_qkt(pe, 0, t, False)
                every_sequence(pe, pe_sequence)
                for n in range(2):
                    pe_av(pe, END, 2 * GROUPS - 1, n, 1, False)
                for t in range(NT):
                    pe_o(pe, END, t, False)
                pe_ont(pe, END, False)
                pe_project(pe, END, False)

            @block.scalar
            def _(act):
                nc.scalar.preload_act_table_set("natural_log_exp_and_others")
                nc.scalar.copy(id16[:], ident).then_inc(id16_done, 1)
                act_x_hi(act, 0)
                act_root(act, 0)
                every_sequence(act, act_sequence)
                act_o_hi(act, END)

            @block.gpsimd
            def _(pool):
                pool_rstd(pool, 0)
                nc.gpsimd.memset(ve[:], 0.0).then_inc(ready_chain, 1)
                pool.wait_ge(ready_chain, 1)
                nc.gpsimd.memset(ve[:, :, :, :, HD:HD + 1], 1.0)
                nc.gpsimd.memset(stack[:], 0.0).then_inc(ready, 1)
                pool_rstd(pool, 1)
                with pool.Fori(2, BATCH) as b:
                    pool_rstd(pool, b)

            @block.vector
            def _(dve):
                p = Steps(dve, chain_p, 0)
                norm_stats(nc, dve, p, x, stats, mv, var, fence, 0, var_done)
                dve_norm(dve, 0)
                dve_x_lo(dve, 0)
                dve.wait_ge(shared["loads"]["bias"], 32)
                dve.wait_ge(ready, 1)
                for t in range(NT):
                    dve_qkv(dve, 0, t, 0)
                dve_rotate(dve, p, 0)
                dve_squares(dve, p, 0)
                dve_refine(dve, p, 0)
                dve_unit(dve, p, 0)
                dve_stack(dve, p, 0)
                assert p.n == CHAIN_P, p.n
                for t in range(NT):
                    dve_qkt(dve, 0, t, 0)
                every_sequence(dve, dve_sequence)
                e = Steps(dve, chain_e, END * CHAIN_E)
                dve_av_copy(dve, END, GROUPS - 1, False)
                for t in range(NT):
                    dve_o(dve, e, END, t)
                dve_o_lo(dve, END)
                dve_update(dve, e, END)
                dve.wait_ge(x_done, BATCH)



def macaron_block(nc, x, weights, router, expert_bias, qkv_b, out_b, consts, out, stages=("ffn1", "attn", "ffn2")):
    dram = dict(x=x, weights=weights, router=router, expert_bias=expert_bias, qkv_b=qkv_b, out_b=out_b,
                consts=consts, out=out,
                **{f"{kind}_slots": [nc.dram_tensor(f"{kind}_slots{h}", (BLOCKS * P, D), F32).ap() for h in range(HALVES)]
                   for kind in "xy"})
    with ExitStack() as ctx:
        def sb(name, shape, dt=F32):
            return ctx.enter_context(nc.sbuf_tensor(name, shape, dt))

        def sem(name):
            return ctx.enter_context(nc.semaphore(name))

        w = sb("w_split", [P, 2, WCOLS], F32R)
        shared = dict(
            x=sb("x_res", [P, TILES, D]), w=w, wh=w[:, 0, :], wl=w[:, 1, :],
            cst=sb("cst", [P, C_ALL]), ones16=sb("ones16", [P, P], F16), tri16=sb("tri16", [P, P], F16),
            loads=dict(first=sem("loaded_first"), x=sem("loaded_x"), w=sem("loaded_w"), bias=sem("loaded_bias"),
                       zeros=[sem(f"slots{h}_zeroed") for h in range(HALVES)]),
            rw=sb("router", [P, EXPERTS]), zeros=sb("zeros", [P, D]),
            eb=sb("expert_bias_row", [P, EXPERTS]), qb=sb("qkv_bias_row", [P, 3 * D]), ob=sb("out_bias_row", [P, D]),
            half=sb("minus_half", [P, 1]), euler=sb("euler", [P, 1]))
        if "ffn1" in stages:
            with stage_semaphores(nc) as stage_sem:
                ffn_stage(nc, stage_sem, shared, dram, "ffn1", True, "ffn2" not in stages and "attn" not in stages)
        if "attn" in stages:
            attention_stage(nc, sem, shared)
        if "ffn2" in stages:
            ffn_stage(nc, sem, shared, dram, "ffn2", False, True)


def constant_table():
    c = np.zeros((P, C_ALL), np.float32)
    c[:, C_ID:C_ID + P] = np.eye(P, dtype=np.float32)
    c[:, C_RANK:C_RANK + EXPERTS] = EXPERTS - np.arange(EXPERTS)
    freqs = np.arange(HD // 2, dtype=np.float32)
    inv = (np.float32(1.0) / np.float32(1250) ** (freqs / np.float32(HD // 2))).astype(np.float32)
    theta = (np.arange(SEQ, dtype=np.float32)[:, None] * inv[None, :]).astype(np.float32)
    cos = np.repeat(np.cos(theta), 2, axis=1).reshape(NT, P, HD).transpose(1, 0, 2)
    sin = np.stack([-np.sin(theta), np.sin(theta)], axis=-1).reshape(NT, P, HD).transpose(1, 0, 2)
    c[:, C_COS:C_COS + NT * HD] = cos.reshape(P, NT * HD)
    c[:, C_SIN:C_SIN + NT * HD] = sin.reshape(P, NT * HD)
    c[:, C_TRI:C_TRI + P] = np.triu(np.ones((P, P), np.float32), 1)
    c[:, C_BLOCK:C_BLOCK + BLOCKS] = np.arange(BLOCKS)
    c[:, C_RESTART:C_RESTART + TILES * EXPERTS] = np.arange(TILES * EXPERTS) % HTILES != 0
    return c


def kernel(**inputs):
    import concourse.bacc as bacc
    from concourse.bass_utils import run_bass_kernel_spmd

    g = {k.removeprefix("L0_"): np.asarray(v) for k, v in inputs.items()}
    cat = np.concatenate
    w1 = cat([g["ffn_w1"], g["ffn_sw1"]]).transpose(2, 0, 1)
    w3 = cat([g["ffn_w3"], g["ffn_sw3"]]).transpose(2, 0, 1)
    w2 = cat([g["ffn_w2"], g["ffn_sw2"]]).transpose(2, 0, 1)
    w2 = w2.reshape(HC, P, FFNS, D).transpose(1, 2, 0, 3).reshape(P, FFNS, HC * D)
    ffn = cat([w1, w3, w2], axis=2).reshape(P, QKV0)
    arrays = {
        "x": g["attn_tokens"].reshape(BATCH * SEQ, D),
        "weights": cat([ffn, g["attn_qkv_w"].T, g["attn_out_w"].T], axis=1),
        "router": g["ffn_router_w"].T,
        "expert_bias": g["ffn_expert_bias"].reshape(1, EXPERTS),
        "qkv_b": g["attn_qkv_b"].reshape(1, 3 * D),
        "out_b": g["attn_out_b"].reshape(1, D),
        "consts": constant_table(),
    }
    arrays = {k: np.ascontiguousarray(v) for k, v in arrays.items()}
    nc = bacc.Bacc("TRN2", target_bir_lowering=False, num_devices=1)
    args = [nc.dram_tensor(f"in_{k}", a.shape, mybir.dt.from_np(a.dtype), kind="ExternalInput").ap()
            for k, a in arrays.items()]
    args.append(nc.dram_tensor("out", (BATCH * SEQ, D), F32, kind="ExternalOutput").ap())
    macaron_block(nc, *args)
    r = run_bass_kernel_spmd(nc, [{f"in_{k}": a for k, a in arrays.items()}], core_ids=[0])
    return r.results[0]["out"].reshape(BATCH, SEQ, D)
```
